# Optimizing a Trainium2 kernel written in Bass

```python
import numpy as np
import jax
import jax.numpy as jnp

def _softmax(x, axis=-1):
    return jax.nn.softmax(x, axis=axis)

def _gelu(x):
    return jax.nn.gelu(x, approximate=True)

def _silu(x):
    return jax.nn.silu(x)

def _sigmoid(x):
    return jax.nn.sigmoid(x)

def _layernorm(x, axis=-1, eps=1e-05):
    m = jnp.mean(x, axis=axis, keepdims=True)
    v = jnp.var(x, axis=axis, keepdims=True)
    return (x - m) / jnp.sqrt(v + eps)

def _scatter_add(tgt, idx, src, axis=0):
    return tgt.at[idx].add(src)

def _segment_sum(src, seg, n):
    return jax.ops.segment_sum(src, seg, n)
kernel_name = 'mk_flamingo_gated_d1_seqx_r4_ab7b42'

def setup_inputs(seed: int=0):
    np.random.seed(seed)
    _w = jnp.asarray

    def _rec_inputs():
        import jax
        import jax.numpy as jnp
        _rk = jax.random.key(seed)
        x = -0.0003929 + 0.9999 * jax.random.normal(jax.random.fold_in(_rk, 1), (4, 512, 1024), jnp.float32)
        _lenS = 512 - jax.random.randint(jax.random.fold_in(_rk, 7), (4,), 0, max(1, 512 // 4) + 1, jnp.int32)
        _lenS2 = 64 - jax.random.randint(jax.random.fold_in(_rk, 8), (4,), 0, max(1, 64 // 4) + 1, jnp.int32)
        _ctx_4096P = jax.random.normal(jax.random.fold_in(_rk, 11), (4, 16, 1024), jnp.float32)
        _ctx_4096c = jax.random.dirichlet(jax.random.fold_in(_rk, 511), 0.3 * jnp.ones((16,), jnp.float32), (4, 64))
        _ctx_4096t = jnp.einsum('bsk,bkd->bsd', _ctx_4096c, _ctx_4096P)
        _ctx_4096t = _ctx_4096t * jax.lax.rsqrt(jnp.mean(jnp.square(_ctx_4096t)) + 1e-12) * 0.953939
        ctx_4096 = 2.81802e-05 + 1.00001 * (_ctx_4096t + 0.3 * jax.random.normal(jax.random.fold_in(_rk, 611), (4, 64, 1024), jnp.float32))
        _validS = jnp.arange(512)[None, :] < _lenS[:, None]
        _validS2 = jnp.arange(64)[None, :] < _lenS2[:, None]
        _causal = jnp.tril(jnp.ones((512, 512), dtype=bool))
        mask_BxSxS2_ff0 = jnp.where(jnp.ones((4, 512, 64), dtype=bool), 0.0, -1000000000.0).astype(jnp.float32)
        _g = jax.random.normal(jax.random.fold_in(_rk, 9001), (2, 1), jnp.float32)
        _g = jnp.sign(_g) * jnp.maximum(jnp.abs(_g), 1.0) + (_g == 0) * 1.0
        g_xattn = _g[0]
        g_ffn = _g[1]
        return (x, ctx_4096, mask_BxSxS2_ff0, g_xattn, g_ffn)
    x, ctx_4096, mask_BxSxS2_ff0, g_xattn, g_ffn = _rec_inputs()

    def _L0_xattn_setup():
        import jax, jax.numpy as jnp
        import numpy as np
        B, S, D = (4, 256, 1024)
        HQ, HKV, DK, DV = (32, 8, 128, 128)

        def apply_rope(x, positions):
            d = x.shape[-1]
            inv_freq = 1.0 / 10000.0 ** (jnp.arange(0, d, 2, dtype=jnp.float32) / d)
            ang = positions.astype(jnp.float32)[:, None] * inv_freq[None, :]
            cos = jnp.cos(ang)[None, None]
            sin = jnp.sin(ang)[None, None]
            x1, x2 = (x[..., :d // 2], x[..., d // 2:])
            return jnp.concatenate([x1 * cos - x2 * sin, x2 * cos + x1 * sin], axis=-1)
        key = jax.random.key(seed)
        ks = jax.random.split(key, 8)
        return {'query': jax.random.normal(ks[0], (B, S, D), jnp.float32), 'key': jax.random.normal(ks[1], (B, S, D), jnp.float32), 'value': jax.random.normal(ks[2], (B, S, D), jnp.float32), 'mask': jnp.zeros((B, S, S), jnp.float32), 'wq': jax.random.normal(ks[3], (D, HQ * DK), jnp.float32) * 0.02, 'wk': jax.random.normal(ks[4], (D, HKV * DK), jnp.float32) * 0.02, 'wv': jax.random.normal(ks[5], (D, HKV * DV), jnp.float32) * 0.02, 'wo': jax.random.normal(ks[6], (HQ * DV, D), jnp.float32) * 0.02, 'curr_seq_pos': 0}
    _L0_xattn_all = _L0_xattn_setup()
    _L0_xattn_in = {k: v for k, v in _L0_xattn_all.items() if k in ('wq', 'wk', 'wv', 'wo')}
    del _L0_xattn_all

    def _L0_ffn_setup():
        import jax, jax.numpy as jnp
        import numpy as np

        @jax.custom_vjp
        def ste_sign(w):
            return jnp.sign(w)

        def _ste_fwd(w):
            return (jnp.sign(w), w)

        def _ste_bwd(w, g):
            mask = ((w > -1) & (w < 1)).astype(g.dtype)
            return (g * mask,)
        ste_sign.defvjp(_ste_fwd, _ste_bwd)
        key = jax.random.key(seed)
        k = jax.random.split(key, 6)
        B, S, H, O, E = (4, 512, 1024, 1024, 8)
        return {'x': jax.random.normal(k[0], (B, S, H), dtype=jnp.float32), 'weight': jax.random.normal(k[1], (O, H), dtype=jnp.float32) * 0.02, 'bias': jax.random.normal(k[2], (O,), dtype=jnp.float32) * 0.02, 'gate_w': jax.random.normal(k[3], (E, H), dtype=jnp.float32) * 0.02, 'in_channel_scale': jax.random.normal(k[4], (E, H), dtype=jnp.float32), 'out_channel_scale': jax.random.normal(k[5], (E, O), dtype=jnp.float32)}
    _L0_ffn_all = _L0_ffn_setup()
    _L0_ffn_in = {k: v for k, v in _L0_ffn_all.items() if k in ('weight', 'bias', 'gate_w', 'in_channel_scale', 'out_channel_scale')}
    del _L0_ffn_all
    return {'x': x, 'ctx_4096': ctx_4096, 'mask_BxSxS2_ff0': mask_BxSxS2_ff0, 'g_xattn': g_xattn, 'g_ffn': g_ffn, 'L0_xattn_wq': _L0_xattn_in['wq'], 'L0_xattn_wk': _L0_xattn_in['wk'], 'L0_xattn_wv': _L0_xattn_in['wv'], 'L0_xattn_wo': _L0_xattn_in['wo'], 'L0_ffn_weight': _L0_ffn_in['weight'], 'L0_ffn_bias': _L0_ffn_in['bias'], 'L0_ffn_gate_w': _L0_ffn_in['gate_w'], 'L0_ffn_in_channel_scale': _L0_ffn_in['in_channel_scale'], 'L0_ffn_out_channel_scale': _L0_ffn_in['out_channel_scale']}

def reference(x, ctx_4096, mask_BxSxS2_ff0, g_xattn, g_ffn, L0_xattn_wq, L0_xattn_wk, L0_xattn_wv, L0_xattn_wo, L0_ffn_weight, L0_ffn_bias, L0_ffn_gate_w, L0_ffn_in_channel_scale, L0_ffn_out_channel_scale):
    import jax
    import jax.numpy as jnp

    def _L0_xattn_ref(query, key, value, mask, wq, wk, wv, wo, curr_seq_pos):
        import jax, jax.numpy as jnp
        import numpy as np
        B, S, D = (4, 256, 1024)
        HQ, HKV, DK, DV = (32, 8, 128, 128)

        def apply_rope(x, positions):
            d = x.shape[-1]
            inv_freq = 1.0 / 10000.0 ** (jnp.arange(0, d, 2, dtype=jnp.float32) / d)
            ang = positions.astype(jnp.float32)[:, None] * inv_freq[None, :]
            cos = jnp.cos(ang)[None, None]
            sin = jnp.sin(ang)[None, None]
            x1, x2 = (x[..., :d // 2], x[..., d // 2:])
            return jnp.concatenate([x1 * cos - x2 * sin, x2 * cos + x1 * sin], axis=-1)
        bs, sq, _ = query.shape
        sk = key.shape[1]
        n_groups = HQ // HKV
        q = (query @ wq).reshape(bs, sq, HQ, DK).transpose(0, 2, 1, 3)
        k = (key @ wk).reshape(bs, sk, HKV, DK)
        v = (value @ wv).reshape(bs, sk, HKV, DV)
        k = jnp.repeat(k, n_groups, axis=2).transpose(0, 2, 1, 3)
        v = jnp.repeat(v, n_groups, axis=2).transpose(0, 2, 1, 3)
        scale = jnp.sqrt(jnp.float32(DK))
        pos = curr_seq_pos + jnp.arange(sq)
        q = apply_rope(q, pos)
        k = apply_rope(k, curr_seq_pos + jnp.arange(sk))
        scores = jnp.einsum('bhqd,bhkd->bhqk', q, k) / scale
        m = jax.lax.dynamic_slice(mask, (0, curr_seq_pos, 0), (bs, sq, sk))
        attn = jax.nn.softmax(scores + m[:, None, :, :], axis=-1)
        out = jnp.einsum('bhqk,bhkd->bhqd', attn, v)
        out = out.transpose(0, 2, 1, 3).reshape(bs, sq, HQ * DV)
        return out @ wo

    def _L0_ffn_ref(x, weight, bias, gate_w, in_channel_scale, out_channel_scale):
        import jax, jax.numpy as jnp
        import numpy as np

        @jax.custom_vjp
        def ste_sign(w):
            return jnp.sign(w)

        def _ste_fwd(w):
            return (jnp.sign(w), w)

        def _ste_bwd(w, g):
            mask = ((w > -1) & (w < 1)).astype(g.dtype)
            return (g * mask,)
        ste_sign.defvjp(_ste_fwd, _ste_bwd)
        B, S, H = x.shape
        xf = x.reshape(-1, H)
        router_logits = xf @ gate_w.T
        routing = jax.nn.softmax(router_logits.astype(jnp.float32), axis=1).astype(x.dtype)
        in_scale = routing @ in_channel_scale
        out_scale = routing @ out_channel_scale
        wb = ste_sign(weight)
        out = xf * in_scale @ wb.T * out_scale + bias
        return out.reshape(B, S, -1)
    x = x + jnp.tanh(g_xattn[0]) * _L0_xattn_ref(_layernorm(x, axis=-1), ctx_4096, ctx_4096, mask_BxSxS2_ff0, L0_xattn_wq, L0_xattn_wk, L0_xattn_wv, L0_xattn_wo, 0)
    x = x + jnp.tanh(g_ffn[0]) * _L0_ffn_ref(_layernorm(x, axis=-1), L0_ffn_weight, L0_ffn_bias, L0_ffn_gate_w, L0_ffn_in_channel_scale, L0_ffn_out_channel_scale)
    return x

_drawn_inputs = setup_inputs


def setup_inputs(seed=0):
    import zlib

    import numpy as np

    out = dict(_drawn_inputs(seed))
    spreads = {}
    factors = {'L0_ffn_bias': 8.0}
    for name, (base, spread) in spreads.items():
        noise = np.random.default_rng([zlib.crc32(name.encode()), seed]).standard_normal(out[name].shape)
        drawn = base * np.exp(spread * noise) if base else spread * noise
        out[name] = jnp.asarray(drawn.astype(out[name].dtype))
    for name, factor in factors.items():
        out[name] = (out[name] * factor).astype(out[name].dtype)
    return out
```

```python
from contextlib import ExitStack

import concourse.bass as bass
import numpy as np
from concourse import mybir

ALU = mybir.AluOpType
ACT = mybir.ActivationFunctionType
AX = mybir.AxisListType
F32 = mybir.dt.float32
F32R = mybir.dt.float32r

P = 128
B, S, D = 4, 512, 1024
SK = 64
HQ, HKV, DK = 32, 8, 128
E = 8
EPS = 1e-5
T = B * S
KT = D // P
HP = HQ // 2
HALF = DK // 2
TT = S // P
CTX = B * SK
GP = HKV // 2
NLN = T // P
PB = 2
NQ = 4
QW = D // NQ
BT = 256
NB = T // BT


def wait(eng, semaphore, count):
    if isinstance(count, int) and count <= 0:
        return
    eng.wait_ge(semaphore, count)


def three(pe, out, hi, lo, rhs_hi, rhs_lo, first, last, **kw):
    pe.matmul(out, hi, rhs_hi, start=first, stop=False, **kw)
    pe.matmul(out, hi, rhs_lo, start=False, stop=False, **kw)
    return pe.matmul(out, lo, rhs_hi, start=False, stop=last, **kw)


def prepare(nc, a, scratch, x_hi, x_lo, ident):
    NU = 2 * HKV
    with ExitStack() as ctx:
        def sb(name, shape, dt=F32):
            return ctx.enter_context(nc.sbuf_tensor(name, shape, dt))

        def sem(name):
            return ctx.enter_context(nc.semaphore(name))

        ctx_raw = sb("ctx_raw", [P, KT, CTX])
        ctx_hi = sb("ctx_hi", [P, KT, CTX], F32R)
        ctx_lo = sb("ctx_lo", [P, KT, CTX], F32R)
        kw_raw = sb("kw_raw", [P, 2, KT, P])
        kw_hi = sb("kw_hi", [P, 2, KT, P], F32R)
        kw_lo = sb("kw_lo", [P, 2, KT, P], F32R)
        x_in = sb("x_in", [P, 2, D])
        xn = sb("xn", [P, 2, D])
        k_rot = sb("k_rot", [P, 4, CTX])
        v_hi = sb("v_hi", [P, 2, CTX], F32R)
        v_lo = sb("v_lo", [P, 2, CTX], F32R)
        cos_k = sb("cos_k", [P, CTX])
        sin_k = sb("sin_k", [P, CTX])
        stats = sb("stats", [P, 2, 2, 6])
        mean_var = sb("mean_var", [P, 2, 2])
        var_eps = sb("var_eps", [P, 2])
        rstd = sb("rstd", [P, 2])
        minus_half = sb("minus_half", [P, 1])
        kv_ps = [ctx.enter_context(nc.psum_tensor(f"kv_ps{i}", [P, 512], F32)) for i in range(4)]
        xt_ps = [ctx.enter_context(nc.psum_tensor(f"xt_ps{i}", [P, 4, P], F32)) for i in range(4)]

        consts_in = sem("consts_in")
        ctx_in = sem("ctx_in")
        ctx_hi_ready = sem("ctx_hi_ready")
        ctx_lo_ready = sem("ctx_lo_ready")
        kw_in = [sem(f"kw_in{i}") for i in range(2)]
        kw_hi_ready = sem("kw_hi_ready")
        kw_lo_ready = sem("kw_lo_ready")
        kv_done = sem("kv_done")
        k_read = sem("k_read")
        k_roped = sem("k_roped")
        k_stored = sem("k_stored")
        v_hi_ready = sem("v_hi_ready")
        v_lo_ready = sem("v_lo_ready")
        v_stored = [sem(f"v_stored{i}") for i in range(2)]
        x_in_sem = [sem(f"x_in_sem{i}") for i in range(2)]
        half_ready = sem("half_ready")
        stats_ready = sem("stats_ready")
        mean_ready = sem("mean_ready")
        var_ready = sem("var_ready")
        rstd_ready = sem("rstd_ready")
        xn_ready = sem("xn_ready")
        xt_ready = sem("xt_ready")
        x_hi_ready = sem("x_hi_ready")
        x_lo_ready = sem("x_lo_ready")

        block = ctx.enter_context(nc.Block())

        @block.sync
        def _(sp):
            sp.dma_start(ctx_raw[:], a["ctx_t"].rearrange("(k p) t -> p k t", p=P)).then_inc(ctx_in, 16)
            sp.dma_start(x_in[:, 0], a["x"][0:P, :]).then_inc(x_in_sem[0], 16)
            sp.dma_start(ident[:], a["ident"]).then_inc(consts_in, 16)
            sp.dma_start(cos_k[:], a["cos_k"]).then_inc(consts_in, 16)
            sp.dma_start(sin_k[:], a["sin_k"]).then_inc(consts_in, 16)
            for n in range(NU):
                wait(sp, kw_lo_ready, n - 1)
                sp.dma_start(kw_raw[:, n % 2], a["wkv"][n]).then_inc(kw_in[n % 2], 16)
                if n + 1 < NLN:
                    wait(sp, xn_ready, n)
                    sp.dma_start(x_in[:, (n + 1) % 2], a["x"][(n + 1) * P:(n + 2) * P, :]).then_inc(x_in_sem[(n + 1) % 2], 16)

        @block.tensor
        def _(pe):
            pe.wait_ge(consts_in, 48)
            for n in range(NU + 1):
                if n < NU:
                    if n == 0:
                        pe.wait_ge(ctx_hi_ready, 1)
                        pe.wait_ge(ctx_lo_ready, 1)
                    pe.wait_ge(kw_hi_ready, n + 1)
                    pe.wait_ge(kw_lo_ready, n + 1)
                    if n >= 4 + HKV:
                        pe.wait_ge(v_lo_ready, n - 4 - HKV + 1)
                    elif n >= 4:
                        pe.wait_ge(k_read, (n - 4) // 2 + 1)
                    for k in range(KT):
                        last = three(pe, kv_ps[n % 4][:, 0:CTX], kw_hi[:, n % 2, k, :], kw_lo[:, n % 2, k, :],
                                     ctx_hi[:, k, :], ctx_lo[:, k, :], k == 0, k == KT - 1)
                    last.then_inc(kv_done, 1)
                if n >= 1:
                    i = n - 1
                    pe.wait_ge(xn_ready, i + 1)
                    wait(pe, x_lo_ready, i - 1)
                    for k in range(KT):
                        last = pe.transpose(xt_ps[2 * (i % 2) + k // 4][:, k % 4, :],
                                            xn[:, i % 2, k * P:(k + 1) * P], ident[:])
                    last.then_inc(xt_ready, 1)

        @block.scalar
        def _(act):
            act.wait_ge(ctx_in, 16)
            nc.scalar.copy(ctx_hi[:], ctx_raw[:]).then_inc(ctx_hi_ready, 1)

            def turned(i):
                act.wait_ge(xt_ready, i + 1)
                for j in range(2):
                    last = nc.scalar.copy(x_hi[:, 4 * j:4 * j + 4, i * P:(i + 1) * P], xt_ps[2 * (i % 2) + j][:])
                last.then_inc(x_hi_ready, 1)

            for n in range(NU + 2):
                if n < NU:
                    act.wait_ge(kw_in[n % 2], 16 * (n // 2 + 1))
                    wait(act, kv_done, n - 1)
                    nc.scalar.copy(kw_hi[:, n % 2], kw_raw[:, n % 2]).then_inc(kw_hi_ready, 1)
                if HKV <= n - 1 < NU:
                    g = n - 1 - HKV
                    act.wait_ge(kv_done, n)
                    wait(act, v_stored[g % 2], 32 * (g // 2))
                    nc.scalar.copy(v_hi[:, g % 2], kv_ps[(n - 1) % 4][:, 0:CTX]).then_inc(v_hi_ready, 1)
                if n >= 2:
                    turned(n - 2)
            act.wait_ge(k_stored, 32 * GP)
            for i in range(2):
                act.wait_ge(v_stored[i], 32 * HKV // 2)

        @block.gpsimd
        def _(pool):
            nc.gpsimd.memset(minus_half[:], -0.5).then_inc(half_ready, 1)
            pool.wait_ge(half_ready, 1)
            def store_values(g):
                pool.wait_ge(v_lo_ready, g + 1)
                pool.dma_start(scratch["values"][0, g], v_hi[:, g % 2].bitcast(F32)).then_inc(v_stored[g % 2], 16)
                pool.dma_start(scratch["values"][1, g], v_lo[:, g % 2].bitcast(F32)).then_inc(v_stored[g % 2], 16)

            for n in range(NU):
                pool.wait_ge(var_ready, n + 1)
                wait(pool, xn_ready, n - 1)
                nc.gpsimd.tensor_tensor(rstd[:, n % 2:n % 2 + 1], var_eps[:, n % 2:n % 2 + 1], minus_half[:],
                                        ALU.pow).then_inc(rstd_ready, 1)
                pool.wait_ge(kw_hi_ready, n + 1)
                nc.gpsimd.tensor_tensor(kw_lo[:, n % 2], kw_raw[:, n % 2], kw_hi[:, n % 2].bitcast(F32),
                                        ALU.subtract).then_inc(kw_lo_ready, 1)
                if n >= 1 and (n - 1) < HKV and (n - 1) % 2 == 1:
                    gp = (n - 1) // 2
                    pool.wait_ge(k_roped, gp + 1)
                    for c in range(2):
                        pool.dma_start(scratch["keys"][c, gp * P:(gp + 1) * P, :], k_rot[:, 2 * c, :]).then_inc(k_stored, 16)
                if n >= HKV + 2:
                    store_values(n - HKV - 2)
            store_values(HKV - 2)
            store_values(HKV - 1)

        @block.vector
        def _(dve):
            def statistics(i):
                dve.wait_ge(x_in_sem[i % 2], 16 * (i // 2 + 1))
                for j in range(2):
                    last = nc.vector.bn_stats(stats[:, i % 2, j, :], x_in[:, i % 2, j * 512:(j + 1) * 512])
                last.then_inc(stats_ready, 1)
                dve.wait_ge(stats_ready, i + 1)
                nc.vector.bn_aggr(mean_var[:, i % 2, :], stats[:, i % 2]).then_inc(mean_ready, 1)
                dve.wait_ge(mean_ready, i + 1)
                wait(dve, rstd_ready, i - 1)
                nc.vector.tensor_scalar(var_eps[:, i % 2:i % 2 + 1], mean_var[:, i % 2, 1:2], EPS, None,
                                        ALU.add).then_inc(var_ready, 1)

            def rotate(gp):
                k1, k2 = kv_ps[(2 * gp) % 4][:, 0:CTX], kv_ps[(2 * gp + 1) % 4][:, 0:CTX]
                dve.wait_ge(kv_done, 2 * gp + 2)
                wait(dve, k_stored, 32 * gp)
                nc.vector.tensor_tensor(k_rot[:, 0], k1, cos_k[:], ALU.mult)
                nc.vector.tensor_tensor(k_rot[:, 1], k2, sin_k[:], ALU.mult)
                nc.vector.tensor_tensor(k_rot[:, 2], k2, cos_k[:], ALU.mult)
                nc.vector.tensor_tensor(k_rot[:, 3], k1, sin_k[:], ALU.mult).then_inc(k_read, 1)
                dve.wait_ge(k_read, gp + 1)
                nc.vector.tensor_tensor(k_rot[:, 0], k_rot[:, 0], k_rot[:, 1], ALU.subtract)
                nc.vector.tensor_tensor(k_rot[:, 2], k_rot[:, 2], k_rot[:, 3], ALU.add).then_inc(k_roped, 1)

            statistics(0)
            dve.wait_ge(ctx_hi_ready, 1)
            nc.vector.tensor_tensor(ctx_lo[:], ctx_raw[:], ctx_hi[:].bitcast(F32), ALU.subtract).then_inc(ctx_lo_ready, 1)
            dve.wait_ge(consts_in, 48)
            for n in range(NU + 2):
                if n < NLN:
                    dve.wait_ge(rstd_ready, n + 1)
                    wait(dve, xt_ready, n - 1)
                    nc.vector.tensor_scalar(xn[:, n % 2], x_in[:, n % 2], mean_var[:, n % 2, 0:1], rstd[:, n % 2:n % 2 + 1],
                                            ALU.subtract, ALU.mult).then_inc(xn_ready, 1)
                    if n + 1 < NLN:
                        statistics(n + 1)
                if 0 <= n - 1 < HKV and (n - 1) % 2 == 1:
                    rotate((n - 1) // 2)
                if HKV <= n - 1 < NU:
                    g = n - 1 - HKV
                    dve.wait_ge(v_hi_ready, g + 1)
                    wait(dve, v_stored[g % 2], 32 * (g // 2))
                    nc.vector.tensor_tensor(v_lo[:, g % 2], kv_ps[(n - 1) % 4][:, 0:CTX], v_hi[:, g % 2].bitcast(F32),
                                            ALU.subtract).then_inc(v_lo_ready, 1)
                if n >= 2:
                    i = n - 2
                    dve.wait_ge(x_hi_ready, i + 1)
                    for j in range(2):
                        at = (slice(None), slice(4 * j, 4 * j + 4), slice(i * P, (i + 1) * P))
                        last = nc.vector.tensor_tensor(x_lo[at], xt_ps[2 * (i % 2) + j][:], x_hi[at].bitcast(F32), ALU.subtract)
                    last.then_inc(x_lo_ready, 1)


def attend(nc, a, scratch, x_hi, x_lo, ident):
    STEPS_G = 2 * B
    STEPS = HKV * STEPS_G
    with ExitStack() as ctx:
        def sb(name, shape, dt=F32):
            return ctx.enter_context(nc.sbuf_tensor(name, shape, dt))

        def ps(name, shape):
            return ctx.enter_context(nc.psum_tensor(name, shape, F32))

        def sem(name):
            return ctx.enter_context(nc.semaphore(name))

        w_raw = sb("w_raw", [P, 2, KT, P])
        w_hi = sb("w_hi", [P, 2, KT, P], F32R)
        w_lo = sb("w_lo", [P, 2, KT, P], F32R)
        key_raw = sb("key_raw", [P, 2, B, P])
        key_hi = sb("key_hi", [P, 2, B, P], F32R)
        key_lo = sb("key_lo", [P, 2, B, P], F32R)
        cos_q = sb("cos_q", [P, S])
        sin_q = sb("sin_q", [P, S])
        mask = sb("mask", [P, B, TT, SK])
        rot = sb("rot", [P, 4, S])
        q_hi = sb("q_hi", [P, 2, S], F32R)
        q_lo = sb("q_lo", [P, 2, S], F32R)
        scores_t = sb("scores_t", [P, S])
        shifted = sb("shifted", [P, TT, 2, SK])
        exps = sb("exps", [P, TT, 2, SK])
        probs = sb("probs", [P, TT, 2, SK])
        row_max = sb("row_max", [P, TT, 2])
        row_sum = sb("row_sum", [P, TT, 2])
        row_inv = sb("row_inv", [P, TT, 2])
        pt_hi = sb("pt_hi", [P, 2, S], F32R)
        pt_lo = sb("pt_lo", [P, 2, S], F32R)
        q_ps = [ps(f"q_ps{i}", [P, S]) for i in range(4)]
        st_ps = ps("st_ps", [P, S])
        s_ps = ps("s_ps", [P, TT, 2, SK])
        pt_ps = ps("pt_ps", [P, S])

        consts_in = sem("att_consts_in")
        w_in = [sem(f"w_in{c}") for c in range(2)]
        w_hi_ready = sem("w_hi_ready")
        w_lo_ready = sem("w_lo_ready")
        key_zeroed = sem("key_zeroed")
        key_in = sem("key_in")
        key_hi_ready = sem("key_hi_ready")
        key_lo_ready = sem("key_lo_ready")
        q_done = sem("q_done")
        prod_ready = sem("prod_ready")
        rot_ready = sem("rot_ready")
        q_hi_ready = sem("q_hi_ready")
        q_lo_ready = sem("q_lo_ready")
        st_done = sem("st_done")
        st_copied = sem("st_copied")
        s_done = sem("s_done")
        masked_ready = sem("masked_ready")
        max_ready = sem("max_ready")
        shifted_ready = sem("shifted_ready")
        exps_ready = sem("exps_ready")
        sum_ready = sem("sum_ready")
        inv_ready = sem("inv_ready")
        probs_ready = sem("probs_ready")
        pt_done = sem("pt_done")
        pt_hi_ready = sem("pt_hi_ready")
        pt_lo_ready = sem("pt_lo_ready")
        pt_stored = [sem(f"pt_stored{i}") for i in range(2)]

        block = ctx.enter_context(nc.Block())

        def over_key_heads(eng, slot, peel_last):
            for j in range(STEPS_G):
                slot(0, j, False)
            end = HKV - 1 if peel_last else HKV
            with eng.Fori(1, end) as g:
                for j in range(STEPS_G):
                    slot(g, j, False)
            if peel_last:
                for j in range(STEPS_G):
                    slot(HKV - 1, j, True)
            for j in range(STEPS_G, STEPS_G + 3):
                slot(HKV - 1, j, True)

        def has(g, j, lag):
            if isinstance(g, int):
                return 0 <= g * STEPS_G + j - lag < STEPS
            return True

        @block.sync
        def _(sp):
            def load_w(hp, c, uses):
                wait(sp, w_lo_ready, 2 * (uses - 1) + c + 1)
                sp.dma_start(w_raw[:, c], a["wq"][bass.ds(hp, 1), c].rearrange("o p k n -> p (o k) n")).then_inc(w_in[c], 16)

            def load_keys(g):
                wait(sp, key_lo_ready, g)
                for c in range(2):
                    for h in range(2):
                        src = scratch["keys"][c].rearrange("(g f) t -> g f t", f=HALF)[bass.ds(g, 1)]
                        sp.dma_start(key_raw[h * HALF:(h + 1) * HALF, c, :, h * SK:(h + 1) * SK],
                                     src.rearrange("o f (b s) -> (o f) b s", b=B)).then_inc(key_in, 16)

            def slot(g, j, last):
                if j == 2 and not last:
                    load_keys(g + 1)
                if j % B == 1 and not (last and j >= B):
                    hp = 2 * g + j // B + 1
                    load_w(hp, 0, hp)
                    load_w(hp, 1, hp)
                if has(g, j, 3):
                    i = (j - 3) % 2
                    hp, b = 2 * g + (j - 3) // B, (j - 3) % B
                    wait(sp, pt_hi_ready, STEPS_G * g + j - 2)
                    wait(sp, pt_lo_ready, STEPS_G * g + j - 2)
                    for n, part in enumerate((pt_hi, pt_lo)):
                        dst = scratch["probs"][n][bass.ds(hp, 1), :, b * S:(b + 1) * S].rearrange("o p t -> (o p) t")
                        sp.dma_start(dst, part[:, i].bitcast(F32)).then_inc(pt_stored[i], 16)

            load_w(0, 0, 0)
            sp.dma_start(cos_q[:], a["cos_q"]).then_inc(consts_in, 16)
            sp.dma_start(sin_q[:], a["sin_q"]).then_inc(consts_in, 16)
            load_w(0, 1, 0)
            sp.dma_start(mask[:], a["mask"]).then_inc(consts_in, 16)
            sp.wait_ge(key_zeroed, 1)
            load_keys(0)
            over_key_heads(sp, slot, True)
            for i in range(2):
                sp.wait_ge(pt_stored[i], 32 * STEPS // 2)

        @block.tensor
        def _(pe):
            def queries(g, j, c, ks):
                b = j % B
                u = STEPS_G * g + j
                hp = 2 * g + j // B
                if b == 0 and ks[0] == 0:
                    pe.wait_ge(w_hi_ready, 2 * hp + c + 1)
                    pe.wait_ge(w_lo_ready, 2 * hp + c + 1)
                if c == 0 and ks[0] == 0:
                    wait(pe, prod_ready, 2 * u - 2)
                for k in ks:
                    at = (slice(None), k, slice(b * S, (b + 1) * S))
                    last = three(pe, q_ps[2 * (j % 2) + c][:], w_hi[:, c, k, :], w_lo[:, c, k, :], x_hi[at], x_lo[at],
                                 k == 0, k == KT - 1)
                if ks[-1] == KT - 1:
                    last.then_inc(q_done, 1)

            def slot(g, j, last_g):
                u = STEPS_G * g + j
                if has(g, j, 0):
                    queries(g, j, 0, range(KT))
                    queries(g, j, 1, range(KT // 2))
                if has(g, j, 1):
                    b = (j - 1) % B
                    if j == 1:
                        pe.wait_ge(key_hi_ready, g + 1)
                        pe.wait_ge(key_lo_ready, g + 1)
                    wait(pe, st_copied, u - 1)
                    for c in range(2):
                        pe.wait_ge(q_hi_ready, 2 * u - 1 + c)
                        pe.wait_ge(q_lo_ready, 2 * u - 1 + c)
                        last = three(pe, st_ps[:], key_hi[:, c, b, :], key_lo[:, c, b, :], q_hi[:, c, :], q_lo[:, c, :],
                                     c == 0, c == 1)
                    last.then_inc(st_done, 1)
                if has(g, j, 0):
                    queries(g, j, 1, range(KT // 2, KT))
                if has(g, j, 2):
                    pe.wait_ge(probs_ready, u - 1)
                    wait(pe, pt_hi_ready, u - 2)
                    wait(pe, pt_lo_ready, u - 2)
                    for i in range(TT):
                        last = pe.transpose(pt_ps[:, i * P:(i + 1) * P], probs[:, i].rearrange("p h s -> p (h s)"), ident[:])
                    last.then_inc(pt_done, 1)
                if has(g, j, 1):
                    pe.wait_ge(st_copied, u)
                    wait(pe, masked_ready, u - 1)
                    for i in range(TT):
                        last = pe.transpose(s_ps[:, i].rearrange("p h s -> p (h s)"), scores_t[:, i * P:(i + 1) * P], ident[:])
                    last.then_inc(s_done, 1)

            over_key_heads(pe, slot, False)

        @block.scalar
        def _(act):
            def split_w(hp, c):
                act.wait_ge(w_in[c], 16 * (hp + 1))
                wait(act, q_done, 2 * B * hp - 1 + c)
                nc.scalar.copy(w_hi[:, c], w_raw[:, c]).then_inc(w_hi_ready, 1)

            def slot(g, j, last):
                u = STEPS_G * g + j
                hp = 2 * g + j // B
                if has(g, j, 3):
                    i = (j - 3) % 2
                    act.wait_ge(pt_done, u - 2)
                    wait(act, pt_stored[i], 32 * (4 * g + (j - 3) // 2))
                    nc.scalar.copy(pt_hi[:, i], pt_ps[:]).then_inc(pt_hi_ready, 1)
                if j % B == 0 and has(g, j, 0) and not (isinstance(g, int) and g == 0 and j == 0):
                    split_w(hp, 1)
                if j == 1:
                    act.wait_ge(key_in, 64 * (g + 1))
                    wait(act, st_done, u - 1)
                    nc.scalar.copy(key_hi[:], key_raw[:]).then_inc(key_hi_ready, 1)
                if has(g, j, 1):
                    for c in range(2):
                        act.wait_ge(rot_ready, 2 * u - 1 + c)
                        wait(act, st_done, u - 1)
                        nc.scalar.copy(q_hi[:, c], rot[:, 2 * c]).then_inc(q_hi_ready, 1)
                if has(g, j, 2):
                    act.wait_ge(shifted_ready, u - 1)
                    wait(act, probs_ready, u - 2)
                    nc.scalar.activation(exps[:], shifted[:], ACT.Exp).then_inc(exps_ready, 1)
                if j % B == B - 1 and not (last and j >= B):
                    split_w(hp + 1, 0)
                if has(g, j, 1):
                    act.wait_ge(st_done, u)
                    wait(act, s_done, u - 1)
                    nc.scalar.copy(scores_t[:], st_ps[:]).then_inc(st_copied, 1)

            split_w(0, 0)
            split_w(0, 1)
            over_key_heads(act, slot, True)

        @block.gpsimd
        def _(pool):
            def split_w(hp, c):
                pool.wait_ge(w_hi_ready, 2 * hp + c + 1)
                nc.gpsimd.tensor_tensor(w_lo[:, c], w_raw[:, c], w_hi[:, c].bitcast(F32), ALU.subtract).then_inc(w_lo_ready, 1)

            def slot(g, j, last):
                u = STEPS_G * g + j
                hp = 2 * g + j // B
                if j % B == 0 and has(g, j, 0) and not (isinstance(g, int) and g == 0 and j == 0):
                    split_w(hp, 1)
                if j == 1:
                    pool.wait_ge(key_hi_ready, g + 1)
                    nc.gpsimd.tensor_tensor(key_lo[:], key_raw[:], key_hi[:].bitcast(F32), ALU.subtract).then_inc(key_lo_ready, 1)
                if has(g, j, 1):
                    for c in range(2):
                        pool.wait_ge(q_hi_ready, 2 * u - 1 + c)
                        nc.gpsimd.tensor_tensor(q_lo[:, c], rot[:, 2 * c], q_hi[:, c].bitcast(F32),
                                                ALU.subtract).then_inc(q_lo_ready, 1)
                if has(g, j, 2):
                    pool.wait_ge(inv_ready, u - 1)
                    wait(pool, pt_done, u - 2)
                    nc.gpsimd.tensor_tensor(probs[:], exps[:], row_inv[:].unsqueeze(3).to_broadcast([P, TT, 2, SK]),
                                            ALU.mult).then_inc(probs_ready, 1)
                if j % B == B - 1 and not (last and j >= B):
                    split_w(hp + 1, 0)

            split_w(0, 0)
            split_w(0, 1)
            over_key_heads(pool, slot, True)

        @block.vector
        def _(dve):
            def slot(g, j, last):
                u = STEPS_G * g + j
                if has(g, j, 1):
                    q1, q2 = q_ps[2 * ((j - 1) % 2)][:], q_ps[2 * ((j - 1) % 2) + 1][:]
                    dve.wait_ge(q_done, 2 * u)
                    wait(dve, q_lo_ready, 2 * u - 2)
                    nc.vector.tensor_tensor(rot[:, 0], q1, cos_q[:], ALU.mult)
                    nc.vector.tensor_tensor(rot[:, 1], q2, sin_q[:], ALU.mult).then_inc(prod_ready, 1)
                    nc.vector.tensor_tensor(rot[:, 2], q2, cos_q[:], ALU.mult)
                    dve.wait_ge(prod_ready, 2 * u - 1)
                    nc.vector.tensor_tensor(rot[:, 0], rot[:, 0], rot[:, 1], ALU.subtract).then_inc(rot_ready, 1)
                    nc.vector.tensor_tensor(rot[:, 3], q1, sin_q[:], ALU.mult).then_inc(prod_ready, 1)
                    dve.wait_ge(prod_ready, 2 * u)
                    nc.vector.tensor_tensor(rot[:, 2], rot[:, 2], rot[:, 3], ALU.add).then_inc(rot_ready, 1)
                if has(g, j, 2):
                    b = (j - 2) % B
                    dve.wait_ge(s_done, u - 1)
                    wait(dve, exps_ready, u - 2)
                    nc.vector.tensor_tensor(shifted[:], s_ps[:], mask[:, b].unsqueeze(2).to_broadcast([P, TT, 2, SK]),
                                            ALU.add).then_inc(masked_ready, 1)
                    dve.wait_ge(masked_ready, u - 1)
                    nc.vector.tensor_reduce(row_max[:], shifted[:], AX.X, ALU.max).then_inc(max_ready, 1)
                    dve.wait_ge(max_ready, u - 1)
                    nc.vector.tensor_tensor(shifted[:], shifted[:], row_max[:].unsqueeze(3).to_broadcast([P, TT, 2, SK]),
                                            ALU.subtract).then_inc(shifted_ready, 1)
                if has(g, j, 3):
                    i = (j - 3) % 2
                    dve.wait_ge(pt_hi_ready, u - 2)
                    nc.vector.tensor_tensor(pt_lo[:, i], pt_ps[:], pt_hi[:, i].bitcast(F32), ALU.subtract).then_inc(pt_lo_ready, 1)
                if has(g, j, 2):
                    dve.wait_ge(exps_ready, u - 1)
                    wait(dve, probs_ready, u - 2)
                    nc.vector.tensor_reduce(row_sum[:], exps[:], AX.X, ALU.add).then_inc(sum_ready, 1)
                    dve.wait_ge(sum_ready, u - 1)
                    nc.vector.reciprocal(row_inv[:], row_sum[:]).then_inc(inv_ready, 1)

            nc.vector.memset(key_raw[:], 0.0).then_inc(key_zeroed, 1)
            dve.wait_ge(consts_in, 48)
            over_key_heads(dve, slot, False)


def project(nc, a, scratch):
    with ExitStack() as ctx:
        def sb(name, shape, dt=F32):
            return ctx.enter_context(nc.sbuf_tensor(name, shape, dt))

        def ps(name, shape):
            return ctx.enter_context(nc.psum_tensor(name, shape, F32))

        def sem(name):
            return ctx.enter_context(nc.semaphore(name))

        NBUF = 4
        VW_AHEAD, WO_AHEAD = 2, 5
        NACC = QW // P * PB
        PAIRS = B // PB
        p_hi = sb("p_hi", [P, HP, PB * S], F32R)
        p_lo = sb("p_lo", [P, HP, PB * S], F32R)
        vt_hi = sb("vt_hi", [P, HKV, CTX], F32R)
        vt_lo = sb("vt_lo", [P, HKV, CTX], F32R)
        wo_raw = sb("wo_raw", [P, NBUF, 2, QW])
        wo_hi = sb("wo_hi", [P, NBUF, 2, QW], F32R)
        wo_lo = sb("wo_lo", [P, NBUF, 2, QW], F32R)
        vw_hi = sb("vw_hi", [P, NBUF, PB, QW], F32R)
        vw_lo = sb("vw_lo", [P, NBUF, PB, QW], F32R)
        attn_sb = sb("attn_sb", [P, QW // P, PB, S])
        gate = sb("gate_x", [P, 1])
        tanh_gate = sb("tanh_gate_x", [P, 1])
        vw_ps = [ps(f"vw_ps{i}", [P, 2, QW]) for i in range(NBUF)]
        acc_ps = [ps(f"acc_ps{i}", [P, S]) for i in range(NACC)]

        gate_in = sem("gate_x_in")
        gate_ready = sem("gate_x_ready")
        vt_in = sem("vt_in")
        p_in = [sem(f"p_in{h}") for h in range(HP)]
        wo_in = [sem(f"wo_in{i}") for i in range(NBUF)]
        wo_hi_ready = sem("wo_hi_ready")
        wo_lo_ready = sem("wo_lo_ready")
        vw_done = sem("vw_done")
        vw_hi_ready = sem("vw_hi_ready")
        vw_lo_ready = sem("vw_lo_ready")
        av_done = sem("av_done")
        acc_done = sem("acc_done")
        acc_read = sem("acc_read")
        attn_stored = sem("attn_stored")

        block = ctx.enter_context(nc.Block())

        def over_quarters(eng, quarter):
            quarter(0, 0, (0, 1))
            with eng.Fori(1, NQ - 1) as q:
                quarter(0, q, (0, q + 1))
            quarter(0, NQ - 1, (1, 0))
            with eng.Fori(0, NQ - 1) as q:
                quarter(1, q, (1, q + 1))
            quarter(1, NQ - 1, None)

        def place(pair, q, hp):
            return (pair * NQ + q) * HP + hp

        @block.sync
        def _(sp):
            def load_probs(pair, hp):
                wait(sp, av_done, place(pair - 1, NQ - 1, hp) + 1)
                for n, part in enumerate((p_hi, p_lo)):
                    src = scratch["probs"][n, hp, :, pair * PB * S:(pair + 1) * PB * S]
                    sp.dma_start(part[:, hp].bitcast(F32), src).then_inc(p_in[hp], 16)

            def quarter(pair, q, before=(), after=()):
                for hp in range(HP):
                    if hp in before:
                        load_probs(pair, hp)
                    wait(sp, wo_lo_ready, place(pair, q, hp) - NBUF + 1)
                    sp.dma_start(wo_raw[:, hp % NBUF], a["wo"][bass.ds(q, 1), hp].rearrange("o p h n -> p (o h) n")
                                 ).then_inc(wo_in[hp % NBUF], 16)
                    for later in after:
                        if later[0] == hp:
                            load_probs(*later[1:])

            sp.dma_start(vt_hi[:].bitcast(F32), scratch["values"][0].rearrange("g p t -> p g t")).then_inc(vt_in, 16)
            sp.dma_start(vt_lo[:].bitcast(F32), scratch["values"][1].rearrange("g p t -> p g t")).then_inc(vt_in, 16)
            sp.dma_start(gate[:], a["g_xattn"]).then_inc(gate_in, 16)
            LAG = 6
            quarter(0, 0, before=range(HP))
            with sp.Fori(1, NQ - 1) as q:
                quarter(0, q)
            quarter(0, NQ - 1, after=[(hp + LAG, 1, hp) for hp in range(HP - LAG)])
            quarter(1, 0, after=[(hp - HP + LAG, 1, hp) for hp in range(HP - LAG, HP)])
            with sp.Fori(1, NQ) as q:
                quarter(1, q)

        @block.tensor
        def _(pe):
            def values_wo(pair, q, hp):
                n, i, g = place(pair, q, hp), hp % NBUF, hp // 2
                pe.wait_ge(wo_hi_ready, n + 1)
                pe.wait_ge(wo_lo_ready, n + 1)
                wait(pe, vw_lo_ready, n - NBUF + 1)
                cols = slice(pair * PB * SK, (pair + 1) * PB * SK)
                for h in range(2):
                    last = three(pe, vw_ps[i][:, h, :], vt_hi[:, g, cols], vt_lo[:, g, cols],
                                 wo_hi[:, i, h, :], wo_lo[:, i, h, :], True, True)
                last.then_inc(vw_done, 1)

            def probs_times(pair, q, hp):
                n, i = place(pair, q, hp), hp % NBUF
                pe.wait_ge(vw_hi_ready, n + 1)
                pe.wait_ge(vw_lo_ready, n + 1)
                pe.wait_ge(p_in[hp], 32 * (pair + 1))
                for bank in range(NACC):
                    d, b = bank // PB, bank % PB
                    if hp == 0:
                        wait(pe, acc_read, NACC * (pair * NQ + q - 1) + bank + 1)
                    last = three(pe, acc_ps[bank][:], vw_hi[:, i, b, d * P:(d + 1) * P], vw_lo[:, i, b, d * P:(d + 1) * P],
                                 p_hi[:, hp, b * S:(b + 1) * S], p_lo[:, hp, b * S:(b + 1) * S], hp == 0, hp == HP - 1)
                    if hp == HP - 1 and bank < NACC - 1:
                        last.then_inc(acc_done, 1)
                last.then_inc(av_done, 1)

            def quarter(pair, q, following):
                for hp in range(HP):
                    if hp + VW_AHEAD < HP:
                        values_wo(pair, q, hp + VW_AHEAD)
                    elif following is not None:
                        values_wo(*following, hp + VW_AHEAD - HP)
                    probs_times(pair, q, hp)

            pe.wait_ge(vt_in, 32)
            for hp in range(VW_AHEAD):
                values_wo(0, 0, hp)
            over_quarters(pe, quarter)

        @block.scalar
        def _(act):
            def split_wo(pair, q, hp):
                n, i = place(pair, q, hp), hp % NBUF
                act.wait_ge(wo_in[i], 16 * ((pair * NQ + q) * (HP // NBUF) + hp // NBUF + 1))
                wait(act, vw_done, n - NBUF + 1)
                nc.scalar.copy(wo_hi[:, i], wo_raw[:, i]).then_inc(wo_hi_ready, 1)

            def split_vw(pair, q, hp):
                n, i = place(pair, q, hp), hp % NBUF
                act.wait_ge(vw_done, n + 1)
                wait(act, av_done, n - NBUF + 1)
                for b in range(PB):
                    for h in range(2):
                        done = nc.scalar.copy(vw_hi[h * SK:(h + 1) * SK, i, b, :], vw_ps[i][b * SK:(b + 1) * SK, h, :])
                done.then_inc(vw_hi_ready, 1)

            def quarter(pair, q, following):
                for hp in range(HP):
                    for ahead, split in ((VW_AHEAD, split_vw), (WO_AHEAD, split_wo)):
                        if hp + ahead < HP:
                            split(pair, q, hp + ahead)
                        elif following is not None:
                            split(*following, hp + ahead - HP)
                wait(act, attn_stored, 16 * (pair * NQ + q))
                for bank in range(NACC):
                    if bank < NACC - 1:
                        act.wait_ge(acc_done, (NACC - 1) * (pair * NQ + q) + bank + 1)
                    else:
                        act.wait_ge(av_done, HP * (pair * NQ + q + 1))
                    nc.scalar.activation(attn_sb[:, bank // PB, bank % PB, :], acc_ps[bank][:], ACT.Copy,
                                         scale=tanh_gate[:, 0:1]).then_inc(acc_read, 1)
                act.wait_ge(acc_read, NACC * (pair * NQ + q + 1))
                dst = scratch["attn"].rearrange("(q d p) t -> q p d t", p=P, d=QW // P)[bass.ds(q, 1), :, :, pair * PB * S:(pair + 1) * PB * S]
                act.dma_start(dst.rearrange("o p d t -> p (o d) t"), attn_sb[:].rearrange("p d b t -> p d (b t)")).then_inc(attn_stored, 16)

            act.wait_ge(gate_in, 16)
            nc.scalar.activation(tanh_gate[:], gate[:], ACT.Tanh).then_inc(gate_ready, 1)
            act.wait_ge(gate_ready, 1)
            for hp in range(NBUF):
                split_wo(0, 0, hp)
            for hp in range(VW_AHEAD):
                split_vw(0, 0, hp)
            for hp in range(NBUF, WO_AHEAD):
                split_wo(0, 0, hp)
            over_quarters(act, quarter)
            act.wait_ge(attn_stored, 16 * PAIRS * NQ)

        @block.gpsimd
        def _(pool):
            for pair in range(PAIRS):
                with pool.Fori(0, NQ) as q:
                    for hp in range(HP):
                        i = hp % NBUF
                        pool.wait_ge(wo_hi_ready, place(pair, q, hp) + 1)
                        nc.gpsimd.tensor_tensor(wo_lo[:, i], wo_raw[:, i], wo_hi[:, i].bitcast(F32),
                                                ALU.subtract).then_inc(wo_lo_ready, 1)

        @block.vector
        def _(dve):
            for pair in range(PAIRS):
                with dve.Fori(0, NQ) as q:
                    for hp in range(HP):
                        i = hp % NBUF
                        dve.wait_ge(vw_hi_ready, place(pair, q, hp) + 1)
                        for b in range(PB):
                            for h in range(2):
                                at = (slice(h * SK, (h + 1) * SK), i, b)
                                done = nc.vector.tensor_tensor(vw_lo[at], vw_ps[i][b * SK:(b + 1) * SK, h, :],
                                                               vw_hi[at].bitcast(F32), ALU.subtract)
                        done.then_inc(vw_lo_ready, 1)


def feed(nc, a, scratch, ident, out):
    NT = BT // P
    NC = NT * 2
    HW = D // 2
    NW = 4
    with ExitStack() as ctx:
        def sb(name, shape, dt=F32):
            return ctx.enter_context(nc.sbuf_tensor(name, shape, dt))

        def ps(name, shape):
            return ctx.enter_context(nc.psum_tensor(name, shape, F32))

        def sem(name):
            return ctx.enter_context(nc.semaphore(name))

        w_raw = sb("ffn_w_raw", [P, 2, D])
        w_sign = sb("w_sign", [P, KT, D], F32R)
        bias = sb("bias", [P, D])
        gate_w = sb("gate_w", [P, KT, E])
        gate = sb("gate_f", [P, 1])
        tanh_gate = sb("tanh_gate_f", [P, 1])
        row_is_hi = sb("row_is_hi", [P, 2])
        scale_raw = sb("scale_raw", [P, 2, D])
        scale_hi = sb("scale_hi", [P, 2, D], F32R)
        scale_lo = sb("scale_lo", [P, 2, D])
        scale_stack = sb("scale_stack", [P, 2, D], F32R)
        zeros = sb("zeros", [P, BT])
        attn_in_sb = sb("attn_in_sb", [P, KT, BT])
        x_in_sb = sb("x_in_sb", [P, NT, D])
        x1 = sb("x1", [P, 2, NT, D])
        x1n = sb("x1n", [P, NT, D])
        x1n_t = sb("x1n_t", [P, KT, BT])
        xs = sb("xs", [P, KT, BT])
        xs_hi = sb("xs_hi", [P, 2, KT, BT], F32R)
        xs_lo = sb("xs_lo", [P, 2, KT, BT], F32R)
        out_scale = sb("out_scale_sb", [P, 2, HW])
        y_part = sb("y_part", [P, 2, HW])
        y = sb("y", [P, NC, HW])
        stats = sb("ffn_stats", [P, NT, 2, 6])
        mean_var = sb("ffn_mean_var", [P, NT, 2])
        var_eps = sb("ffn_var_eps", [P, NT])
        rstd = sb("ffn_rstd", [P, NT])
        minus_half = sb("ffn_minus_half", [P, NT])
        logits_t = sb("logits_t", [E, BT])
        r_max = sb("r_max", [P, NT])
        r_exp = sb("r_exp", [P, NT, E])
        r_sum = sb("r_sum", [P, NT])
        r_inv = sb("r_inv", [P, NT])
        routing = sb("routing", [P, NT, E])
        r_stack = sb("r_stack", [P, NT, 4, E], F32R)
        r_stack_t = sb("r_stack_t", [P, 2, BT], F32R)
        wk = [ps(f"wk{i}", [P, 512]) for i in range(NW)]
        f_ps = [ps(f"f_ps{i}", [P, HW]) for i in range(2)]
        o_ps = ps("o_ps", [P, HW])
        r_ps = ps("r_ps", [P, 512])

        consts_in = sem("ffn_consts_in")
        w_in = [sem(f"ffn_w_in{i}") for i in range(2)]
        sign_ready = sem("sign_ready")
        setup_d = sem("setup_d")
        setup_a = sem("setup_a")
        bias_ready = sem("bias_ready")
        half_ready = sem("ffn_half_ready")
        attn_in = sem("attn_in")
        x_in = sem("x_in")
        ta_done = sem("ta_done")
        x1_ready = sem("x1_ready")
        stats_ready = sem("ffn_stats_ready")
        mean_ready = sem("ffn_mean_ready")
        var_ready = sem("ffn_var_ready")
        rstd_ready = sem("ffn_rstd_ready")
        x1n_ready = sem("x1n_ready")
        x1b_ready = sem("x1b_ready")
        tb_done = sem("tb_done")
        x1n_t_ready = sem("x1n_t_ready")
        logits_done = sem("logits_done")
        logits_copied = sem("logits_copied")
        lt_done = sem("lt_done")
        r_max_ready = sem("r_max_ready")
        r_shift_ready = sem("r_shift_ready")
        r_exp_ready = sem("r_exp_ready")
        r_sum_ready = sem("r_sum_ready")
        r_inv_ready = sem("r_inv_ready")
        routing_ready = sem("routing_ready")
        r_hi_ready = sem("r_hi_ready")
        r_stack_ready = sem("r_stack_ready")
        rt_done = sem("rt_done")
        r_stack_t_ready = sem("r_stack_t_ready")
        is_done = sem("is_done")
        xs_ready = sem("xs_ready")
        xs_hi_ready = sem("xs_hi_ready")
        xs_lo_ready = sem("xs_lo_ready")
        os_done = sem("os_done")
        os_copied = sem("os_copied")
        f_done = sem("f_done")
        y_part_ready = sem("y_part_ready")
        y_ready = sem("y_ready")
        y_stored = [sem(f"y_stored{i}") for i in range(NC)]

        block = ctx.enter_context(nc.Block())

        def over_blocks(eng, slot, peel_last):
            slot(0, 0, False)
            slot(1, 1, False)
            with eng.Fori(1, NB // 2 - 1 if peel_last else NB // 2) as g:
                slot(2 * g, 0, False)
                slot(2 * g + 1, 1, False)
            if peel_last:
                slot(NB - 2, 0, False)
                slot(NB - 1, 1, True)
            slot(NB, 0, True)

        def has(i, lag):
            return 0 <= i - lag < NB if isinstance(i, int) else True

        @block.sync
        def _(sp):
            def load(i):
                wait(sp, ta_done, i)
                src = scratch["attn"].rearrange("(k p) (i t) -> i p k t", p=P, t=BT)[bass.ds(i, 1)]
                sp.dma_start(attn_in_sb[:], src.rearrange("o p k t -> p (o k) t")).then_inc(attn_in, 16)
                wait(sp, x1_ready, i)
                src = a["x"].rearrange("(i n p) d -> i p n d", p=P, n=NT)[bass.ds(i, 1)]
                sp.dma_start(x_in_sb[:], src.rearrange("o p n d -> p (o n) d")).then_inc(x_in, 16)

            def slot(i, j, last):
                if not last:
                    load(i + 1)
                if has(i, 1):
                    for c in range(NC):
                        wait(sp, y_ready, NC * (i - 1) + c + 1)
                        dst = out.rearrange("(i n p) (h w) -> i n h p w", p=P, n=NT, h=2)[bass.ds(i - 1, 1), c // 2, c % 2]
                        sp.dma_start(dst.rearrange("o p w -> (o p) w"), y[:, c]).then_inc(y_stored[c], 16)

            load(0)
            sp.dma_start(gate[:], a["g_ffn"]).then_inc(consts_in, 16)
            sp.dma_start(gate_w[:], a["gate_t"]).then_inc(consts_in, 16)
            sp.dma_start(scale_raw[:, 0], a["in_scale"]).then_inc(consts_in, 16)
            sp.dma_start(scale_raw[:, 1], a["out_scale"]).then_inc(consts_in, 16)
            sp.dma_start(row_is_hi[:], a["row_is_hi"]).then_inc(consts_in, 16)
            sp.dma_start(bias[:], a["bias"]).then_inc(consts_in, 16)
            for k in range(KT):
                wait(sp, sign_ready, k - 1)
                sp.dma_start(w_raw[:, k % 2], a["weight_t"][k * P:(k + 1) * P, :]).then_inc(w_in[k % 2], 16)
            over_blocks(sp, slot, True)
            for c in range(NC):
                sp.wait_ge(y_stored[c], 16 * NB)

        @block.tensor
        def _(pe):
            def out_scales(i, j, c):
                wait(pe, os_copied, NC * i + c)
                t, h = c // 2, c % 2
                pe.matmul(o_ps[:], r_stack_t[:, j, t * P:(t + 1) * P], scale_stack[:, 1, h * HW:(h + 1) * HW],
                          start=True, stop=True).then_inc(os_done, 1)

            def products(i, j, c, ks):
                t, h = c // 2, c % 2
                if ks[0] == 0:
                    wait(pe, y_part_ready, NC * i + c - 1)
                for k in ks:
                    if c == 0 and k % 2 == 0:
                        pe.wait_ge(xs_lo_ready, 4 * i + k // 2 + 1)
                    for n, part in enumerate((xs_hi, xs_lo)):
                        last = pe.matmul(f_ps[c % 2][:], part[:, j, k, t * P:(t + 1) * P], w_sign[:, k, h * HW:(h + 1) * HW],
                                         start=(k == 0 and n == 0), stop=(k == KT - 1 and n == 1))
                if ks[-1] == KT - 1:
                    last.then_inc(f_done, 1)

            def slot(i, j, last_block):
                if has(i, 0):
                    pe.wait_ge(attn_in, 16 * (i + 1))
                    wait(pe, xs_ready, 4 * i)
                    for t in range(NT):
                        for k in range(KT):
                            last = pe.transpose(wk[2 * t + k // 4][:, k % 4 * P:(k % 4 + 1) * P],
                                                attn_in_sb[:, k, t * P:(t + 1) * P], ident[:])
                    last.then_inc(ta_done, 1)
                if has(i, 1):
                    if isinstance(i, int) and i == 1:
                        pe.wait_ge(sign_ready, KT)
                    for c in range(NC - 1):
                        out_scales(i - 1, 1 - j, c)
                        products(i - 1, 1 - j, c, range(KT))
                if has(i, 0):
                    pe.wait_ge(x1n_ready, i + 1)
                    for t in range(NT):
                        for k in range(KT):
                            last = pe.transpose(wk[k // 2][:, k % 2 * BT + t * P:k % 2 * BT + (t + 1) * P],
                                                x1n[:, t, k * P:(k + 1) * P], ident[:])
                    last.then_inc(tb_done, 1)
                if has(i, 1):
                    out_scales(i - 1, 1 - j, NC - 1)
                    products(i - 1, 1 - j, NC - 1, range(0, 3))
                if has(i, 0):
                    pe.wait_ge(x1n_t_ready, i + 1)
                    wait(pe, r_stack_t_ready, i)
                    for k in range(KT):
                        last = pe.matmul(r_ps[0:E, 0:BT], gate_w[:, k, :], x1n_t[:, k, :], start=k == 0, stop=k == KT - 1)
                    last.then_inc(logits_done, 1)
                if has(i, 1):
                    products(i - 1, 1 - j, NC - 1, range(3, 4))
                if has(i, 0):
                    pe.wait_ge(logits_copied, i + 1)
                if has(i, 1):
                    products(i - 1, 1 - j, NC - 1, range(4, 5))
                if has(i, 0):
                    for t in range(NT):
                        last = pe.transpose(r_ps[:, BT + t * E:BT + (t + 1) * E], logits_t[:, t * P:(t + 1) * P], ident[0:E, 0:E])
                    last.then_inc(lt_done, 1)
                if has(i, 1):
                    products(i - 1, 1 - j, NC - 1, range(5, KT))
                if has(i, 0):
                    pe.wait_ge(r_stack_ready, i + 1)
                    for t in range(NT):
                        last = pe.transpose(r_ps[0:4 * E, t * P:(t + 1) * P], r_stack[:, t].rearrange("p n e -> p (n e)").bitcast(F32), ident[:])
                    last.then_inc(rt_done, 1)
                    pe.wait_ge(r_stack_t_ready, i + 1)
                    for k in range(KT):
                        last = pe.matmul(wk[k // 2][:, k % 2 * BT:(k % 2 + 1) * BT], scale_stack[:, 0, k * P:(k + 1) * P],
                                         r_stack_t[:, j, :], start=True, stop=True)
                    last.then_inc(is_done, 1)

            pe.wait_ge(consts_in, 96)
            pe.wait_ge(setup_d, 5)
            over_blocks(pe, slot, False)

        @block.scalar
        def _(act):
            def copy_out_scales(i, c):
                act.wait_ge(os_done, NC * i + c + 1)
                wait(act, y_part_ready, NC * i + c - 1)
                nc.scalar.copy(out_scale[:, c % 2], o_ps[:]).then_inc(os_copied, 1)

            def slot(i, j, last):
                if has(i, 1):
                    for c in range(NC - 1):
                        copy_out_scales(i - 1, c)
                if has(i, 0):
                    act.wait_ge(tb_done, i + 1)
                    wait(act, xs_ready, 4 * i)
                    for m in range(NW):
                        done = nc.scalar.copy(x1n_t[:, 2 * m:2 * m + 2, :], wk[m][:].rearrange("p (k t) -> p k t", k=2))
                    done.then_inc(x1n_t_ready, 1)
                if has(i, 1):
                    copy_out_scales(i - 1, NC - 1)
                if has(i, 0):
                    act.wait_ge(logits_done, i + 1)
                    wait(act, lt_done, i)
                    nc.scalar.copy(logits_t[:], r_ps[0:E, 0:BT]).then_inc(logits_copied, 1)
                    act.wait_ge(r_shift_ready, i + 1)
                    nc.scalar.activation(r_exp[:], routing[:], ACT.Exp).then_inc(r_exp_ready, 1)
                    act.wait_ge(rt_done, i + 1)
                    wait(act, os_done, NC * (i - 1))
                    nc.scalar.copy(r_stack_t[0:4 * E, j, :], r_ps[0:4 * E, 0:BT]).then_inc(r_stack_t_ready, 1)
                    wait(act, f_done, NC * (i - 1))
                    for m in range(NW):
                        act.wait_ge(xs_ready, 4 * i + m + 1)
                        nc.scalar.copy(xs_hi[:, j, 2 * m:2 * m + 2, :], xs[:, 2 * m:2 * m + 2, :]).then_inc(xs_hi_ready, 1)

            act.wait_ge(consts_in, 96)
            nc.scalar.activation(tanh_gate[:], gate[:], ACT.Tanh).then_inc(setup_a, 1)
            for k in range(KT):
                act.wait_ge(w_in[k % 2], 16 * (k // 2 + 1))
                nc.scalar.activation(w_sign[:, k, :], w_raw[:, k % 2], ACT.Sign).then_inc(sign_ready, 1)
            over_blocks(act, slot, False)

        @block.gpsimd
        def _(pool):
            def add(i, j, c):
                t, h = c // 2, c % 2
                pool.wait_ge(y_part_ready, NC * i + c + 1)
                pool.wait_ge(x1b_ready, i + 1)
                wait(pool, y_stored[c], 16 * i)
                nc.gpsimd.tensor_tensor(y[:, c], y_part[:, c % 2], x1[:, j, t, h * HW:(h + 1) * HW], ALU.add).then_inc(y_ready, 1)

            def slot(i, j, last):
                if has(i, 0):
                    pool.wait_ge(var_ready, i + 1)
                    wait(pool, x1n_ready, i)
                    nc.gpsimd.tensor_tensor(rstd[:], var_eps[:], minus_half[:], ALU.pow).then_inc(rstd_ready, 1)
                if has(i, 1):
                    add(i - 1, 1 - j, 0)
                    add(i - 1, 1 - j, 1)
                if has(i, 0):
                    pool.wait_ge(x1n_ready, i + 1)
                    nc.gpsimd.tensor_tensor(x1[:, j], x1[:, j], bias[:].unsqueeze(1).to_broadcast([P, NT, D]), ALU.add).then_inc(x1b_ready, 1)
                if has(i, 1):
                    add(i - 1, 1 - j, 2)
                    add(i - 1, 1 - j, 3)

            nc.gpsimd.memset(minus_half[:], -0.5).then_inc(half_ready, 1)
            pool.wait_ge(half_ready, 1)
            pool.wait_ge(bias_ready, 1)
            over_blocks(pool, slot, False)

        @block.vector
        def _(dve):
            def scaled(i, c):
                dve.wait_ge(f_done, NC * i + c + 1)
                dve.wait_ge(os_copied, NC * i + c + 1)
                wait(dve, y_ready, NC * i + c - 1)
                nc.vector.tensor_tensor(y_part[:, c % 2], f_ps[c % 2][:], out_scale[:, c % 2], ALU.mult).then_inc(y_part_ready, 1)

            def slot(i, j, last):
                if has(i, 0):
                    dve.wait_ge(ta_done, i + 1)
                    dve.wait_ge(x_in, 16 * (i + 1))
                    wait(dve, y_ready, NC * (i - 1))
                    for t in range(NT):
                        for h in range(2):
                            at = (slice(None), t, slice(h * HW, (h + 1) * HW))
                            done = nc.vector.tensor_tensor(x1[:, j][at], wk[2 * t + h][:], x_in_sb[at], ALU.add)
                    done.then_inc(x1_ready, 1)
                    dve.wait_ge(x1_ready, i + 1)
                    for t in range(NT):
                        for h in range(2):
                            done = nc.vector.bn_stats(stats[:, t, h, :], x1[:, j, t, h * HW:(h + 1) * HW])
                    done.then_inc(stats_ready, 1)
                    dve.wait_ge(stats_ready, i + 1)
                if has(i, 1):
                    scaled(i - 1, 0)
                if has(i, 0):
                    for t in range(NT):
                        done = nc.vector.bn_aggr(mean_var[:, t, :], stats[:, t])
                    done.then_inc(mean_ready, 1)
                    dve.wait_ge(mean_ready, i + 1)
                    wait(dve, rstd_ready, i)
                    nc.vector.tensor_scalar(var_eps[:], mean_var[:, :, 1], EPS, None, ALU.add).then_inc(var_ready, 1)
                if has(i, 0):
                    dve.wait_ge(rstd_ready, i + 1)
                    wait(dve, tb_done, i)
                    for t in range(NT):
                        done = nc.vector.tensor_scalar(x1n[:, t], x1[:, j, t], mean_var[:, t, 0:1], rstd[:, t:t + 1],
                                                       ALU.subtract, ALU.mult)
                    done.then_inc(x1n_ready, 1)
                if has(i, 1):
                    scaled(i - 1, 1)
                    scaled(i - 1, 2)
                if has(i, 0):
                    logits = r_ps[:, BT:BT + NT * E].rearrange("p (t e) -> p t e", e=E)
                    dve.wait_ge(lt_done, i + 1)
                    nc.vector.tensor_reduce(r_max[:], logits, AX.X, ALU.max).then_inc(r_max_ready, 1)
                    dve.wait_ge(r_max_ready, i + 1)
                    nc.vector.tensor_tensor(routing[:], logits, r_max[:].unsqueeze(2).to_broadcast([P, NT, E]),
                                            ALU.subtract).then_inc(r_shift_ready, 1)
                    dve.wait_ge(r_exp_ready, i + 1)
                    nc.vector.tensor_reduce(r_sum[:], r_exp[:], AX.X, ALU.add).then_inc(r_sum_ready, 1)
                    dve.wait_ge(r_sum_ready, i + 1)
                    nc.vector.reciprocal(r_inv[:], r_sum[:]).then_inc(r_inv_ready, 1)
                    dve.wait_ge(r_inv_ready, i + 1)
                    nc.vector.tensor_tensor(routing[:], r_exp[:], r_inv[:].unsqueeze(2).to_broadcast([P, NT, E]),
                                            ALU.mult).then_inc(routing_ready, 1)
                    dve.wait_ge(routing_ready, i + 1)
                    wait(dve, rt_done, i)
                    nc.vector.tensor_copy(r_stack[:, :, 0:2, :], routing[:].unsqueeze(2).to_broadcast([P, NT, 2, E])).then_inc(r_hi_ready, 1)
                    dve.wait_ge(r_hi_ready, i + 1)
                    for n in range(2):
                        done = nc.vector.tensor_tensor(r_stack[:, :, 2 + n, :], routing[:], r_stack[:, :, 0, :].bitcast(F32), ALU.subtract)
                    done.then_inc(r_stack_ready, 1)
                if has(i, 1):
                    scaled(i - 1, 3)
                if has(i, 0):
                    dve.wait_ge(is_done, i + 1)
                    wait(dve, xs_lo_ready, 4 * i)

                    def low(m):
                        dve.wait_ge(xs_hi_ready, 4 * i + m + 1)
                        at = (slice(None), slice(2 * m, 2 * m + 2))
                        nc.vector.tensor_tensor(xs_lo[:, j][at], xs[at], xs_hi[:, j][at].bitcast(F32), ALU.subtract).then_inc(xs_lo_ready, 1)

                    for m in range(NW):
                        at = (slice(None), slice(2 * m, 2 * m + 2))
                        nc.vector.tensor_tensor(xs[at], wk[m][:].rearrange("p (k t) -> p k t", k=2), x1n_t[at], ALU.mult).then_inc(xs_ready, 1)
                        if m >= 1:
                            low(m - 1)
                    low(NW - 1)

            nc.vector.memset(zeros[:], 0.0).then_inc(setup_d, 1)
            dve.wait_ge(consts_in, 96)
            dve.wait_ge(setup_d, 1)
            for n in range(2):
                done = nc.vector.tensor_copy(r_stack_t[:, n], zeros[:])
            dve.wait_ge(setup_a, 1)
            nc.vector.tensor_scalar(bias[:], bias[:], tanh_gate[:, 0:1], None, ALU.mult).then_inc(bias_ready, 1)
            nc.vector.tensor_scalar(scale_raw[:, 1], scale_raw[:, 1], tanh_gate[:, 0:1], None, ALU.mult).then_inc(setup_d, 1)
            dve.wait_ge(setup_d, 2)
            nc.vector.tensor_copy(scale_hi[:], scale_raw[:]).then_inc(setup_d, 1)
            dve.wait_ge(setup_d, 3)
            nc.vector.tensor_tensor(scale_lo[:], scale_raw[:], scale_hi[:].bitcast(F32), ALU.subtract).then_inc(setup_d, 1)
            dve.wait_ge(setup_d, 4)
            nc.vector.tensor_scalar(scale_lo[:], scale_lo[:], row_is_hi[:, 1:2], None, ALU.mult).then_inc(bias_ready, 1)
            dve.wait_ge(bias_ready, 2)
            nc.vector.scalar_tensor_tensor(out=scale_stack[:], in0=scale_hi[:].bitcast(F32), scalar=row_is_hi[:, 0:1], in1=scale_lo[:],
                                           op0=ALU.mult, op1=ALU.add).then_inc(setup_d, 1)
            over_blocks(dve, slot, False)



_OUT = ((B, S, D), "float32")


def build(nc, a, out):
    scratch = {
        "keys": nc.dram_tensor("keys_scratch", (2, HKV * HALF, CTX), F32, kind="Internal").ap(),
        "values": nc.dram_tensor("values_scratch", (2, HKV, P, CTX), F32, kind="Internal").ap(),
        "probs": nc.dram_tensor("probs_scratch", (2, HP, P, T), F32, kind="Internal").ap(),
        "attn": nc.dram_tensor("attn_scratch", (D, T), F32, kind="Internal").ap(),
    }
    with ExitStack() as ctx:
        ident = ctx.enter_context(nc.sbuf_tensor("ident", [P, P], F32))
        with nc.sbuf_tensor("x_hi", [P, KT, T], F32R) as x_hi, nc.sbuf_tensor("x_lo", [P, KT, T], F32R) as x_lo:
            prepare(nc, a, scratch, x_hi, x_lo, ident)
            attend(nc, a, scratch, x_hi, x_lo, ident)
        project(nc, a, scratch)
        feed(nc, a, scratch, ident, out)


def constants():
    inv_freq = (np.float32(1.0) / np.float32(10000.0) ** (np.arange(0, DK, 2, dtype=np.float32) / np.float32(DK)))
    angle = np.arange(S, dtype=np.float32)[:, None] * inv_freq.astype(np.float32)[None, :]
    cos = np.concatenate([np.cos(angle).T] * 2, 0).astype(np.float32)
    sin = np.concatenate([np.sin(angle).T] * 2, 0).astype(np.float32)
    scale = np.float32(1.0) / np.sqrt(np.float32(DK))
    row = np.arange(P)
    used = row < 4 * E
    is_hi = np.stack([used & (row // E % 2 == 0), used & (row // E % 2 == 1)], 1).astype(np.float32)
    return {
        "row_is_hi": is_hi,
        "ident": np.eye(P, dtype=np.float32), "cos_q": cos, "sin_q": sin,
        "cos_k": np.tile(cos[:, :SK] * scale, (1, B)), "sin_k": np.tile(sin[:, :SK] * scale, (1, B)),
    }


def laid_out(x, ctx_4096, mask_BxSxS2_ff0, g_xattn, g_ffn, L0_xattn_wq, L0_xattn_wk, L0_xattn_wv, L0_xattn_wo,
             L0_ffn_weight, L0_ffn_bias, L0_ffn_gate_w, L0_ffn_in_channel_scale, L0_ffn_out_channel_scale):
    n = np.asarray
    wk = n(L0_xattn_wk).reshape(KT, P, GP, 2, 2, HALF).transpose(2, 4, 1, 0, 3, 5).reshape(HKV, P, KT, P)
    wv = n(L0_xattn_wv).reshape(KT, P, HKV, P).transpose(2, 1, 0, 3)
    return {
        "x": n(x).reshape(T, D),
        "ctx_t": n(ctx_4096).reshape(CTX, D).T,
        "mask": n(mask_BxSxS2_ff0).reshape(B, TT, P, SK).transpose(2, 0, 1, 3),
        "g_xattn": np.broadcast_to(n(g_xattn), (P, 1)), "g_ffn": np.broadcast_to(n(g_ffn), (P, 1)),
        "wq": n(L0_xattn_wq).reshape(KT, P, HP, 2, 2, HALF).transpose(2, 4, 1, 0, 3, 5).reshape(HP, 2, P, KT, P),
        "wkv": np.concatenate([wk, wv], 0),
        "wo": n(L0_xattn_wo).reshape(HP, 2, P, NQ, QW).transpose(3, 0, 2, 1, 4),
        "weight_t": n(L0_ffn_weight).T,
        "bias": np.broadcast_to(n(L0_ffn_bias), (P, D)),
        "gate_t": n(L0_ffn_gate_w).T.reshape(KT, P, E).transpose(1, 0, 2),
        "in_scale": np.tile(n(L0_ffn_in_channel_scale), (P // E, 1)),
        "out_scale": np.tile(n(L0_ffn_out_channel_scale), (P // E, 1)),
    }


def kernel(**inputs):
    import concourse.bacc as bacc
    from concourse.bass_utils import run_bass_kernel_spmd

    nc = bacc.Bacc("TRN2", target_bir_lowering=False, num_devices=1)
    arrays, aps = {}, {}
    for name, value in (laid_out(**inputs) | constants()).items():
        value = np.ascontiguousarray(value)
        arrays[f"in_{name}"] = value
        aps[name] = nc.dram_tensor(f"in_{name}", value.shape, mybir.dt.from_np(value.dtype), kind="ExternalInput").ap()
    out = nc.dram_tensor("out_y", (T, D), F32, kind="ExternalOutput").ap()
    build(nc, aps, out)
    r = run_bass_kernel_spmd(nc, [arrays], core_ids=[0])
    return r.results[0]["out_y"].reshape(_OUT[0])
```

```python
from contextlib import ExitStack

import concourse.bass as bass
import numpy as np
from concourse import mybir

ALU = mybir.AluOpType
ACT = mybir.ActivationFunctionType
AX = mybir.AxisListType
F32 = mybir.dt.float32
F32R = mybir.dt.float32r

P = 128
B, S, D = 4, 512, 1024
SK = 64
HQ, HKV, DK = 32, 8, 128
E = 8
EPS = 1e-5
T = B * S
KT = D // P
HP = HQ // 2
HALF = DK // 2
TT = S // P
CTX = B * SK
GP = HKV // 2
NLN = T // P
PB = 2
NQ = 4
QW = D // NQ
BT = 256
NB = T // BT
WO_BUFS = 4
R = 4 * E


def wait(eng, semaphore, count):
    if isinstance(count, int) and count <= 0:
        return
    eng.wait_ge(semaphore, count)


def three(pe, out, hi, lo, rhs_hi, rhs_lo, first, last, **kw):
    pe.matmul(out, hi, rhs_hi, start=first, stop=False, **kw)
    pe.matmul(out, hi, rhs_lo, start=False, stop=False, **kw)
    return pe.matmul(out, lo, rhs_hi, start=False, stop=last, **kw)


def prepare(nc, a, scratch, x_hi, x_lo, ident):
    NU = 2 * HKV
    with ExitStack() as ctx:
        def sb(name, shape, dt=F32):
            return ctx.enter_context(nc.sbuf_tensor(name, shape, dt))

        def sem(name):
            return ctx.enter_context(nc.semaphore(name))

        ctx_raw = sb("ctx_raw", [P, KT, CTX])
        ctx_hi = sb("ctx_hi", [P, KT, CTX], F32R)
        ctx_lo = sb("ctx_lo", [P, KT, CTX], F32R)
        kw_raw = sb("kw_raw", [P, 2, KT, P])
        kw_hi = sb("kw_hi", [P, 2, KT, P], F32R)
        kw_lo = sb("kw_lo", [P, 2, KT, P], F32R)
        x_in = sb("x_in", [P, 2, D])
        xn = sb("xn", [P, 2, D])
        k_rot = sb("k_rot", [P, 4, CTX])
        v_hi = sb("v_hi", [P, 2, CTX], F32R)
        v_lo = sb("v_lo", [P, 2, CTX], F32R)
        cos_k = sb("cos_k", [P, CTX])
        sin_k = sb("sin_k", [P, CTX])
        stats = sb("stats", [P, 2, 2, 6])
        mean_var = sb("mean_var", [P, 2, 2])
        var_eps = sb("var_eps", [P, 2])
        rstd = sb("rstd", [P, 2])
        minus_half = sb("minus_half", [P, 1])
        kv_ps = [ctx.enter_context(nc.psum_tensor(f"kv_ps{i}", [P, 512], F32)) for i in range(4)]
        xt_ps = [ctx.enter_context(nc.psum_tensor(f"xt_ps{i}", [P, 4, P], F32)) for i in range(4)]

        consts_in = sem("consts_in")
        ctx_in = sem("ctx_in")
        ctx_hi_ready = sem("ctx_hi_ready")
        ctx_lo_ready = sem("ctx_lo_ready")
        kw_in = [sem(f"kw_in{i}") for i in range(2)]
        kw_hi_ready = sem("kw_hi_ready")
        kw_lo_ready = sem("kw_lo_ready")
        kv_done = sem("kv_done")
        k_read = sem("k_read")
        k_roped = sem("k_roped")
        k_stored = sem("k_stored")
        v_hi_ready = sem("v_hi_ready")
        v_lo_ready = sem("v_lo_ready")
        v_stored = [sem(f"v_stored{i}") for i in range(2)]
        x_in_sem = [sem(f"x_in_sem{i}") for i in range(2)]
        half_ready = sem("half_ready")
        stats_ready = sem("stats_ready")
        mean_ready = sem("mean_ready")
        var_ready = sem("var_ready")
        rstd_ready = sem("rstd_ready")
        xn_ready = sem("xn_ready")
        xt_ready = sem("xt_ready")
        x_hi_ready = sem("x_hi_ready")
        x_lo_ready = sem("x_lo_ready")

        block = ctx.enter_context(nc.Block())

        @block.sync
        def _(sp):
            sp.dma_start(ctx_raw[:], a["ctx_t"].rearrange("(k p) t -> p k t", p=P)).then_inc(ctx_in, 16)
            sp.dma_start(x_in[:, 0], a["x"][0:P, :]).then_inc(x_in_sem[0], 16)
            sp.dma_start(ident[:], a["ident"]).then_inc(consts_in, 16)
            sp.dma_start(cos_k[:], a["cos_k"]).then_inc(consts_in, 16)
            sp.dma_start(sin_k[:], a["sin_k"]).then_inc(consts_in, 16)
            for n in range(NU):
                wait(sp, kw_lo_ready, n - 1)
                sp.dma_start(kw_raw[:, n % 2], a["wkv"][n]).then_inc(kw_in[n % 2], 16)
                if n + 1 < NLN:
                    wait(sp, xn_ready, n)
                    sp.dma_start(x_in[:, (n + 1) % 2], a["x"][(n + 1) * P:(n + 2) * P, :]).then_inc(x_in_sem[(n + 1) % 2], 16)

        @block.tensor
        def _(pe):
            pe.wait_ge(consts_in, 48)
            for n in range(NU + 1):
                if n < NU:
                    if n == 0:
                        pe.wait_ge(ctx_hi_ready, 1)
                        pe.wait_ge(ctx_lo_ready, 1)
                    pe.wait_ge(kw_hi_ready, n + 1)
                    pe.wait_ge(kw_lo_ready, n + 1)
                    if n >= 4 + HKV:
                        pe.wait_ge(v_lo_ready, n - 4 - HKV + 1)
                    elif n >= 4:
                        pe.wait_ge(k_read, (n - 4) // 2 + 1)
                    for k in range(KT):
                        last = three(pe, kv_ps[n % 4][:, 0:CTX], kw_hi[:, n % 2, k, :], kw_lo[:, n % 2, k, :],
                                     ctx_hi[:, k, :], ctx_lo[:, k, :], k == 0, k == KT - 1)
                    last.then_inc(kv_done, 1)
                if n >= 1:
                    i = n - 1
                    pe.wait_ge(xn_ready, i + 1)
                    wait(pe, x_lo_ready, i - 1)
                    for k in range(KT):
                        last = pe.transpose(xt_ps[2 * (i % 2) + k // 4][:, k % 4, :],
                                            xn[:, i % 2, k * P:(k + 1) * P], ident[:])
                    last.then_inc(xt_ready, 1)

        @block.scalar
        def _(act):
            act.wait_ge(ctx_in, 16)
            nc.scalar.copy(ctx_hi[:], ctx_raw[:]).then_inc(ctx_hi_ready, 1)

            def turned(i):
                act.wait_ge(xt_ready, i + 1)
                for j in range(2):
                    last = nc.scalar.copy(x_hi[:, 4 * j:4 * j + 4, i * P:(i + 1) * P], xt_ps[2 * (i % 2) + j][:])
                last.then_inc(x_hi_ready, 1)

            for n in range(NU + 2):
                if n < NU:
                    act.wait_ge(kw_in[n % 2], 16 * (n // 2 + 1))
                    wait(act, kv_done, n - 1)
                    nc.scalar.copy(kw_hi[:, n % 2], kw_raw[:, n % 2]).then_inc(kw_hi_ready, 1)
                if HKV <= n - 1 < NU:
                    g = n - 1 - HKV
                    act.wait_ge(kv_done, n)
                    wait(act, v_stored[g % 2], 32 * (g // 2))
                    nc.scalar.copy(v_hi[:, g % 2], kv_ps[(n - 1) % 4][:, 0:CTX]).then_inc(v_hi_ready, 1)
                if n >= 2:
                    turned(n - 2)
            act.wait_ge(k_stored, 32 * GP)
            for i in range(2):
                act.wait_ge(v_stored[i], 32 * HKV // 2)

        @block.gpsimd
        def _(pool):
            nc.gpsimd.memset(minus_half[:], -0.5).then_inc(half_ready, 1)
            pool.wait_ge(half_ready, 1)
            def store_values(g):
                pool.wait_ge(v_lo_ready, g + 1)
                pool.dma_start(scratch["values"][0, g], v_hi[:, g % 2].bitcast(F32)).then_inc(v_stored[g % 2], 16)
                pool.dma_start(scratch["values"][1, g], v_lo[:, g % 2].bitcast(F32)).then_inc(v_stored[g % 2], 16)

            for n in range(NU):
                pool.wait_ge(var_ready, n + 1)
                wait(pool, xn_ready, n - 1)
                nc.gpsimd.tensor_tensor(rstd[:, n % 2:n % 2 + 1], var_eps[:, n % 2:n % 2 + 1], minus_half[:],
                                        ALU.pow).then_inc(rstd_ready, 1)
                pool.wait_ge(kw_hi_ready, n + 1)
                nc.gpsimd.tensor_tensor(kw_lo[:, n % 2], kw_raw[:, n % 2], kw_hi[:, n % 2].bitcast(F32),
                                        ALU.subtract).then_inc(kw_lo_ready, 1)
                if n >= 1 and (n - 1) < HKV and (n - 1) % 2 == 1:
                    gp = (n - 1) // 2
                    pool.wait_ge(k_roped, gp + 1)
                    for c in range(2):
                        pool.dma_start(scratch["keys"][c, gp * P:(gp + 1) * P, :], k_rot[:, 2 * c, :]).then_inc(k_stored, 16)
                if n >= HKV + 2:
                    store_values(n - HKV - 2)
            store_values(HKV - 2)
            store_values(HKV - 1)

        @block.vector
        def _(dve):
            def statistics(i):
                dve.wait_ge(x_in_sem[i % 2], 16 * (i // 2 + 1))
                for j in range(2):
                    last = nc.vector.bn_stats(stats[:, i % 2, j, :], x_in[:, i % 2, j * 512:(j + 1) * 512])
                last.then_inc(stats_ready, 1)
                dve.wait_ge(stats_ready, i + 1)
                nc.vector.bn_aggr(mean_var[:, i % 2, :], stats[:, i % 2]).then_inc(mean_ready, 1)
                dve.wait_ge(mean_ready, i + 1)
                wait(dve, rstd_ready, i - 1)
                nc.vector.tensor_scalar(var_eps[:, i % 2:i % 2 + 1], mean_var[:, i % 2, 1:2], EPS, None,
                                        ALU.add).then_inc(var_ready, 1)

            def rotate(gp):
                k1, k2 = kv_ps[(2 * gp) % 4][:, 0:CTX], kv_ps[(2 * gp + 1) % 4][:, 0:CTX]
                dve.wait_ge(kv_done, 2 * gp + 2)
                wait(dve, k_stored, 32 * gp)
                nc.vector.tensor_tensor(k_rot[:, 0], k1, cos_k[:], ALU.mult)
                nc.vector.tensor_tensor(k_rot[:, 1], k2, sin_k[:], ALU.mult)
                nc.vector.tensor_tensor(k_rot[:, 2], k2, cos_k[:], ALU.mult)
                nc.vector.tensor_tensor(k_rot[:, 3], k1, sin_k[:], ALU.mult).then_inc(k_read, 1)
                dve.wait_ge(k_read, gp + 1)
                nc.vector.tensor_tensor(k_rot[:, 0], k_rot[:, 0], k_rot[:, 1], ALU.subtract)
                nc.vector.tensor_tensor(k_rot[:, 2], k_rot[:, 2], k_rot[:, 3], ALU.add).then_inc(k_roped, 1)

            statistics(0)
            dve.wait_ge(ctx_hi_ready, 1)
            nc.vector.tensor_tensor(ctx_lo[:], ctx_raw[:], ctx_hi[:].bitcast(F32), ALU.subtract).then_inc(ctx_lo_ready, 1)
            dve.wait_ge(consts_in, 48)
            for n in range(NU + 2):
                if n < NLN:
                    dve.wait_ge(rstd_ready, n + 1)
                    wait(dve, xt_ready, n - 1)
                    nc.vector.tensor_scalar(xn[:, n % 2], x_in[:, n % 2], mean_var[:, n % 2, 0:1], rstd[:, n % 2:n % 2 + 1],
                                            ALU.subtract, ALU.mult).then_inc(xn_ready, 1)
                    if n + 1 < NLN:
                        statistics(n + 1)
                if 0 <= n - 1 < HKV and (n - 1) % 2 == 1:
                    rotate((n - 1) // 2)
                if HKV <= n - 1 < NU:
                    g = n - 1 - HKV
                    dve.wait_ge(v_hi_ready, g + 1)
                    wait(dve, v_stored[g % 2], 32 * (g // 2))
                    nc.vector.tensor_tensor(v_lo[:, g % 2], kv_ps[(n - 1) % 4][:, 0:CTX], v_hi[:, g % 2].bitcast(F32),
                                            ALU.subtract).then_inc(v_lo_ready, 1)
                if n >= 2:
                    i = n - 2
                    dve.wait_ge(x_hi_ready, i + 1)
                    for j in range(2):
                        at = (slice(None), slice(4 * j, 4 * j + 4), slice(i * P, (i + 1) * P))
                        last = nc.vector.tensor_tensor(x_lo[at], xt_ps[2 * (i % 2) + j][:], x_hi[at].bitcast(F32), ALU.subtract)
                    last.then_inc(x_lo_ready, 1)


def attend(nc, a, scratch, x_hi, x_lo, ident):
    STEPS_G = 2 * B
    STEPS = HKV * STEPS_G
    with ExitStack() as ctx:
        def sb(name, shape, dt=F32):
            return ctx.enter_context(nc.sbuf_tensor(name, shape, dt))

        def ps(name, shape):
            return ctx.enter_context(nc.psum_tensor(name, shape, F32))

        def sem(name):
            return ctx.enter_context(nc.semaphore(name))

        w_raw = sb("w_raw", [P, 2, KT, P])
        w_hi = sb("w_hi", [P, 2, KT, P], F32R)
        w_lo = sb("w_lo", [P, 2, KT, P], F32R)
        key_raw = sb("key_raw", [P, 2, B, P])
        key_hi = sb("key_hi", [P, 2, B, P], F32R)
        key_lo = sb("key_lo", [P, 2, B, P], F32R)
        cos_q = sb("cos_q", [P, S])
        sin_q = sb("sin_q", [P, S])
        mask = sb("mask", [P, B, TT, SK])
        rot = sb("rot", [P, 4, S])
        q_hi = sb("q_hi", [P, 2, S], F32R)
        q_lo = sb("q_lo", [P, 2, S], F32R)
        scores_t = sb("scores_t", [P, S])
        shifted = sb("shifted", [P, TT, 2, SK])
        exps = sb("exps", [P, TT, 2, SK])
        probs = sb("probs", [P, TT, 2, SK])
        row_max = sb("row_max", [P, TT, 2])
        row_sum = sb("row_sum", [P, TT, 2])
        row_inv = sb("row_inv", [P, TT, 2])
        pt_hi = sb("pt_hi", [P, 2, S], F32R)
        pt_lo = sb("pt_lo", [P, 2, S], F32R)
        q_ps = [ps(f"q_ps{i}", [P, S]) for i in range(4)]
        st_ps = ps("st_ps", [P, S])
        s_ps = ps("s_ps", [P, TT, 2, SK])
        pt_ps = ps("pt_ps", [P, S])

        consts_in = sem("att_consts_in")
        w_in = [sem(f"w_in{c}") for c in range(2)]
        w_hi_ready = sem("w_hi_ready")
        w_lo_ready = sem("w_lo_ready")
        key_zeroed = sem("key_zeroed")
        key_in = sem("key_in")
        key_hi_ready = sem("key_hi_ready")
        key_lo_ready = sem("key_lo_ready")
        q_done = sem("q_done")
        prod_ready = sem("prod_ready")
        rot_ready = sem("rot_ready")
        q_hi_ready = sem("q_hi_ready")
        q_lo_ready = sem("q_lo_ready")
        st_done = sem("st_done")
        st_copied = sem("st_copied")
        s_done = sem("s_done")
        masked_ready = sem("masked_ready")
        max_ready = sem("max_ready")
        shifted_ready = sem("shifted_ready")
        exps_ready = sem("exps_ready")
        sum_ready = sem("sum_ready")
        inv_ready = sem("inv_ready")
        probs_ready = sem("probs_ready")
        pt_done = sem("pt_done")
        pt_hi_ready = sem("pt_hi_ready")
        pt_lo_ready = sem("pt_lo_ready")
        pt_stored = [sem(f"pt_stored{i}") for i in range(2)]

        block = ctx.enter_context(nc.Block())

        def over_key_heads(eng, slot, peel_last):
            for j in range(STEPS_G):
                slot(0, j, False)
            end = HKV - 1 if peel_last else HKV
            with eng.Fori(1, end) as g:
                for j in range(STEPS_G):
                    slot(g, j, False)
            if peel_last:
                for j in range(STEPS_G):
                    slot(HKV - 1, j, True)
            for j in range(STEPS_G, STEPS_G + 3):
                slot(HKV - 1, j, True)

        def has(g, j, lag):
            if isinstance(g, int):
                return 0 <= g * STEPS_G + j - lag < STEPS
            return True

        @block.sync
        def _(sp):
            def load_w(hp, c, uses):
                wait(sp, w_lo_ready, 2 * (uses - 1) + c + 1)
                sp.dma_start(w_raw[:, c], a["wq"][bass.ds(hp, 1), c].rearrange("o p k n -> p (o k) n")).then_inc(w_in[c], 16)

            def load_keys(g):
                wait(sp, key_lo_ready, g)
                for c in range(2):
                    for h in range(2):
                        src = scratch["keys"][c].rearrange("(g f) t -> g f t", f=HALF)[bass.ds(g, 1)]
                        sp.dma_start(key_raw[h * HALF:(h + 1) * HALF, c, :, h * SK:(h + 1) * SK],
                                     src.rearrange("o f (b s) -> (o f) b s", b=B)).then_inc(key_in, 16)

            def slot(g, j, last):
                if j == 2 and not last:
                    load_keys(g + 1)
                if j % B == 1 and not (last and j >= B):
                    hp = 2 * g + j // B + 1
                    load_w(hp, 0, hp)
                    load_w(hp, 1, hp)
                if has(g, j, 3):
                    i = (j - 3) % 2
                    hp, b = 2 * g + (j - 3) // B, (j - 3) % B
                    wait(sp, pt_hi_ready, STEPS_G * g + j - 2)
                    wait(sp, pt_lo_ready, STEPS_G * g + j - 2)
                    for n, part in enumerate((pt_hi, pt_lo)):
                        dst = scratch["probs"][n][bass.ds(hp, 1), :, b * S:(b + 1) * S].rearrange("o p t -> (o p) t")
                        sp.dma_start(dst, part[:, i].bitcast(F32)).then_inc(pt_stored[i], 16)

            load_w(0, 0, 0)
            sp.dma_start(cos_q[:], a["cos_q"]).then_inc(consts_in, 16)
            sp.dma_start(sin_q[:], a["sin_q"]).then_inc(consts_in, 16)
            load_w(0, 1, 0)
            sp.dma_start(mask[:], a["mask"]).then_inc(consts_in, 16)
            sp.wait_ge(key_zeroed, 1)
            load_keys(0)
            over_key_heads(sp, slot, True)
            for i in range(2):
                sp.wait_ge(pt_stored[i], 32 * STEPS // 2)

        @block.tensor
        def _(pe):
            def queries(g, j, c, ks):
                b = j % B
                u = STEPS_G * g + j
                hp = 2 * g + j // B
                if b == 0 and ks[0] == 0:
                    pe.wait_ge(w_hi_ready, 2 * hp + c + 1)
                    pe.wait_ge(w_lo_ready, 2 * hp + c + 1)
                if c == 0 and ks[0] == 0:
                    wait(pe, prod_ready, 2 * u - 2)
                for k in ks:
                    at = (slice(None), k, slice(b * S, (b + 1) * S))
                    last = three(pe, q_ps[2 * (j % 2) + c][:], w_hi[:, c, k, :], w_lo[:, c, k, :], x_hi[at], x_lo[at],
                                 k == 0, k == KT - 1)
                if ks[-1] == KT - 1:
                    last.then_inc(q_done, 1)

            def slot(g, j, last_g):
                u = STEPS_G * g + j
                if has(g, j, 0):
                    queries(g, j, 0, range(KT))
                    queries(g, j, 1, range(KT // 2))
                if has(g, j, 1):
                    b = (j - 1) % B
                    if j == 1:
                        pe.wait_ge(key_hi_ready, g + 1)
                        pe.wait_ge(key_lo_ready, g + 1)
                    wait(pe, st_copied, u - 1)
                    for c in range(2):
                        pe.wait_ge(q_hi_ready, 2 * u - 1 + c)
                        pe.wait_ge(q_lo_ready, 2 * u - 1 + c)
                        last = three(pe, st_ps[:], key_hi[:, c, b, :], key_lo[:, c, b, :], q_hi[:, c, :], q_lo[:, c, :],
                                     c == 0, c == 1)
                    last.then_inc(st_done, 1)
                if has(g, j, 0):
                    queries(g, j, 1, range(KT // 2, KT))
                if has(g, j, 2):
                    pe.wait_ge(probs_ready, u - 1)
                    wait(pe, pt_hi_ready, u - 2)
                    wait(pe, pt_lo_ready, u - 2)
                    for i in range(TT):
                        last = pe.transpose(pt_ps[:, i * P:(i + 1) * P], probs[:, i].rearrange("p h s -> p (h s)"), ident[:])
                    last.then_inc(pt_done, 1)
                if has(g, j, 1):
                    pe.wait_ge(st_copied, u)
                    wait(pe, masked_ready, u - 1)
                    for i in range(TT):
                        last = pe.transpose(s_ps[:, i].rearrange("p h s -> p (h s)"), scores_t[:, i * P:(i + 1) * P], ident[:])
                    last.then_inc(s_done, 1)

            over_key_heads(pe, slot, False)

        @block.scalar
        def _(act):
            def split_w(hp, c):
                act.wait_ge(w_in[c], 16 * (hp + 1))
                wait(act, q_done, 2 * B * hp - 1 + c)
                nc.scalar.copy(w_hi[:, c], w_raw[:, c]).then_inc(w_hi_ready, 1)

            def slot(g, j, last):
                u = STEPS_G * g + j
                hp = 2 * g + j // B
                if has(g, j, 3):
                    i = (j - 3) % 2
                    act.wait_ge(pt_done, u - 2)
                    wait(act, pt_stored[i], 32 * (4 * g + (j - 3) // 2))
                    nc.scalar.copy(pt_hi[:, i], pt_ps[:]).then_inc(pt_hi_ready, 1)
                if j % B == 0 and has(g, j, 0) and not (isinstance(g, int) and g == 0 and j == 0):
                    split_w(hp, 1)
                if j == 1:
                    act.wait_ge(key_in, 64 * (g + 1))
                    wait(act, st_done, u - 1)
                    nc.scalar.copy(key_hi[:], key_raw[:]).then_inc(key_hi_ready, 1)
                if has(g, j, 1):
                    for c in range(2):
                        act.wait_ge(rot_ready, 2 * u - 1 + c)
                        wait(act, st_done, u - 1)
                        nc.scalar.copy(q_hi[:, c], rot[:, 2 * c]).then_inc(q_hi_ready, 1)
                if has(g, j, 2):
                    act.wait_ge(shifted_ready, u - 1)
                    wait(act, probs_ready, u - 2)
                    nc.scalar.activation(exps[:], shifted[:], ACT.Exp).then_inc(exps_ready, 1)
                if j % B == B - 1 and not (last and j >= B):
                    split_w(hp + 1, 0)
                if has(g, j, 1):
                    act.wait_ge(st_done, u)
                    wait(act, s_done, u - 1)
                    nc.scalar.copy(scores_t[:], st_ps[:]).then_inc(st_copied, 1)

            split_w(0, 0)
            split_w(0, 1)
            over_key_heads(act, slot, True)

        @block.gpsimd
        def _(pool):
            def split_w(hp, c):
                pool.wait_ge(w_hi_ready, 2 * hp + c + 1)
                nc.gpsimd.tensor_tensor(w_lo[:, c], w_raw[:, c], w_hi[:, c].bitcast(F32), ALU.subtract).then_inc(w_lo_ready, 1)

            def slot(g, j, last):
                u = STEPS_G * g + j
                hp = 2 * g + j // B
                if j % B == 0 and has(g, j, 0) and not (isinstance(g, int) and g == 0 and j == 0):
                    split_w(hp, 1)
                if j == 1:
                    pool.wait_ge(key_hi_ready, g + 1)
                    nc.gpsimd.tensor_tensor(key_lo[:], key_raw[:], key_hi[:].bitcast(F32), ALU.subtract).then_inc(key_lo_ready, 1)
                if has(g, j, 1):
                    for c in range(2):
                        pool.wait_ge(q_hi_ready, 2 * u - 1 + c)
                        nc.gpsimd.tensor_tensor(q_lo[:, c], rot[:, 2 * c], q_hi[:, c].bitcast(F32),
                                                ALU.subtract).then_inc(q_lo_ready, 1)
                if has(g, j, 2):
                    pool.wait_ge(inv_ready, u - 1)
                    wait(pool, pt_done, u - 2)
                    nc.gpsimd.tensor_tensor(probs[:], exps[:], row_inv[:].unsqueeze(3).to_broadcast([P, TT, 2, SK]),
                                            ALU.mult).then_inc(probs_ready, 1)
                if j % B == B - 1 and not (last and j >= B):
                    split_w(hp + 1, 0)

            split_w(0, 0)
            split_w(0, 1)
            over_key_heads(pool, slot, True)

        @block.vector
        def _(dve):
            def slot(g, j, last):
                u = STEPS_G * g + j
                if has(g, j, 1):
                    q1, q2 = q_ps[2 * ((j - 1) % 2)][:], q_ps[2 * ((j - 1) % 2) + 1][:]
                    dve.wait_ge(q_done, 2 * u)
                    wait(dve, q_lo_ready, 2 * u - 2)
                    nc.vector.tensor_tensor(rot[:, 0], q1, cos_q[:], ALU.mult)
                    nc.vector.tensor_tensor(rot[:, 1], q2, sin_q[:], ALU.mult).then_inc(prod_ready, 1)
                    nc.vector.tensor_tensor(rot[:, 2], q2, cos_q[:], ALU.mult)
                    dve.wait_ge(prod_ready, 2 * u - 1)
                    nc.vector.tensor_tensor(rot[:, 0], rot[:, 0], rot[:, 1], ALU.subtract).then_inc(rot_ready, 1)
                    nc.vector.tensor_tensor(rot[:, 3], q1, sin_q[:], ALU.mult).then_inc(prod_ready, 1)
                    dve.wait_ge(prod_ready, 2 * u)
                    nc.vector.tensor_tensor(rot[:, 2], rot[:, 2], rot[:, 3], ALU.add).then_inc(rot_ready, 1)
                if has(g, j, 2):
                    b = (j - 2) % B
                    dve.wait_ge(s_done, u - 1)
                    wait(dve, exps_ready, u - 2)
                    nc.vector.tensor_tensor(shifted[:], s_ps[:], mask[:, b].unsqueeze(2).to_broadcast([P, TT, 2, SK]),
                                            ALU.add).then_inc(masked_ready, 1)
                    dve.wait_ge(masked_ready, u - 1)
                    nc.vector.tensor_reduce(row_max[:], shifted[:], AX.X, ALU.max).then_inc(max_ready, 1)
                    dve.wait_ge(max_ready, u - 1)
                    nc.vector.tensor_tensor(shifted[:], shifted[:], row_max[:].unsqueeze(3).to_broadcast([P, TT, 2, SK]),
                                            ALU.subtract).then_inc(shifted_ready, 1)
                if has(g, j, 3):
                    i = (j - 3) % 2
                    dve.wait_ge(pt_hi_ready, u - 2)
                    nc.vector.tensor_tensor(pt_lo[:, i], pt_ps[:], pt_hi[:, i].bitcast(F32), ALU.subtract).then_inc(pt_lo_ready, 1)
                if has(g, j, 2):
                    dve.wait_ge(exps_ready, u - 1)
                    wait(dve, probs_ready, u - 2)
                    nc.vector.tensor_reduce(row_sum[:], exps[:], AX.X, ALU.add).then_inc(sum_ready, 1)
                    dve.wait_ge(sum_ready, u - 1)
                    nc.vector.reciprocal(row_inv[:], row_sum[:]).then_inc(inv_ready, 1)

            nc.vector.memset(key_raw[:], 0.0).then_inc(key_zeroed, 1)
            dve.wait_ge(consts_in, 48)
            over_key_heads(dve, slot, False)


def project(nc, a, scratch, wo_raw, attn_stored, ahead):
    with ExitStack() as ctx:
        def sb(name, shape, dt=F32):
            return ctx.enter_context(nc.sbuf_tensor(name, shape, dt))

        def ps(name, shape):
            return ctx.enter_context(nc.psum_tensor(name, shape, F32))

        def sem(name):
            return ctx.enter_context(nc.semaphore(name))

        NBUF = WO_BUFS
        VW_AHEAD, WO_AHEAD = 2, 5
        NACC = QW // P * PB
        PAIRS = B // PB
        p_hi = sb("p_hi", [P, HP, PB * S], F32R)
        p_lo = sb("p_lo", [P, HP, PB * S], F32R)
        vt_hi = sb("vt_hi", [P, HKV, CTX], F32R)
        vt_lo = sb("vt_lo", [P, HKV, CTX], F32R)
        wo_hi = sb("wo_hi", [P, NBUF, 2, QW], F32R)
        wo_lo = sb("wo_lo", [P, NBUF, 2, QW], F32R)
        vw_hi = sb("vw_hi", [P, NBUF, PB, QW], F32R)
        vw_lo = sb("vw_lo", [P, NBUF, PB, QW], F32R)
        attn_sb = sb("attn_sb", [P, QW // P, PB, S])
        gate = sb("gate_x", [P, 1])
        tanh_gate = sb("tanh_gate_x", [P, 1])
        vw_ps = [ps(f"vw_ps{i}", [P, 2, QW]) for i in range(NBUF)]
        acc_ps = [ps(f"acc_ps{i}", [P, S]) for i in range(NACC)]

        gate_in = sem("gate_x_in")
        gate_ready = sem("gate_x_ready")
        vt_in = sem("vt_in")
        p_in = [sem(f"p_in{h}") for h in range(HP)]
        wo_in = [sem(f"wo_in{i}") for i in range(NBUF)]
        wo_hi_ready = sem("wo_hi_ready")
        wo_lo_ready = sem("wo_lo_ready")
        vw_done = sem("vw_done")
        vw_hi_ready = sem("vw_hi_ready")
        vw_lo_ready = sem("vw_lo_ready")
        av_done = sem("av_done")
        acc_done = sem("acc_done")
        acc_read = sem("acc_read")

        block = ctx.enter_context(nc.Block())

        def over_quarters(eng, quarter):
            quarter(0, 0, (0, 1))
            with eng.Fori(1, NQ - 1) as q:
                quarter(0, q, (0, q + 1))
            quarter(0, NQ - 1, (1, 0))
            with eng.Fori(0, NQ - 1) as q:
                quarter(1, q, (1, q + 1))
            quarter(1, NQ - 1, None)

        def place(pair, q, hp):
            return (pair * NQ + q) * HP + hp

        @block.sync
        def _(sp):
            def load_probs(pair, hp):
                wait(sp, av_done, place(pair - 1, NQ - 1, hp) + 1)
                for n, part in enumerate((p_hi, p_lo)):
                    src = scratch["probs"][n, hp, :, pair * PB * S:(pair + 1) * PB * S]
                    sp.dma_start(part[:, hp].bitcast(F32), src).then_inc(p_in[hp], 16)

            def quarter(pair, q, before=(), after=()):
                for hp in range(HP):
                    if hp in before:
                        load_probs(pair, hp)
                    wait(sp, wo_lo_ready, place(pair, q, hp) - NBUF + 1)
                    sp.dma_start(wo_raw[:, hp % NBUF], a["wo"][bass.ds(q, 1), hp].rearrange("o p h n -> p (o h) n")
                                 ).then_inc(wo_in[hp % NBUF], 16)
                    for later in after:
                        if later[0] == hp:
                            load_probs(*later[1:])

            sp.dma_start(vt_hi[:].bitcast(F32), scratch["values"][0].rearrange("g p t -> p g t")).then_inc(vt_in, 16)
            sp.dma_start(vt_lo[:].bitcast(F32), scratch["values"][1].rearrange("g p t -> p g t")).then_inc(vt_in, 16)
            sp.dma_start(gate[:], a["g_xattn"]).then_inc(gate_in, 16)
            LAG = 6
            quarter(0, 0, before=range(HP))
            with sp.Fori(1, NQ - 1) as q:
                quarter(0, q)
            quarter(0, NQ - 1, after=[(hp + LAG, 1, hp) for hp in range(HP - LAG)])
            quarter(1, 0, after=[(hp - HP + LAG, 1, hp) for hp in range(HP - LAG, HP)])
            with sp.Fori(1, NQ) as q:
                quarter(1, q)
            sp.wait_ge(attn_stored, 16 * NQ)
            sp.dma_start(ahead["attn"][:], attn_block(scratch, 0)).then_inc(ahead["attn_in"], 16)
            for name in ("g_ffn", "row_is_hi", "gate_t"):
                sp.dma_start(ahead[name][:], a[name]).then_inc(ahead["small_in"], 16)
            sp.wait_ge(wo_lo_ready, PAIRS * NQ * HP)
            sp.dma_start(ahead["x"], x_block(a, 0)).then_inc(ahead["x_in"], 16)

        @block.tensor
        def _(pe):
            def values_wo(pair, q, hp):
                n, i, g = place(pair, q, hp), hp % NBUF, hp // 2
                pe.wait_ge(wo_hi_ready, n + 1)
                pe.wait_ge(wo_lo_ready, n + 1)
                wait(pe, vw_lo_ready, n - NBUF + 1)
                cols = slice(pair * PB * SK, (pair + 1) * PB * SK)
                for h in range(2):
                    last = three(pe, vw_ps[i][:, h, :], vt_hi[:, g, cols], vt_lo[:, g, cols],
                                 wo_hi[:, i, h, :], wo_lo[:, i, h, :], True, True)
                last.then_inc(vw_done, 1)

            def probs_times(pair, q, hp):
                n, i = place(pair, q, hp), hp % NBUF
                pe.wait_ge(vw_hi_ready, n + 1)
                pe.wait_ge(vw_lo_ready, n + 1)
                pe.wait_ge(p_in[hp], 32 * (pair + 1))
                for bank in range(NACC):
                    d, b = bank // PB, bank % PB
                    if hp == 0:
                        wait(pe, acc_read, NACC * (pair * NQ + q - 1) + bank + 1)
                    last = three(pe, acc_ps[bank][:], vw_hi[:, i, b, d * P:(d + 1) * P], vw_lo[:, i, b, d * P:(d + 1) * P],
                                 p_hi[:, hp, b * S:(b + 1) * S], p_lo[:, hp, b * S:(b + 1) * S], hp == 0, hp == HP - 1)
                    if hp == HP - 1 and bank < NACC - 1:
                        last.then_inc(acc_done, 1)
                last.then_inc(av_done, 1)

            def quarter(pair, q, following):
                for hp in range(HP):
                    if hp + VW_AHEAD < HP:
                        values_wo(pair, q, hp + VW_AHEAD)
                    elif following is not None:
                        values_wo(*following, hp + VW_AHEAD - HP)
                    probs_times(pair, q, hp)

            pe.wait_ge(vt_in, 32)
            for hp in range(VW_AHEAD):
                values_wo(0, 0, hp)
            over_quarters(pe, quarter)

        @block.scalar
        def _(act):
            def split_wo(pair, q, hp):
                n, i = place(pair, q, hp), hp % NBUF
                act.wait_ge(wo_in[i], 16 * ((pair * NQ + q) * (HP // NBUF) + hp // NBUF + 1))
                wait(act, vw_done, n - NBUF + 1)
                nc.scalar.copy(wo_hi[:, i], wo_raw[:, i]).then_inc(wo_hi_ready, 1)

            def split_vw(pair, q, hp):
                n, i = place(pair, q, hp), hp % NBUF
                act.wait_ge(vw_done, n + 1)
                wait(act, av_done, n - NBUF + 1)
                for b in range(PB):
                    for h in range(2):
                        done = nc.scalar.copy(vw_hi[h * SK:(h + 1) * SK, i, b, :], vw_ps[i][b * SK:(b + 1) * SK, h, :])
                done.then_inc(vw_hi_ready, 1)

            def quarter(pair, q, following):
                for hp in range(HP):
                    for ahead, split in ((VW_AHEAD, split_vw), (WO_AHEAD, split_wo)):
                        if hp + ahead < HP:
                            split(pair, q, hp + ahead)
                        elif following is not None:
                            split(*following, hp + ahead - HP)
                wait(act, attn_stored, 16 * (pair * NQ + q))
                for bank in range(NACC):
                    if bank < NACC - 1:
                        act.wait_ge(acc_done, (NACC - 1) * (pair * NQ + q) + bank + 1)
                    else:
                        act.wait_ge(av_done, HP * (pair * NQ + q + 1))
                    nc.scalar.activation(attn_sb[:, bank // PB, bank % PB, :], acc_ps[bank][:], ACT.Copy,
                                         scale=tanh_gate[:, 0:1]).then_inc(acc_read, 1)
                act.wait_ge(acc_read, NACC * (pair * NQ + q + 1))
                dst = scratch["attn"].rearrange("(q d p) t -> q p d t", p=P, d=QW // P)[bass.ds(q, 1), :, :, pair * PB * S:(pair + 1) * PB * S]
                act.dma_start(dst.rearrange("o p d t -> p (o d) t"), attn_sb[:].rearrange("p d b t -> p d (b t)")).then_inc(attn_stored, 16)

            act.wait_ge(gate_in, 16)
            nc.scalar.activation(tanh_gate[:], gate[:], ACT.Tanh).then_inc(gate_ready, 1)
            act.wait_ge(gate_ready, 1)
            for hp in range(NBUF):
                split_wo(0, 0, hp)
            for hp in range(VW_AHEAD):
                split_vw(0, 0, hp)
            for hp in range(NBUF, WO_AHEAD):
                split_wo(0, 0, hp)
            over_quarters(act, quarter)

        @block.gpsimd
        def _(pool):
            for pair in range(PAIRS):
                with pool.Fori(0, NQ) as q:
                    for hp in range(HP):
                        i = hp % NBUF
                        pool.wait_ge(wo_hi_ready, place(pair, q, hp) + 1)
                        nc.gpsimd.tensor_tensor(wo_lo[:, i], wo_raw[:, i], wo_hi[:, i].bitcast(F32),
                                                ALU.subtract).then_inc(wo_lo_ready, 1)

        @block.vector
        def _(dve):
            for pair in range(PAIRS):
                with dve.Fori(0, NQ) as q:
                    for hp in range(HP):
                        i = hp % NBUF
                        dve.wait_ge(vw_hi_ready, place(pair, q, hp) + 1)
                        for b in range(PB):
                            for h in range(2):
                                at = (slice(h * SK, (h + 1) * SK), i, b)
                                done = nc.vector.tensor_tensor(vw_lo[at], vw_ps[i][b * SK:(b + 1) * SK, h, :],
                                                               vw_hi[at].bitcast(F32), ALU.subtract)
                        done.then_inc(vw_lo_ready, 1)


def attn_block(scratch, i):
    return scratch["attn"].rearrange("(k p) (i t) -> i p k t", p=P, t=BT)[bass.ds(i, 1)].rearrange("o p k t -> p (o k) t")


def x_block(a, i):
    return a["x"].rearrange("(i n p) d -> i p n d", p=P, n=BT // P)[bass.ds(i, 1)].rearrange("o p n d -> p (o n) d")


def feed(nc, a, scratch, ident, out, attn_stored, ahead):
    NT = BT // P
    NC = NT * 2
    HW = D // 2
    NW = 4
    STEPS = NC * KT
    WBUF = 3
    with ExitStack() as ctx:
        def sb(name, shape, dt=F32):
            return ctx.enter_context(nc.sbuf_tensor(name, shape, dt))

        def ps(name, shape):
            return ctx.enter_context(nc.psum_tensor(name, shape, F32))

        def sem(name):
            return ctx.enter_context(nc.semaphore(name))

        attn_in_sb, x_in_sb, gate, row_is_hi, gate_w = (ahead[name] for name in ("attn", "x", "g_ffn", "row_is_hi", "gate_t"))
        attn_in, x_in, small_in = ahead["attn_in"], ahead["x_in"], ahead["small_in"]
        w_raw = sb("ffn_w_raw", [P, WBUF, D])
        w_sign = sb("w_sign", [P, KT, D], F32R)
        bias = sb("bias", [P, D])
        scale_raw = sb("scale_raw", [R, 2, D])
        tanh_gate = sb("tanh_gate_f", [P, 1])
        scale_hi = sb("scale_hi", [R, 2, D], F32R)
        scale_lo = sb("scale_lo", [R, 2, D])
        scale_stack = sb("scale_stack", [P, 2, D], F32R)
        zeros = sb("zeros", [P, 1])
        x1 = sb("x1", [P, 2, NT, D])
        x1b = sb("x1b", [P, 2, NT, D])
        x1n = sb("x1n", [P, NT, D])
        x1n_t = sb("x1n_t", [P, KT, BT])
        xs = sb("xs", [P, KT, BT])
        xs_hi = sb("xs_hi", [P, 2, KT, BT], F32R)
        xs_lo = sb("xs_lo", [P, 2, KT, BT], F32R)
        out_scale = sb("out_scale_sb", [P, 2, HW])
        y_part = sb("y_part", [P, 2, HW])
        y = sb("y", [P, NC, HW])
        stats = sb("ffn_stats", [P, NT, 2, 6])
        mean_var = sb("ffn_mean_var", [P, NT, 2])
        var_eps = sb("ffn_var_eps", [P, NT])
        rstd = sb("ffn_rstd", [P, NT])
        shift = sb("ffn_shift", [P, NT])
        minus_half = sb("ffn_minus_half", [P, NT])
        minus_one = sb("ffn_minus_one", [P, NT])
        logits_t = sb("logits_t", [E, BT])
        r_max = sb("r_max", [P, NT])
        r_exp = sb("r_exp", [P, NT, E])
        r_sum = sb("r_sum", [P, NT])
        r_inv = sb("r_inv", [P, NT])
        routing = sb("routing", [P, NT, E])
        r_stack = sb("r_stack", [P, NT, 4, E], F32R)
        r_stack_t = sb("r_stack_t", [P, 2, BT], F32R)
        wk = [ps(f"wk{i}", [P, 512]) for i in range(NW)]
        f_ps = [ps(f"f_ps{i}", [P, HW]) for i in range(2)]
        o_ps = ps("o_ps", [P, HW])
        r_ps = ps("r_ps", [P, 512])

        scales_in = sem("scales_in")
        bias_in = sem("bias_in")
        w_in = [sem(f"ffn_w_in{i}") for i in range(WBUF)]
        sign_ready = sem("sign_ready")
        gate_ready = sem("gate_f_ready")
        zeros_ready = sem("zeros_ready")
        rows_zeroed = sem("rows_zeroed")
        scales_gated = sem("scales_gated")
        scale_hi_ready = sem("scale_hi_ready")
        scale_lo_ready = sem("scale_lo_ready")
        stack_ready = sem("stack_ready")
        bias_ready = sem("bias_ready")
        half_ready = sem("ffn_half_ready")
        ta_done = sem("ta_done")
        x1_ready = sem("x1_ready")
        stats_ready = sem("ffn_stats_ready")
        mean_ready = sem("ffn_mean_ready")
        var_ready = sem("ffn_var_ready")
        rstd_ready = sem("ffn_rstd_ready")
        mean_scaled = sem("ffn_mean_scaled")
        shift_ready = sem("ffn_shift_ready")
        x1n_ready = sem("x1n_ready")
        x1b_ready = sem("x1b_ready")
        tb_done = sem("tb_done")
        x1n_t_ready = sem("x1n_t_ready")
        logits_done = sem("logits_done")
        logits_copied = sem("logits_copied")
        lt_done = sem("lt_done")
        r_max_ready = sem("r_max_ready")
        r_shift_ready = sem("r_shift_ready")
        r_exp_ready = sem("r_exp_ready")
        r_sum_ready = sem("r_sum_ready")
        r_inv_ready = sem("r_inv_ready")
        routing_ready = sem("routing_ready")
        r_hi_ready = sem("r_hi_ready")
        r_stack_ready = sem("r_stack_ready")
        rt_done = sem("rt_done")
        r_stack_t_ready = sem("r_stack_t_ready")
        is_done = sem("is_done")
        xs_ready = sem("xs_ready")
        xs_hi_ready = sem("xs_hi_ready")
        xs_lo_ready = sem("xs_lo_ready")
        os_done = sem("os_done")
        os_copied = sem("os_copied")
        f_done = sem("f_done")
        y_part_ready = sem("y_part_ready")
        y_ready = sem("y_ready")
        y_stored = [sem(f"y_stored{i}") for i in range(NC)]

        block = ctx.enter_context(nc.Block())

        def has(i, lag):
            return 0 <= i - lag < NB if isinstance(i, int) else True

        @block.sync
        def _(sp):
            def load(i):
                wait(sp, ta_done, i)
                sp.dma_start(attn_in_sb[:], attn_block(scratch, i)).then_inc(attn_in, 16)
                wait(sp, x1_ready, i)
                sp.dma_start(x_in_sb, x_block(a, i)).then_inc(x_in, 16)

            def slot(i, j):
                if has(i, -2):
                    load(i + 2)
                if has(i, 1):
                    for c in range(NC):
                        sp.wait_ge(y_ready, NC * (i - 1) + c + 1)
                        dst = out.rearrange("(i n p) (h w) -> i n h p w", p=P, n=NT, h=2)[bass.ds(i - 1, 1), c // 2, c % 2]
                        sp.dma_start(dst.rearrange("o p w -> (o p) w"), y[:, c]).then_inc(y_stored[c], 16)

            def load_weights(ks):
                for k in ks:
                    wait(sp, sign_ready, k - WBUF + 1)
                    sp.dma_start(w_raw[:, k % WBUF], a["weight_t"][k * P:(k + 1) * P, :]).then_inc(w_in[k % WBUF], 16)

            load_weights(range(WBUF))
            slot(-1, 1)
            load_weights(range(WBUF, KT))
            sp.wait_ge(attn_stored, 16 * B // PB * NQ)
            slot(0, 0)
            slot(1, 1)
            with sp.Fori(1, NB // 2 - 1) as g:
                slot(2 * g, 0)
                slot(2 * g + 1, 1)
            for i in range(NB - 2, NB + 1):
                slot(i, i % 2)
            for c in range(NC):
                sp.wait_ge(y_stored[c], 16 * NB)

        @block.tensor
        def _(pe):
            def products(i, j, steps):
                for step in steps:
                    c, k = step // KT, step % KT
                    t, h = c // 2, c % 2
                    if k == 0:
                        wait(pe, os_copied, NC * i + c)
                        pe.matmul(o_ps[:], r_stack_t[:, j, t * P:(t + 1) * P], scale_stack[:, 1, h * HW:(h + 1) * HW],
                                  start=True, stop=True).then_inc(os_done, 1)
                        wait(pe, y_part_ready, NC * i + c - 1)
                    if c == 0 and k % 2 == 0:
                        pe.wait_ge(xs_lo_ready, NW * i + k // 2 + 1)
                    for n, part in enumerate((xs_hi, xs_lo)):
                        last = pe.matmul(f_ps[c % 2][:], part[:, j, k, t * P:(t + 1) * P], w_sign[:, k, h * HW:(h + 1) * HW],
                                         start=(k == 0 and n == 0), stop=(k == KT - 1 and n == 1))
                    if k == KT - 1:
                        last.then_inc(f_done, 1)

            def turn_attention(i):
                pe.wait_ge(attn_in, 16 * (i + 1))
                wait(pe, x1n_t_ready, i)
                for t in range(NT):
                    for k in range(KT):
                        last = pe.transpose(wk[2 * t + k // 4][:, k % 4 * P:(k % 4 + 1) * P],
                                            attn_in_sb[:, k, t * P:(t + 1) * P], ident[:])
                last.then_inc(ta_done, 1)

            def turn_normalised(i):
                pe.wait_ge(x1n_ready, i + 1)
                wait(pe, xs_ready, NW * i)
                for t in range(NT):
                    for k in range(KT):
                        last = pe.transpose(wk[k // 2][:, k % 2 * BT + t * P:k % 2 * BT + (t + 1) * P],
                                            x1n[:, t, k * P:(k + 1) * P], ident[:])
                last.then_inc(tb_done, 1)

            def router_logits(i):
                pe.wait_ge(x1n_t_ready, i + 1)
                wait(pe, r_stack_t_ready, i)
                for k in range(KT):
                    last = pe.matmul(r_ps[0:E, 0:BT], gate_w[:, k, :], x1n_t[:, k, :], start=k == 0, stop=k == KT - 1)
                last.then_inc(logits_done, 1)

            def turn_logits():
                for t in range(NT):
                    last = pe.transpose(r_ps[:, BT + t * E:BT + (t + 1) * E], logits_t[:, t * P:(t + 1) * P], ident[0:E, 0:E])
                last.then_inc(lt_done, 1)

            def turn_routing(i):
                pe.wait_ge(r_stack_ready, i + 1)
                for t in range(NT):
                    last = pe.transpose(r_ps[0:R, t * P:(t + 1) * P], r_stack[:, t].rearrange("p n e -> p (n e)").bitcast(F32), ident[:])
                last.then_inc(rt_done, 1)

            def in_scales(i, j):
                pe.wait_ge(r_stack_t_ready, i + 1)
                if isinstance(i, int) and i == 0:
                    pe.wait_ge(stack_ready, 1)
                wait(pe, x1_ready, i + 2 if has(i, -1) else i + 1)
                for k in range(KT):
                    last = pe.matmul(wk[k // 2][:, k % 2 * BT:(k % 2 + 1) * BT], scale_stack[:, 0, k * P:(k + 1) * P],
                                     r_stack_t[:, j, :], start=True, stop=True)
                last.then_inc(is_done, 1)

            def slot(i, j):
                def some_products(first, count):
                    if has(i, 1):
                        products(i - 1, 1 - j, range(first, first + count))

                if has(i, 0):
                    turn_normalised(i)
                if isinstance(i, int) and i == 1:
                    pe.wait_ge(sign_ready, KT)
                some_products(0, 6)
                if has(i, -1):
                    turn_attention(i + 1)
                if has(i, 0):
                    router_logits(i)
                some_products(6, 2)
                if has(i, 0):
                    pe.wait_ge(logits_copied, i + 1)
                some_products(8, 1)
                if has(i, 0):
                    turn_logits()
                some_products(9, 6)
                if has(i, 0):
                    turn_routing(i)
                some_products(15, 1)
                if has(i, 0):
                    in_scales(i, j)
                some_products(16, STEPS - 16)

            slot(-1, 1)
            pe.wait_ge(small_in, 48)
            slot(0, 0)
            slot(1, 1)
            with pe.Fori(1, NB // 2 - 1) as g:
                slot(2 * g, 0)
                slot(2 * g + 1, 1)
            for i in range(NB - 2, NB + 1):
                slot(i, i % 2)

        @block.scalar
        def _(act):
            def copy_out_scales(i, c):
                act.wait_ge(os_done, NC * i + c + 1)
                wait(act, y_part_ready, NC * i + c - 1)
                nc.scalar.copy(out_scale[:, c % 2], o_ps[:]).then_inc(os_copied, 1)

            def normalise(i, j):
                act.wait_ge(shift_ready, i + 1)
                wait(act, tb_done, i)
                for t in range(NT):
                    done = nc.scalar.activation(x1n[:, t], x1[:, j, t], ACT.Identity, bias=shift[:, t:t + 1], scale=rstd[:, t:t + 1])
                done.then_inc(x1n_ready, 1)

            def high(i, j, m):
                act.wait_ge(xs_ready, NW * i + m + 1)
                nc.scalar.copy(xs_hi[:, j, 2 * m:2 * m + 2, :], xs[:, 2 * m:2 * m + 2, :]).then_inc(xs_hi_ready, 1)

            FIRST_SIGNS = 3

            def sign(k):
                act.wait_ge(w_in[k % WBUF], 16 * (k // WBUF + 1))
                nc.scalar.activation(w_sign[:, k, :], w_raw[:, k % WBUF], ACT.Sign).then_inc(sign_ready, 1)

            def slot(i, j):
                if has(i, 0):
                    act.wait_ge(tb_done, i + 1)
                    for m in range(NW):
                        done = nc.scalar.copy(x1n_t[:, 2 * m:2 * m + 2, :], wk[m][:].rearrange("p (k t) -> p k t", k=2))
                    done.then_inc(x1n_t_ready, 1)
                if isinstance(i, int) and i == 0:
                    for k in range(FIRST_SIGNS, KT):
                        sign(k)
                if has(i, 1):
                    copy_out_scales(i - 1, 0)
                if has(i, 0):
                    act.wait_ge(logits_done, i + 1)
                    wait(act, lt_done, i)
                    nc.scalar.copy(logits_t[:], r_ps[0:E, 0:BT]).then_inc(logits_copied, 1)
                    act.wait_ge(r_shift_ready, i + 1)
                    nc.scalar.activation(r_exp[:], routing[:], ACT.Exp).then_inc(r_exp_ready, 1)
                if has(i, 1):
                    copy_out_scales(i - 1, 1)
                if has(i, 0):
                    act.wait_ge(rt_done, i + 1)
                    wait(act, os_done, NC * (i - 1))
                    nc.scalar.copy(r_stack_t[0:R, j, :], r_ps[0:R, 0:BT]).then_inc(r_stack_t_ready, 1)
                    wait(act, f_done, NC * (i - 1))
                    high(i, j, 0)
                    high(i, j, 1)
                if has(i, 1):
                    copy_out_scales(i - 1, 2)
                if has(i, 0):
                    high(i, j, 2)
                    high(i, j, 3)
                if has(i, -1):
                    normalise(i + 1, 1 - j)
                if has(i, 1):
                    copy_out_scales(i - 1, 3)

            act.dma_start(scale_raw[:], a["scales"]).then_inc(scales_in, 16)
            act.wait_ge(small_in, 48)
            nc.scalar.activation(tanh_gate[:], gate[:], ACT.Tanh).then_inc(gate_ready, 1)
            act.dma_start(bias[:], a["bias"]).then_inc(bias_in, 16)
            for k in range(FIRST_SIGNS):
                sign(k)
            for i in range(-1, 2):
                slot(i, i % 2)
            with act.Fori(1, NB // 2 - 1) as g:
                slot(2 * g, 0)
                slot(2 * g + 1, 1)
            for i in range(NB - 2, NB + 1):
                slot(i, i % 2)

        @block.gpsimd
        def _(pool):
            def add(i, j, c):
                t, h = c // 2, c % 2
                pool.wait_ge(y_part_ready, NC * i + c + 1)
                pool.wait_ge(x1b_ready, i + 1)
                wait(pool, y_stored[c], 16 * i)
                nc.gpsimd.tensor_tensor(y[:, c], y_part[:, c % 2], x1b[:, j, t, h * HW:(h + 1) * HW], ALU.add).then_inc(y_ready, 1)

            def slot(i, j):
                if has(i, 0):
                    wait(pool, y_ready, NC * (i - 1))
                    pool.wait_ge(x1_ready, i + 1)
                    nc.gpsimd.tensor_tensor(x1b[:, j], x1[:, j], bias[:].unsqueeze(1).to_broadcast([P, NT, D]), ALU.add).then_inc(x1b_ready, 1)
                if has(i, 1):
                    add(i - 1, 1 - j, 0)
                if has(i, -1):
                    pool.wait_ge(var_ready, i + 2)
                    wait(pool, x1n_ready, i + 1)
                    nc.gpsimd.tensor_tensor(rstd[:], var_eps[:], minus_half[:], ALU.pow).then_inc(rstd_ready, 1)
                    pool.wait_ge(rstd_ready, i + 2)
                    nc.gpsimd.tensor_tensor(shift[:], mean_var[:, :, 0], rstd[:], ALU.mult).then_inc(mean_scaled, 1)
                    pool.wait_ge(mean_scaled, i + 2)
                    nc.gpsimd.tensor_tensor(shift[:], shift[:], minus_one[:], ALU.mult).then_inc(shift_ready, 1)
                if has(i, 1):
                    for c in range(1, NC):
                        add(i - 1, 1 - j, c)

            nc.gpsimd.memset(minus_one[:], -1.0)
            nc.gpsimd.memset(minus_half[:], -0.5).then_inc(half_ready, 1)
            pool.wait_ge(half_ready, 1)
            slot(-1, 1)
            pool.wait_ge(bias_ready, 1)
            slot(0, 0)
            slot(1, 1)
            with pool.Fori(1, NB // 2 - 1) as g:
                slot(2 * g, 0)
                slot(2 * g + 1, 1)
            for i in range(NB - 2, NB + 1):
                slot(i, i % 2)

        @block.vector
        def _(dve):
            def scaled(i, c):
                dve.wait_ge(f_done, NC * i + c + 1)
                dve.wait_ge(os_copied, NC * i + c + 1)
                wait(dve, y_ready, NC * i + c - 1)
                nc.vector.tensor_tensor(y_part[:, c % 2], f_ps[c % 2][:], out_scale[:, c % 2], ALU.mult).then_inc(y_part_ready, 1)

            def residual(i, j):
                dve.wait_ge(ta_done, i + 1)
                dve.wait_ge(x_in, 16 * (i + 1))
                wait(dve, x1n_ready, i - 1)
                wait(dve, x1b_ready, i - 1)
                for t in range(NT):
                    for h in range(2):
                        at = (slice(None), t, slice(h * HW, (h + 1) * HW))
                        done = nc.vector.tensor_tensor(x1[:, j][at], wk[2 * t + h][:], x_in_sb[at], ALU.add)
                done.then_inc(x1_ready, 1)
                dve.wait_ge(x1_ready, i + 1)
                for t in range(NT):
                    for h in range(2):
                        done = nc.vector.bn_stats(stats[:, t, h, :], x1[:, j, t, h * HW:(h + 1) * HW])
                done.then_inc(stats_ready, 1)

            def slot(i, j):
                if has(i, -1):
                    residual(i + 1, 1 - j)
                    dve.wait_ge(stats_ready, i + 2)
                    wait(dve, shift_ready, i + 1)
                if has(i, 1):
                    scaled(i - 1, 0)
                if has(i, -1):
                    for t in range(NT):
                        done = nc.vector.bn_aggr(mean_var[:, t, :], stats[:, t])
                    done.then_inc(mean_ready, 1)
                    dve.wait_ge(mean_ready, i + 2)
                    nc.vector.tensor_scalar(var_eps[:], mean_var[:, :, 1], EPS, None, ALU.add).then_inc(var_ready, 1)
                if has(i, 0):
                    logits = r_ps[:, BT:BT + NT * E].rearrange("p (t e) -> p t e", e=E)
                    dve.wait_ge(lt_done, i + 1)
                    nc.vector.tensor_reduce(r_max[:], logits, AX.X, ALU.max).then_inc(r_max_ready, 1)
                    dve.wait_ge(r_max_ready, i + 1)
                    nc.vector.tensor_tensor(routing[:], logits, r_max[:].unsqueeze(2).to_broadcast([P, NT, E]),
                                            ALU.subtract).then_inc(r_shift_ready, 1)
                    dve.wait_ge(r_exp_ready, i + 1)
                    nc.vector.tensor_reduce(r_sum[:], r_exp[:], AX.X, ALU.add).then_inc(r_sum_ready, 1)
                    dve.wait_ge(r_sum_ready, i + 1)
                    nc.vector.reciprocal(r_inv[:], r_sum[:]).then_inc(r_inv_ready, 1)
                    dve.wait_ge(r_inv_ready, i + 1)
                    nc.vector.tensor_tensor(routing[:], r_exp[:], r_inv[:].unsqueeze(2).to_broadcast([P, NT, E]),
                                            ALU.mult).then_inc(routing_ready, 1)
                    dve.wait_ge(routing_ready, i + 1)
                    wait(dve, rt_done, i)
                    nc.vector.tensor_copy(r_stack[:, :, 0:2, :], routing[:].unsqueeze(2).to_broadcast([P, NT, 2, E])).then_inc(r_hi_ready, 1)
                    dve.wait_ge(r_hi_ready, i + 1)
                    for n in range(2):
                        done = nc.vector.tensor_tensor(r_stack[:, :, 2 + n, :], routing[:], r_stack[:, :, 0, :].bitcast(F32), ALU.subtract)
                    done.then_inc(r_stack_ready, 1)
                if has(i, 1):
                    scaled(i - 1, 1)
                if has(i, 0):
                    def low(m):
                        dve.wait_ge(xs_hi_ready, NW * i + m + 1)
                        at = (slice(None), slice(2 * m, 2 * m + 2))
                        nc.vector.tensor_tensor(xs_lo[:, j][at], xs[at], xs_hi[:, j][at].bitcast(F32), ALU.subtract).then_inc(xs_lo_ready, 1)

                    dve.wait_ge(is_done, i + 1)
                    wait(dve, xs_lo_ready, NW * i)
                    for m in range(NW):
                        at = (slice(None), slice(2 * m, 2 * m + 2))
                        nc.vector.tensor_tensor(xs[at], wk[m][:].rearrange("p (k t) -> p k t", k=2), x1n_t[at], ALU.mult).then_inc(xs_ready, 1)
                        if m >= 1:
                            low(m - 1)
                    low(NW - 1)
                if has(i, 1):
                    scaled(i - 1, 2)
                    scaled(i - 1, 3)

            def zero():
                nc.vector.memset(zeros[:], 0.0).then_inc(zeros_ready, 1)
                dve.wait_ge(zeros_ready, 1)
                for n in range(2):
                    nc.vector.tensor_copy(scale_stack[:, n], zeros[:, 0:1].to_broadcast([P, D]))
                    done = nc.vector.tensor_copy(r_stack_t[:, n], zeros[:, 0:1].to_broadcast([P, BT]))
                done.then_inc(rows_zeroed, 1)

            def stack_scales():
                dve.wait_ge(scales_in, 16)
                dve.wait_ge(small_in, 48)
                dve.wait_ge(gate_ready, 1)
                nc.vector.tensor_scalar(scale_raw[:, 1], scale_raw[:, 1], tanh_gate[0:R, 0:1], None, ALU.mult).then_inc(scales_gated, 1)
                dve.wait_ge(scales_gated, 1)
                nc.vector.tensor_copy(scale_hi[:], scale_raw[:]).then_inc(scale_hi_ready, 1)
                dve.wait_ge(scale_hi_ready, 1)
                nc.vector.tensor_tensor(scale_lo[:], scale_raw[:], scale_hi[:].bitcast(F32), ALU.subtract).then_inc(scale_lo_ready, 1)
                dve.wait_ge(scale_lo_ready, 1)
                nc.vector.tensor_scalar(scale_lo[:], scale_lo[:], row_is_hi[:, 1:2], None, ALU.mult).then_inc(scale_lo_ready, 1)
                dve.wait_ge(scale_lo_ready, 2)
                dve.wait_ge(rows_zeroed, 1)
                nc.vector.scalar_tensor_tensor(out=scale_stack[0:R], in0=scale_hi[:].bitcast(F32), scalar=row_is_hi[:, 0:1], in1=scale_lo[:],
                                               op0=ALU.mult, op1=ALU.add).then_inc(stack_ready, 1)
                dve.wait_ge(bias_in, 16)
                nc.vector.tensor_scalar(bias[:], bias[:], tanh_gate[:, 0:1], None, ALU.mult).then_inc(bias_ready, 1)

            zero()
            slot(-1, 1)
            stack_scales()
            slot(0, 0)
            slot(1, 1)
            with dve.Fori(1, NB // 2 - 1) as g:
                slot(2 * g, 0)
                slot(2 * g + 1, 1)
            for i in range(NB - 2, NB + 1):
                slot(i, i % 2)



_OUT = ((B, S, D), "float32")


def build(nc, a, out):
    scratch = {
        "keys": nc.dram_tensor("keys_scratch", (2, HKV * HALF, CTX), F32, kind="Internal").ap(),
        "values": nc.dram_tensor("values_scratch", (2, HKV, P, CTX), F32, kind="Internal").ap(),
        "probs": nc.dram_tensor("probs_scratch", (2, HP, P, T), F32, kind="Internal").ap(),
        "attn": nc.dram_tensor("attn_scratch", (D, T), F32, kind="Internal").ap(),
    }
    with ExitStack() as ctx:
        ident = ctx.enter_context(nc.sbuf_tensor("ident", [P, P], F32))
        with nc.sbuf_tensor("x_hi", [P, KT, T], F32R) as x_hi, nc.sbuf_tensor("x_lo", [P, KT, T], F32R) as x_lo:
            prepare(nc, a, scratch, x_hi, x_lo, ident)
            attend(nc, a, scratch, x_hi, x_lo, ident)
        wo_raw = ctx.enter_context(nc.sbuf_tensor("wo_raw", [P, WO_BUFS, 2, QW], F32))
        ahead = {name: ctx.enter_context(nc.sbuf_tensor(f"ahead_{name}", shape, F32)) for name, shape in (
            ("attn", [P, KT, BT]), ("g_ffn", [P, 1]), ("row_is_hi", [R, 2]), ("gate_t", [P, KT, E]))}
        ahead["x"] = wo_raw[:].rearrange("p i h n -> p (i h n)").rearrange("p (n d) -> p n d", d=D)
        for name in ("attn_in", "x_in", "small_in"):
            ahead[name] = ctx.enter_context(nc.semaphore(name))
        attn_stored = ctx.enter_context(nc.semaphore("attn_stored"))
        project(nc, a, scratch, wo_raw, attn_stored, ahead)
        feed(nc, a, scratch, ident, out, attn_stored, ahead)


def constants():
    inv_freq = (np.float32(1.0) / np.float32(10000.0) ** (np.arange(0, DK, 2, dtype=np.float32) / np.float32(DK)))
    angle = np.arange(S, dtype=np.float32)[:, None] * inv_freq.astype(np.float32)[None, :]
    cos = np.concatenate([np.cos(angle).T] * 2, 0).astype(np.float32)
    sin = np.concatenate([np.sin(angle).T] * 2, 0).astype(np.float32)
    scale = np.float32(1.0) / np.sqrt(np.float32(DK))
    row = np.arange(4 * E)
    is_hi = np.stack([row // E % 2 == 0, row // E % 2 == 1], 1).astype(np.float32)
    return {
        "row_is_hi": is_hi,
        "ident": np.eye(P, dtype=np.float32), "cos_q": cos, "sin_q": sin,
        "cos_k": np.tile(cos[:, :SK] * scale, (1, B)), "sin_k": np.tile(sin[:, :SK] * scale, (1, B)),
    }


def laid_out(x, ctx_4096, mask_BxSxS2_ff0, g_xattn, g_ffn, L0_xattn_wq, L0_xattn_wk, L0_xattn_wv, L0_xattn_wo,
             L0_ffn_weight, L0_ffn_bias, L0_ffn_gate_w, L0_ffn_in_channel_scale, L0_ffn_out_channel_scale):
    n = np.asarray
    wk = n(L0_xattn_wk).reshape(KT, P, GP, 2, 2, HALF).transpose(2, 4, 1, 0, 3, 5).reshape(HKV, P, KT, P)
    wv = n(L0_xattn_wv).reshape(KT, P, HKV, P).transpose(2, 1, 0, 3)
    return {
        "x": n(x).reshape(T, D),
        "ctx_t": n(ctx_4096).reshape(CTX, D).T,
        "mask": n(mask_BxSxS2_ff0).reshape(B, TT, P, SK).transpose(2, 0, 1, 3),
        "g_xattn": np.broadcast_to(n(g_xattn), (P, 1)), "g_ffn": np.broadcast_to(n(g_ffn), (P, 1)),
        "wq": n(L0_xattn_wq).reshape(KT, P, HP, 2, 2, HALF).transpose(2, 4, 1, 0, 3, 5).reshape(HP, 2, P, KT, P),
        "wkv": np.concatenate([wk, wv], 0),
        "wo": n(L0_xattn_wo).reshape(HP, 2, P, NQ, QW).transpose(3, 0, 2, 1, 4),
        "weight_t": n(L0_ffn_weight).T,
        "bias": np.broadcast_to(n(L0_ffn_bias), (P, D)),
        "gate_t": n(L0_ffn_gate_w).T.reshape(KT, P, E).transpose(1, 0, 2),
        "scales": np.stack([np.tile(n(s), (4, 1)) for s in (L0_ffn_in_channel_scale, L0_ffn_out_channel_scale)], 1),
    }


def kernel(**inputs):
    import concourse.bacc as bacc
    from concourse.bass_utils import run_bass_kernel_spmd

    nc = bacc.Bacc("TRN2", target_bir_lowering=False, num_devices=1)
    arrays, aps = {}, {}
    for name, value in (laid_out(**inputs) | constants()).items():
        value = np.ascontiguousarray(value)
        arrays[f"in_{name}"] = value
        aps[name] = nc.dram_tensor(f"in_{name}", value.shape, mybir.dt.from_np(value.dtype), kind="ExternalInput").ap()
    out = nc.dram_tensor("out_y", (T, D), F32, kind="ExternalOutput").ap()
    build(nc, aps, out)
    r = run_bass_kernel_spmd(nc, [arrays], core_ids=[0])
    return r.results[0]["out_y"].reshape(_OUT[0])
```

```python
from contextlib import ExitStack

import concourse.bass as bass
import numpy as np
from concourse import mybir

ALU = mybir.AluOpType
ACT = mybir.ActivationFunctionType
AX = mybir.AxisListType
F32 = mybir.dt.float32
F32R = mybir.dt.float32r

P = 128
B, S, D = 4, 512, 1024
SK = 64
HQ, HKV, DK = 32, 8, 128
E = 8
EPS = 1e-5
T = B * S
KT = D // P
HP = HQ // 2
HALF = DK // 2
TT = S // P
CTX = B * SK
GP = HKV // 2
NLN = T // P
PB = 2
NQ = 4
QW = D // NQ
BT = 256
NB = T // BT
WO_BUFS = 4
EARLY_P = 4
R = 4 * E


def wait(eng, semaphore, count):
    if isinstance(count, int) and count <= 0:
        return
    eng.wait_ge(semaphore, count)


def three(pe, out, hi, lo, rhs_hi, rhs_lo, first, last, **kw):
    pe.matmul(out, hi, rhs_hi, start=first, stop=False, **kw)
    pe.matmul(out, hi, rhs_lo, start=False, stop=False, **kw)
    return pe.matmul(out, lo, rhs_hi, start=False, stop=last, **kw)


def prepare(nc, a, scratch, x_hi, x_lo, w_raw, w_hi, w_lo, ident):
    NU = 2 * HKV
    UNITS = NU + 2
    KH = KT // 2
    XB = 3
    with ExitStack() as ctx:
        def sb(name, shape, dt=F32):
            return ctx.enter_context(nc.sbuf_tensor(name, shape, dt))

        def sem(name):
            return ctx.enter_context(nc.semaphore(name))

        ctx_raw = sb("ctx_raw", [P, KT, CTX])
        ctx_hi = sb("ctx_hi", [P, KT, CTX], F32R)
        ctx_lo = sb("ctx_lo", [P, KT, CTX], F32R)
        spare_raw = ctx_raw[:].rearrange("p k t -> p (k t)").rearrange("p (i k n) -> p i k n", i=2, n=P)
        x_in = sb("x_in", [P, XB, D])
        xn = sb("xn", [P, 2, D])
        k_rot = sb("k_rot", [P, 4, CTX])
        v_hi = sb("v_hi", [P, 2, CTX], F32R)
        v_lo = sb("v_lo", [P, 2, CTX], F32R)
        cos_k = sb("cos_k", [P, CTX])
        sin_k = sb("sin_k", [P, CTX])
        stats = sb("stats", [P, 2, 2, 6])
        mean_var = sb("mean_var", [P, 2, 2])
        var_eps = sb("var_eps", [P, 2])
        rstd = sb("rstd", [P, 2])
        mean_rstd = sb("mean_rstd", [P, 2])
        shift = sb("shift", [P, 2])
        minus_half = sb("minus_half", [P, 1])
        minus_one = sb("minus_one", [P, 1])
        kv_ps = [ctx.enter_context(nc.psum_tensor(f"kv_ps{i}", [P, 512], F32)) for i in range(4)]
        xt_ps = [ctx.enter_context(nc.psum_tensor(f"xt_ps{i}", [P, 4, P], F32)) for i in range(4)]

        ident_in = sem("ident_in")
        tables_in = sem("tables_in")
        ctx_in = [sem(f"ctx_in{h}") for h in range(2)]
        ctx_hi_ready = sem("ctx_hi_ready")
        ctx_lo_ready = sem("ctx_lo_ready")
        w_in = [sem(f"kw_in{i}") for i in range(4)]
        w_hi_ready = sem("kw_hi_ready")
        w_lo_ready = sem("kw_lo_ready")
        kv_done = sem("kv_done")
        k_read = sem("k_read")
        k_roped = sem("k_roped")
        k_stored = sem("k_stored")
        v_hi_ready = sem("v_hi_ready")
        v_lo_ready = sem("v_lo_ready")
        v_stored = [sem(f"v_stored{i}") for i in range(2)]
        x_in_sem = [sem(f"x_in_sem{i}") for i in range(XB)]
        constants_ready = sem("constants_ready")
        stats_ready = sem("stats_ready")
        mean_ready = sem("mean_ready")
        var_ready = sem("var_ready")
        rstd_ready = sem("rstd_ready")
        mean_rstd_ready = sem("mean_rstd_ready")
        shift_ready = sem("shift_ready")
        xn_ready = sem("xn_ready")
        xt_ready = sem("xt_ready")
        x_hi_ready = sem("x_hi_ready")
        x_lo_ready = sem("x_lo_ready")

        block = ctx.enter_context(nc.Block())

        def raw(n):
            return w_raw[:, n % 2] if n % 4 < 2 else spare_raw[:, n % 2]

        def half(h):
            return slice(h * KH, (h + 1) * KH)

        @block.sync
        def _(sp):
            def load_unit(n):
                if n >= 4:
                    sp.wait_ge(w_lo_ready, 2 * (n - 3))
                elif n >= 2:
                    sp.wait_ge(ctx_lo_ready, 2)
                sp.dma_start(raw(n), a["wkv"][n] if n < NU else a["wq"][0, n - NU]).then_inc(w_in[n % 4], 16)

            def load_x(i):
                wait(sp, xn_ready, i - XB + 1)
                sp.dma_start(x_in[:, i % XB], a["x"][i * P:(i + 1) * P, :]).then_inc(x_in_sem[i % XB], 16)

            for h in range(2):
                src = a["ctx_t"].rearrange("(k p) t -> p k t", p=P)[:, half(h)]
                sp.dma_start(ctx_raw[:, half(h)], src).then_inc(ctx_in[h], 16)
                if h == 0:
                    load_unit(0)
                    load_x(0)
            load_unit(1)
            load_x(1)
            load_x(2)
            for n in range(2, UNITS):
                load_unit(n)
                if n + 1 < NLN:
                    load_x(n + 1)

        @block.tensor
        def _(pe):
            for n in range(NU + 1):
                if n < NU:
                    if n >= 4 + HKV:
                        pe.wait_ge(v_lo_ready, n - 4 - HKV + 1)
                    elif n >= 4:
                        pe.wait_ge(k_read, (n - 4) // 2 + 1)
                    for h in range(2):
                        if n == 0:
                            pe.wait_ge(ctx_hi_ready, h + 1)
                            pe.wait_ge(ctx_lo_ready, h + 1)
                        pe.wait_ge(w_hi_ready, 2 * n + h + 1)
                        pe.wait_ge(w_lo_ready, 2 * n + h + 1)
                        for k in range(h * KH, (h + 1) * KH):
                            last = three(pe, kv_ps[n % 4][:, 0:CTX], w_hi[:, n % 2, k, :], w_lo[:, n % 2, k, :],
                                         ctx_hi[:, k, :], ctx_lo[:, k, :], k == 0, k == KT - 1)
                        last.then_inc(kv_done, 1)
                if n >= 1:
                    i = n - 1
                    if i == 0:
                        pe.wait_ge(ident_in, 16)
                    pe.wait_ge(xn_ready, i + 1)
                    wait(pe, x_lo_ready, i - 1)
                    for k in range(KT):
                        last = pe.transpose(xt_ps[2 * (i % 2) + k // 4][:, k % 4, :],
                                            xn[:, i % 2, k * P:(k + 1) * P], ident[:])
                    last.then_inc(xt_ready, 1)

        @block.scalar
        def _(act):
            def split_unit(n):
                act.wait_ge(w_in[n % 4], 16 * (n // 4 + 1))
                for h in range(2):
                    wait(act, kv_done, 2 * (n - 2) + h + 1)
                    nc.scalar.copy(w_hi[:, n % 2, half(h)], raw(n)[:, half(h)]).then_inc(w_hi_ready, 1)

            def normalise(i):
                act.wait_ge(shift_ready, i + 1)
                wait(act, xt_ready, i - 1)
                nc.scalar.activation(xn[:, i % 2], x_in[:, i % XB], ACT.Identity, bias=shift[:, i % 2:i % 2 + 1],
                                     scale=rstd[:, i % 2:i % 2 + 1]).then_inc(xn_ready, 1)

            def value_high(g):
                act.wait_ge(kv_done, 2 * (g + HKV) + 2)
                wait(act, v_stored[g % 2], 32 * (g // 2))
                nc.scalar.copy(v_hi[:, g % 2], kv_ps[g % 4][:, 0:CTX]).then_inc(v_hi_ready, 1)

            def turned(i):
                act.wait_ge(xt_ready, i + 1)
                for j in range(2):
                    last = nc.scalar.copy(x_hi[:, 4 * j:4 * j + 4, i * P:(i + 1) * P], xt_ps[2 * (i % 2) + j][:])
                last.then_inc(x_hi_ready, 1)

            def store_keys(gp):
                act.wait_ge(k_roped, gp + 1)
                for c in range(2):
                    act.dma_start(scratch["keys"][c, gp * P:(gp + 1) * P, :], k_rot[:, 2 * c, :]).then_inc(k_stored, 16)

            def store_values(g):
                act.wait_ge(v_lo_ready, g + 1)
                for c, part in enumerate((v_hi, v_lo)):
                    act.dma_start(scratch["values"][c, g], part[:, g % 2].bitcast(F32)).then_inc(v_stored[g % 2], 16)

            act.dma_start(ident[:], a["ident"]).then_inc(ident_in, 16)
            act.dma_start(cos_k[:], a["cos_k"]).then_inc(tables_in, 16)
            act.dma_start(sin_k[:], a["sin_k"]).then_inc(tables_in, 16)
            for h in range(2):
                act.wait_ge(ctx_in[h], 16)
                nc.scalar.copy(ctx_hi[:, half(h)], ctx_raw[:, half(h)]).then_inc(ctx_hi_ready, 1)
            for n in range(NU + 2):
                split_unit(n)
                if n < NLN:
                    normalise(n)
                if HKV <= n - 1 < NU:
                    value_high(n - 1 - HKV)
                if n >= 2:
                    turned(n - 2)
                if 0 <= n - 2 < HKV and (n - 2) % 2 == 1:
                    store_keys((n - 2) // 2)
                if n - 2 >= HKV:
                    store_values(n - 2 - HKV)
            act.wait_ge(k_stored, 32 * GP)
            for i in range(2):
                act.wait_ge(v_stored[i], 32 * HKV // 2)

        @block.gpsimd
        def _(pool):
            def reciprocal_deviation(i):
                at = (slice(None), slice(i % 2, i % 2 + 1))
                pool.wait_ge(var_ready, i + 1)
                wait(pool, xn_ready, i - 1)
                nc.gpsimd.tensor_tensor(rstd[at], var_eps[at], minus_half[:], ALU.pow).then_inc(rstd_ready, 1)
                pool.wait_ge(rstd_ready, i + 1)
                nc.gpsimd.tensor_tensor(mean_rstd[at], mean_var[:, i % 2, 0:1], rstd[at], ALU.mult).then_inc(mean_rstd_ready, 1)
                pool.wait_ge(mean_rstd_ready, i + 1)
                nc.gpsimd.tensor_tensor(shift[at], mean_rstd[at], minus_one[:], ALU.mult).then_inc(shift_ready, 1)

            nc.gpsimd.memset(minus_half[:], -0.5)
            nc.gpsimd.memset(minus_one[:], -1.0).then_inc(constants_ready, 1)
            pool.wait_ge(constants_ready, 1)
            reciprocal_deviation(0)
            for n in range(UNITS):
                for h in range(2):
                    pool.wait_ge(w_hi_ready, 2 * n + h + 1)
                    nc.gpsimd.tensor_tensor(w_lo[:, n % 2, half(h)], raw(n)[:, half(h)], w_hi[:, n % 2, half(h)].bitcast(F32),
                                            ALU.subtract).then_inc(w_lo_ready, 1)
                if n + 1 < NLN:
                    reciprocal_deviation(n + 1)

        @block.vector
        def _(dve):
            def statistics(i):
                dve.wait_ge(x_in_sem[i % XB], 16 * (i // XB + 1))
                for j in range(2):
                    last = nc.vector.bn_stats(stats[:, i % 2, j, :], x_in[:, i % XB, j * 512:(j + 1) * 512])
                last.then_inc(stats_ready, 1)
                dve.wait_ge(stats_ready, i + 1)
                wait(dve, shift_ready, i - 1)
                nc.vector.bn_aggr(mean_var[:, i % 2, :], stats[:, i % 2]).then_inc(mean_ready, 1)
                dve.wait_ge(mean_ready, i + 1)
                nc.vector.tensor_scalar(var_eps[:, i % 2:i % 2 + 1], mean_var[:, i % 2, 1:2], EPS, None,
                                        ALU.add).then_inc(var_ready, 1)

            def rotate(gp):
                k1, k2 = kv_ps[(2 * gp) % 4][:, 0:CTX], kv_ps[(2 * gp + 1) % 4][:, 0:CTX]
                dve.wait_ge(kv_done, 2 * (2 * gp + 2))
                wait(dve, k_stored, 32 * gp)
                nc.vector.tensor_tensor(k_rot[:, 0], k1, cos_k[:], ALU.mult)
                nc.vector.tensor_tensor(k_rot[:, 1], k2, sin_k[:], ALU.mult)
                nc.vector.tensor_tensor(k_rot[:, 2], k2, cos_k[:], ALU.mult)
                nc.vector.tensor_tensor(k_rot[:, 3], k1, sin_k[:], ALU.mult).then_inc(k_read, 1)
                dve.wait_ge(k_read, gp + 1)
                nc.vector.tensor_tensor(k_rot[:, 0], k_rot[:, 0], k_rot[:, 1], ALU.subtract)
                nc.vector.tensor_tensor(k_rot[:, 2], k_rot[:, 2], k_rot[:, 3], ALU.add).then_inc(k_roped, 1)

            def value_low(g):
                dve.wait_ge(v_hi_ready, g + 1)
                wait(dve, v_stored[g % 2], 32 * (g // 2))
                nc.vector.tensor_tensor(v_lo[:, g % 2], kv_ps[g % 4][:, 0:CTX], v_hi[:, g % 2].bitcast(F32),
                                        ALU.subtract).then_inc(v_lo_ready, 1)

            def turned_low(i):
                dve.wait_ge(x_hi_ready, i + 1)
                for j in range(2):
                    at = (slice(None), slice(4 * j, 4 * j + 4), slice(i * P, (i + 1) * P))
                    last = nc.vector.tensor_tensor(x_lo[at], xt_ps[2 * (i % 2) + j][:], x_hi[at].bitcast(F32), ALU.subtract)
                last.then_inc(x_lo_ready, 1)

            statistics(0)
            for h in range(2):
                dve.wait_ge(ctx_hi_ready, h + 1)
                nc.vector.tensor_tensor(ctx_lo[:, half(h)], ctx_raw[:, half(h)], ctx_hi[:, half(h)].bitcast(F32),
                                        ALU.subtract).then_inc(ctx_lo_ready, 1)
            dve.wait_ge(tables_in, 32)
            for n in range(NU + 2):
                if n + 1 < NLN:
                    statistics(n + 1)
                if 0 <= n - 1 < HKV and (n - 1) % 2 == 1:
                    rotate((n - 1) // 2)
                if HKV <= n - 1 < NU:
                    value_low(n - 1 - HKV)
                if n >= 2:
                    turned_low(n - 2)


def load_wo(sp, a, wo_raw, wo_in, q, hp):
    return sp.dma_start(wo_raw[:, hp % WO_BUFS], a["wo"][bass.ds(q, 1), hp].rearrange("o p h n -> p (o h) n")
                        ).then_inc(wo_in[hp % WO_BUFS], 16)


def load_probs(sp, scratch, p_hi, p_lo, p_in, pair, hp):
    for n, part in enumerate((p_hi, p_lo)):
        src = scratch["probs"][n, hp, :, pair * PB * S:(pair + 1) * PB * S]
        sp.dma_start(part[:, hp].bitcast(F32), src).then_inc(p_in[hp], 16)


def attend(nc, a, scratch, x_hi, x_lo, w_raw, w_hi, w_lo, ident, following):
    STEPS_G = 2 * B
    STEPS = HKV * STEPS_G
    with ExitStack() as ctx:
        def sb(name, shape, dt=F32):
            return ctx.enter_context(nc.sbuf_tensor(name, shape, dt))

        def ps(name, shape):
            return ctx.enter_context(nc.psum_tensor(name, shape, F32))

        def sem(name):
            return ctx.enter_context(nc.semaphore(name))

        key_raw = sb("key_raw", [P, 2, B, P])
        key_hi = sb("key_hi", [P, 2, B, P], F32R)
        key_lo = sb("key_lo", [P, 2, B, P], F32R)
        cos_q = sb("cos_q", [P, S])
        sin_q = sb("sin_q", [P, S])
        mask = sb("mask", [P, B, TT, SK])
        rot = sb("rot", [P, 4, S])
        q_hi = sb("q_hi", [P, 2, S], F32R)
        q_lo = sb("q_lo", [P, 2, S], F32R)
        scores_t = sb("scores_t", [P, S])
        shifted = sb("shifted", [P, TT, 2, SK])
        exps = sb("exps", [P, TT, 2, SK])
        probs = sb("probs", [P, TT, 2, SK])
        row_max = sb("row_max", [P, TT, 2])
        row_sum = sb("row_sum", [P, TT, 2])
        row_inv = sb("row_inv", [P, TT, 2])
        pt_hi = sb("pt_hi", [P, 2, S], F32R)
        pt_lo = sb("pt_lo", [P, 2, S], F32R)
        q_ps = [ps(f"q_ps{i}", [P, S]) for i in range(4)]
        st_ps = ps("st_ps", [P, S])
        s_ps = ps("s_ps", [P, TT, 2, SK])
        pt_ps = ps("pt_ps", [P, S])

        consts_in = sem("att_consts_in")
        w_in = [sem(f"w_in{c}") for c in range(2)]
        w_hi_ready = sem("w_hi_ready")
        w_lo_ready = sem("w_lo_ready")
        key_zeroed = sem("key_zeroed")
        key_in = sem("key_in")
        key_hi_ready = sem("key_hi_ready")
        key_lo_ready = sem("key_lo_ready")
        q_done = sem("q_done")
        prod_ready = sem("prod_ready")
        rot_ready = sem("rot_ready")
        q_hi_ready = sem("q_hi_ready")
        q_lo_ready = sem("q_lo_ready")
        st_done = sem("st_done")
        st_copied = sem("st_copied")
        s_done = sem("s_done")
        masked_ready = sem("masked_ready")
        max_ready = sem("max_ready")
        shifted_ready = sem("shifted_ready")
        exps_ready = sem("exps_ready")
        sum_ready = sem("sum_ready")
        inv_ready = sem("inv_ready")
        probs_ready = sem("probs_ready")
        pt_done = sem("pt_done")
        pt_hi_ready = sem("pt_hi_ready")
        pt_lo_ready = sem("pt_lo_ready")
        pt_stored = following["pt_stored"]

        block = ctx.enter_context(nc.Block())

        def over_key_heads(eng, slot, peel_last):
            for j in range(STEPS_G):
                slot(0, j, False)
            end = HKV - 1 if peel_last else HKV
            with eng.Fori(1, end) as g:
                for j in range(STEPS_G):
                    slot(g, j, False)
            if peel_last:
                for j in range(STEPS_G):
                    slot(HKV - 1, j, True)
            for j in range(STEPS_G, STEPS_G + 3):
                slot(HKV - 1, j, True)

        def has(g, j, lag):
            if isinstance(g, int):
                return 0 <= g * STEPS_G + j - lag < STEPS
            return True

        @block.sync
        def _(sp):
            def load_w(hp, c):
                wait(sp, w_lo_ready, 2 * (hp - 2) + c + 1)
                sp.dma_start(w_raw[:, c], a["wq"][bass.ds(hp, 1), c].rearrange("o p k n -> p (o k) n")).then_inc(w_in[c], 16)

            def load_keys(g):
                wait(sp, key_lo_ready, g)
                for c in range(2):
                    for h in range(2):
                        src = scratch["keys"][c].rearrange("(g f) t -> g f t", f=HALF)[bass.ds(g, 1)]
                        sp.dma_start(key_raw[h * HALF:(h + 1) * HALF, c, :, h * SK:(h + 1) * SK],
                                     src.rearrange("o f (b s) -> (o f) b s", b=B)).then_inc(key_in, 16)

            def slot(g, j, last):
                if j == 2 and not last:
                    load_keys(g + 1)
                if last and j == STEPS_G - 1:
                    sp.wait_ge(w_lo_ready, 2 * (HP - 1))
                    for hp in range(WO_BUFS):
                        load_wo(sp, a, following["wo_raw"], following["wo_in"], 0, hp)
                if last and j == STEPS_G:
                    sp.wait_ge(q_done, 2 * STEPS)
                    for hp in range(EARLY_P):
                        for parity in range(2):
                            sp.wait_ge(pt_stored[parity], 32 * (2 * hp + 1))
                        load_probs(sp, scratch, following["p_hi"], following["p_lo"], following["p_in"], 0, hp)
                if j % B == 1 and not (last and j >= B):
                    hp = 2 * g + j // B + 1
                    load_w(hp, 0)
                    load_w(hp, 1)
                if has(g, j, 3):
                    i = (j - 3) % 2
                    hp, b = 2 * g + (j - 3) // B, (j - 3) % B
                    wait(sp, pt_hi_ready, STEPS_G * g + j - 2)
                    wait(sp, pt_lo_ready, STEPS_G * g + j - 2)
                    for n, part in enumerate((pt_hi, pt_lo)):
                        dst = scratch["probs"][n][bass.ds(hp, 1), :, b * S:(b + 1) * S].rearrange("o p t -> (o p) t")
                        sp.dma_start(dst, part[:, i].bitcast(F32)).then_inc(pt_stored[i], 16)

            sp.dma_start(cos_q[:], a["cos_q"]).then_inc(consts_in, 16)
            sp.dma_start(sin_q[:], a["sin_q"]).then_inc(consts_in, 16)
            sp.dma_start(mask[:], a["mask"]).then_inc(consts_in, 16)
            sp.wait_ge(key_zeroed, 1)
            load_keys(0)
            over_key_heads(sp, slot, True)

        @block.tensor
        def _(pe):
            def queries(g, j, c, ks):
                b = j % B
                u = STEPS_G * g + j
                hp = 2 * g + j // B
                if b == 0 and ks[0] == 0:
                    wait(pe, w_hi_ready, 2 * (hp - 1) + c + 1)
                    wait(pe, w_lo_ready, 2 * (hp - 1) + c + 1)
                if c == 0 and ks[0] == 0:
                    wait(pe, prod_ready, 2 * u - 2)
                for k in ks:
                    at = (slice(None), k, slice(b * S, (b + 1) * S))
                    last = three(pe, q_ps[2 * (j % 2) + c][:], w_hi[:, c, k, :], w_lo[:, c, k, :], x_hi[at], x_lo[at],
                                 k == 0, k == KT - 1)
                if ks[-1] == KT - 1:
                    last.then_inc(q_done, 1)

            def slot(g, j, last_g):
                u = STEPS_G * g + j
                if has(g, j, 0):
                    queries(g, j, 0, range(KT))
                    queries(g, j, 1, range(KT // 2))
                if has(g, j, 1):
                    b = (j - 1) % B
                    if j == 1:
                        pe.wait_ge(key_hi_ready, g + 1)
                        pe.wait_ge(key_lo_ready, g + 1)
                    wait(pe, st_copied, u - 1)
                    for c in range(2):
                        pe.wait_ge(q_hi_ready, 2 * u - 1 + c)
                        pe.wait_ge(q_lo_ready, 2 * u - 1 + c)
                        last = three(pe, st_ps[:], key_hi[:, c, b, :], key_lo[:, c, b, :], q_hi[:, c, :], q_lo[:, c, :],
                                     c == 0, c == 1)
                    last.then_inc(st_done, 1)
                if has(g, j, 0):
                    queries(g, j, 1, range(KT // 2, KT))
                if has(g, j, 2):
                    pe.wait_ge(probs_ready, u - 1)
                    wait(pe, pt_hi_ready, u - 2)
                    wait(pe, pt_lo_ready, u - 2)
                    for i in range(TT):
                        last = pe.transpose(pt_ps[:, i * P:(i + 1) * P], probs[:, i].rearrange("p h s -> p (h s)"), ident[:])
                    last.then_inc(pt_done, 1)
                if has(g, j, 1):
                    pe.wait_ge(st_copied, u)
                    wait(pe, masked_ready, u - 1)
                    for i in range(TT):
                        last = pe.transpose(s_ps[:, i].rearrange("p h s -> p (h s)"), scores_t[:, i * P:(i + 1) * P], ident[:])
                    last.then_inc(s_done, 1)

            over_key_heads(pe, slot, False)

        @block.scalar
        def _(act):
            def split_w(hp, c):
                act.wait_ge(w_in[c], 16 * hp)
                wait(act, q_done, 2 * B * hp - 1 + c)
                nc.scalar.copy(w_hi[:, c], w_raw[:, c]).then_inc(w_hi_ready, 1)

            def slot(g, j, last):
                u = STEPS_G * g + j
                hp = 2 * g + j // B
                if has(g, j, 3):
                    i = (j - 3) % 2
                    act.wait_ge(pt_done, u - 2)
                    wait(act, pt_stored[i], 32 * (4 * g + (j - 3) // 2))
                    nc.scalar.copy(pt_hi[:, i], pt_ps[:]).then_inc(pt_hi_ready, 1)
                if j % B == 0 and has(g, j, 0) and not (isinstance(g, int) and g == 0 and j == 0):
                    split_w(hp, 1)
                if j == 1:
                    act.wait_ge(key_in, 64 * (g + 1))
                    wait(act, st_done, u - 1)
                    nc.scalar.copy(key_hi[:], key_raw[:]).then_inc(key_hi_ready, 1)
                if has(g, j, 1):
                    for c in range(2):
                        act.wait_ge(rot_ready, 2 * u - 1 + c)
                        wait(act, st_done, u - 1)
                        nc.scalar.copy(q_hi[:, c], rot[:, 2 * c]).then_inc(q_hi_ready, 1)
                if has(g, j, 2):
                    act.wait_ge(shifted_ready, u - 1)
                    wait(act, probs_ready, u - 2)
                    nc.scalar.activation(exps[:], shifted[:], ACT.Exp).then_inc(exps_ready, 1)
                if j % B == B - 1 and not (last and j >= B):
                    split_w(hp + 1, 0)
                if has(g, j, 1):
                    act.wait_ge(st_done, u)
                    wait(act, s_done, u - 1)
                    nc.scalar.copy(scores_t[:], st_ps[:]).then_inc(st_copied, 1)

            over_key_heads(act, slot, True)

        @block.gpsimd
        def _(pool):
            def split_w(hp, c):
                pool.wait_ge(w_hi_ready, 2 * (hp - 1) + c + 1)
                nc.gpsimd.tensor_tensor(w_lo[:, c], w_raw[:, c], w_hi[:, c].bitcast(F32), ALU.subtract).then_inc(w_lo_ready, 1)

            def slot(g, j, last):
                u = STEPS_G * g + j
                hp = 2 * g + j // B
                if j % B == 0 and has(g, j, 0) and not (isinstance(g, int) and g == 0 and j == 0):
                    split_w(hp, 1)
                if j == 1:
                    pool.wait_ge(key_hi_ready, g + 1)
                    nc.gpsimd.tensor_tensor(key_lo[:], key_raw[:], key_hi[:].bitcast(F32), ALU.subtract).then_inc(key_lo_ready, 1)
                if has(g, j, 1):
                    for c in range(2):
                        pool.wait_ge(q_hi_ready, 2 * u - 1 + c)
                        nc.gpsimd.tensor_tensor(q_lo[:, c], rot[:, 2 * c], q_hi[:, c].bitcast(F32),
                                                ALU.subtract).then_inc(q_lo_ready, 1)
                if has(g, j, 2):
                    pool.wait_ge(inv_ready, u - 1)
                    wait(pool, pt_done, u - 2)
                    nc.gpsimd.tensor_tensor(probs[:], exps[:], row_inv[:].unsqueeze(3).to_broadcast([P, TT, 2, SK]),
                                            ALU.mult).then_inc(probs_ready, 1)
                if j % B == B - 1 and not (last and j >= B):
                    split_w(hp + 1, 0)

            over_key_heads(pool, slot, True)

        @block.vector
        def _(dve):
            def slot(g, j, last):
                u = STEPS_G * g + j
                if has(g, j, 1):
                    q1, q2 = q_ps[2 * ((j - 1) % 2)][:], q_ps[2 * ((j - 1) % 2) + 1][:]
                    dve.wait_ge(q_done, 2 * u)
                    wait(dve, q_lo_ready, 2 * u - 2)
                    nc.vector.tensor_tensor(rot[:, 0], q1, cos_q[:], ALU.mult)
                    nc.vector.tensor_tensor(rot[:, 1], q2, sin_q[:], ALU.mult).then_inc(prod_ready, 1)
                    nc.vector.tensor_tensor(rot[:, 2], q2, cos_q[:], ALU.mult)
                    dve.wait_ge(prod_ready, 2 * u - 1)
                    nc.vector.tensor_tensor(rot[:, 0], rot[:, 0], rot[:, 1], ALU.subtract).then_inc(rot_ready, 1)
                    nc.vector.tensor_tensor(rot[:, 3], q1, sin_q[:], ALU.mult).then_inc(prod_ready, 1)
                    dve.wait_ge(prod_ready, 2 * u)
                    nc.vector.tensor_tensor(rot[:, 2], rot[:, 2], rot[:, 3], ALU.add).then_inc(rot_ready, 1)
                if has(g, j, 2):
                    b = (j - 2) % B
                    dve.wait_ge(s_done, u - 1)
                    wait(dve, exps_ready, u - 2)
                    nc.vector.tensor_tensor(shifted[:], s_ps[:], mask[:, b].unsqueeze(2).to_broadcast([P, TT, 2, SK]),
                                            ALU.add).then_inc(masked_ready, 1)
                    dve.wait_ge(masked_ready, u - 1)
                    nc.vector.tensor_reduce(row_max[:], shifted[:], AX.X, ALU.max).then_inc(max_ready, 1)
                    dve.wait_ge(max_ready, u - 1)
                    nc.vector.tensor_tensor(shifted[:], shifted[:], row_max[:].unsqueeze(3).to_broadcast([P, TT, 2, SK]),
                                            ALU.subtract).then_inc(shifted_ready, 1)
                if has(g, j, 3):
                    i = (j - 3) % 2
                    dve.wait_ge(pt_hi_ready, u - 2)
                    nc.vector.tensor_tensor(pt_lo[:, i], pt_ps[:], pt_hi[:, i].bitcast(F32), ALU.subtract).then_inc(pt_lo_ready, 1)
                if has(g, j, 2):
                    dve.wait_ge(exps_ready, u - 1)
                    wait(dve, probs_ready, u - 2)
                    nc.vector.tensor_reduce(row_sum[:], exps[:], AX.X, ALU.add).then_inc(sum_ready, 1)
                    dve.wait_ge(sum_ready, u - 1)
                    nc.vector.reciprocal(row_inv[:], row_sum[:]).then_inc(inv_ready, 1)

            nc.vector.memset(key_raw[:], 0.0).then_inc(key_zeroed, 1)
            dve.wait_ge(consts_in, 48)
            over_key_heads(dve, slot, False)


def project(nc, a, scratch, early, wo_hi, wo_lo, attn_stored, ahead):
    with ExitStack() as ctx:
        def sb(name, shape, dt=F32):
            return ctx.enter_context(nc.sbuf_tensor(name, shape, dt))

        def ps(name, shape):
            return ctx.enter_context(nc.psum_tensor(name, shape, F32))

        def sem(name):
            return ctx.enter_context(nc.semaphore(name))

        NBUF = WO_BUFS
        VW_AHEAD, WO_AHEAD = 2, 5
        NACC = QW // P * PB
        PAIRS = B // PB
        p_hi, p_lo, wo_raw = early["p_hi"], early["p_lo"], early["wo_raw"]
        vt_hi = sb("vt_hi", [P, HKV, CTX], F32R)
        vt_lo = sb("vt_lo", [P, HKV, CTX], F32R)
        vw_hi = sb("vw_hi", [P, NBUF, PB, QW], F32R)
        vw_lo = sb("vw_lo", [P, NBUF, PB, QW], F32R)
        attn_sb = ahead["y"][:].rearrange("p (d b) t -> p d b t", b=PB)
        gate = sb("gate_x", [P, 1])
        tanh_gate = sb("tanh_gate_x", [P, 1])
        vw_ps = [ps(f"vw_ps{i}", [P, 2, QW]) for i in range(NBUF)]
        acc_ps = [ps(f"acc_ps{i}", [P, S]) for i in range(NACC)]

        gate_in = sem("gate_x_in")
        gate_ready = sem("gate_x_ready")
        vt_in = [sem(f"vt_in{g}") for g in range(HKV)]
        p_in, wo_in, pt_stored = early["p_in"], early["wo_in"], early["pt_stored"]
        wo_hi_ready = sem("wo_hi_ready")
        wo_lo_ready = sem("wo_lo_ready")
        vw_done = sem("vw_done")
        vw_hi_ready = sem("vw_hi_ready")
        vw_lo_ready = sem("vw_lo_ready")
        av_done = sem("av_done")
        acc_done = sem("acc_done")
        acc_read = sem("acc_read")

        block = ctx.enter_context(nc.Block())

        def over_quarters(eng, quarter):
            quarter(0, 0, (0, 1))
            with eng.Fori(1, NQ - 1) as q:
                quarter(0, q, (0, q + 1))
            quarter(0, NQ - 1, (1, 0))
            with eng.Fori(0, NQ - 1) as q:
                quarter(1, q, (1, q + 1))
            quarter(1, NQ - 1, None)

        def place(pair, q, hp):
            return (pair * NQ + q) * HP + hp

        @block.sync
        def _(sp):
            def load_values(g):
                for n, part in enumerate((vt_hi, vt_lo)):
                    sp.dma_start(part[:, g].bitcast(F32), scratch["values"][n, g]).then_inc(vt_in[g], 16)

            def replace_probs(hp):
                sp.wait_ge(av_done, place(0, NQ - 1, hp) + 1)
                load_probs(sp, scratch, p_hi, p_lo, p_in, 1, hp)

            def quarter(pair, q, after=()):
                for hp in range(HP):
                    wait(sp, wo_lo_ready, place(pair, q, hp) - NBUF + 1)
                    load_wo(sp, a, wo_raw, wo_in, q, hp)
                    if hp in after:
                        replace_probs(after[hp])

            load_values(0)
            sp.dma_start(gate[:], a["g_xattn"]).then_inc(gate_in, 16)
            for hp in range(HP):
                if hp % 2 == 0 and hp // 2 + 1 < HKV:
                    load_values(hp // 2 + 1)
                if hp == HP - 2:
                    for i in range(2):
                        sp.wait_ge(pt_stored[i], 32 * HP * B // 2)
                if hp >= EARLY_P:
                    load_probs(sp, scratch, p_hi, p_lo, p_in, 0, hp)
                if hp >= NBUF:
                    sp.wait_ge(wo_lo_ready, hp - NBUF + 1)
                    load_wo(sp, a, wo_raw, wo_in, 0, hp)
            LAG = 8
            with sp.Fori(1, NQ - 1) as q:
                quarter(0, q)
            quarter(0, NQ - 1, after={hp + LAG: hp for hp in range(HP - LAG)})
            quarter(1, 0, after={hp - HP + LAG: hp for hp in range(HP - LAG, HP)})
            with sp.Fori(1, NQ) as q:
                quarter(1, q)
            sp.wait_ge(attn_stored, 16 * NQ)
            sp.dma_start(ahead["attn"][:], attn_block(scratch, 0)).then_inc(ahead["attn_in"], 16)
            for name in ("g_ffn", "row_is_hi", "gate_t"):
                sp.dma_start(ahead[name][:], a[name]).then_inc(ahead["small_in"], 16)
            sp.wait_ge(wo_lo_ready, PAIRS * NQ * HP)
            sp.dma_start(ahead["x"], x_block(a, 0)).then_inc(ahead["x_in"], 16)

        @block.tensor
        def _(pe):
            def values_wo(pair, q, hp):
                n, i, g = place(pair, q, hp), hp % NBUF, hp // 2
                if isinstance(n, int) and n < HP and n % 2 == 0:
                    pe.wait_ge(vt_in[g], 32)
                pe.wait_ge(wo_hi_ready, n + 1)
                pe.wait_ge(wo_lo_ready, n + 1)
                wait(pe, vw_lo_ready, n - NBUF + 1)
                cols = slice(pair * PB * SK, (pair + 1) * PB * SK)
                for h in range(2):
                    last = three(pe, vw_ps[i][:, h, :], vt_hi[:, g, cols], vt_lo[:, g, cols],
                                 wo_hi[:, i, h, :], wo_lo[:, i, h, :], True, True)
                last.then_inc(vw_done, 1)

            def probs_times(pair, q, hp):
                n, i = place(pair, q, hp), hp % NBUF
                pe.wait_ge(vw_hi_ready, n + 1)
                pe.wait_ge(vw_lo_ready, n + 1)
                pe.wait_ge(p_in[hp], 32 * (pair + 1))
                for bank in range(NACC):
                    d, b = bank // PB, bank % PB
                    if hp == 0:
                        wait(pe, acc_read, NACC * (pair * NQ + q - 1) + bank + 1)
                    last = three(pe, acc_ps[bank][:], vw_hi[:, i, b, d * P:(d + 1) * P], vw_lo[:, i, b, d * P:(d + 1) * P],
                                 p_hi[:, hp, b * S:(b + 1) * S], p_lo[:, hp, b * S:(b + 1) * S], hp == 0, hp == HP - 1)
                    if hp == HP - 1 and bank < NACC - 1:
                        last.then_inc(acc_done, 1)
                last.then_inc(av_done, 1)

            def quarter(pair, q, following):
                for hp in range(HP):
                    if hp + VW_AHEAD < HP:
                        values_wo(pair, q, hp + VW_AHEAD)
                    elif following is not None:
                        values_wo(*following, hp + VW_AHEAD - HP)
                    probs_times(pair, q, hp)

            for hp in range(VW_AHEAD):
                values_wo(0, 0, hp)
            over_quarters(pe, quarter)

        @block.scalar
        def _(act):
            def split_wo(pair, q, hp):
                n, i = place(pair, q, hp), hp % NBUF
                act.wait_ge(wo_in[i], 16 * ((pair * NQ + q) * (HP // NBUF) + hp // NBUF + 1))
                wait(act, vw_done, n - NBUF + 1)
                nc.scalar.copy(wo_hi[:, i], wo_raw[:, i]).then_inc(wo_hi_ready, 1)

            def split_vw(pair, q, hp):
                n, i = place(pair, q, hp), hp % NBUF
                act.wait_ge(vw_done, n + 1)
                wait(act, av_done, n - NBUF + 1)
                for b in range(PB):
                    for h in range(2):
                        done = nc.scalar.copy(vw_hi[h * SK:(h + 1) * SK, i, b, :], vw_ps[i][b * SK:(b + 1) * SK, h, :])
                done.then_inc(vw_hi_ready, 1)

            def quarter(pair, q, following):
                for hp in range(HP):
                    for ahead, split in ((VW_AHEAD, split_vw), (WO_AHEAD, split_wo)):
                        if hp + ahead < HP:
                            split(pair, q, hp + ahead)
                        elif following is not None:
                            split(*following, hp + ahead - HP)
                wait(act, attn_stored, 16 * (pair * NQ + q))
                for bank in range(NACC):
                    if bank < NACC - 1:
                        act.wait_ge(acc_done, (NACC - 1) * (pair * NQ + q) + bank + 1)
                    else:
                        act.wait_ge(av_done, HP * (pair * NQ + q + 1))
                    nc.scalar.activation(attn_sb[:, bank // PB, bank % PB, :], acc_ps[bank][:], ACT.Copy,
                                         scale=tanh_gate[:, 0:1]).then_inc(acc_read, 1)
                act.wait_ge(acc_read, NACC * (pair * NQ + q + 1))
                dst = scratch["attn"].rearrange("(q d p) t -> q p d t", p=P, d=QW // P)[bass.ds(q, 1), :, :, pair * PB * S:(pair + 1) * PB * S]
                act.dma_start(dst.rearrange("o p d t -> p (o d) t"), attn_sb.rearrange("p d b t -> p d (b t)")).then_inc(attn_stored, 16)

            act.wait_ge(gate_in, 16)
            nc.scalar.activation(tanh_gate[:], gate[:], ACT.Tanh).then_inc(gate_ready, 1)
            act.wait_ge(gate_ready, 1)
            for hp in range(NBUF):
                split_wo(0, 0, hp)
            for hp in range(VW_AHEAD):
                split_vw(0, 0, hp)
            for hp in range(NBUF, WO_AHEAD):
                split_wo(0, 0, hp)
            over_quarters(act, quarter)

        @block.gpsimd
        def _(pool):
            for pair in range(PAIRS):
                with pool.Fori(0, NQ) as q:
                    for hp in range(HP):
                        i = hp % NBUF
                        pool.wait_ge(wo_hi_ready, place(pair, q, hp) + 1)
                        nc.gpsimd.tensor_tensor(wo_lo[:, i], wo_raw[:, i], wo_hi[:, i].bitcast(F32),
                                                ALU.subtract).then_inc(wo_lo_ready, 1)

        @block.vector
        def _(dve):
            for pair in range(PAIRS):
                with dve.Fori(0, NQ) as q:
                    for hp in range(HP):
                        i = hp % NBUF
                        dve.wait_ge(vw_hi_ready, place(pair, q, hp) + 1)
                        for b in range(PB):
                            for h in range(2):
                                at = (slice(h * SK, (h + 1) * SK), i, b)
                                done = nc.vector.tensor_tensor(vw_lo[at], vw_ps[i][b * SK:(b + 1) * SK, h, :],
                                                               vw_hi[at].bitcast(F32), ALU.subtract)
                        done.then_inc(vw_lo_ready, 1)


def attn_block(scratch, i):
    return scratch["attn"].rearrange("(k p) (i t) -> i p k t", p=P, t=BT)[bass.ds(i, 1)].rearrange("o p k t -> p (o k) t")


def x_block(a, i):
    return a["x"].rearrange("(i n p) d -> i p n d", p=P, n=BT // P)[bass.ds(i, 1)].rearrange("o p n d -> p (o n) d")


def feed(nc, a, scratch, ident, out, attn_stored, ahead):
    NT = BT // P
    NC = NT * 2
    HW = D // 2
    NW = 4
    STEPS = NC * KT
    WBUF = 3
    with ExitStack() as ctx:
        def sb(name, shape, dt=F32):
            return ctx.enter_context(nc.sbuf_tensor(name, shape, dt))

        def ps(name, shape):
            return ctx.enter_context(nc.psum_tensor(name, shape, F32))

        def sem(name):
            return ctx.enter_context(nc.semaphore(name))

        attn_in_sb, x_in_sb, gate, row_is_hi, gate_w = (ahead[name] for name in ("attn", "x", "g_ffn", "row_is_hi", "gate_t"))
        attn_in, x_in, small_in = ahead["attn_in"], ahead["x_in"], ahead["small_in"]
        w_raw = sb("ffn_w_raw", [P, WBUF, D])
        w_sign = sb("w_sign", [P, KT, D], F32R)
        bias = sb("bias", [P, D])
        scale_raw = sb("scale_raw", [R, 2, D])
        tanh_gate = sb("tanh_gate_f", [P, 1])
        scale_hi = sb("scale_hi", [R, 2, D], F32R)
        scale_lo = sb("scale_lo", [R, 2, D])
        scale_stack = sb("scale_stack", [P, 2, D], F32R)
        zeros = sb("zeros", [P, 1])
        x1 = sb("x1", [P, 2, NT, D])
        x1b = sb("x1b", [P, 2, NT, D])
        x1n = sb("x1n", [P, NT, D])
        x1n_t = sb("x1n_t", [P, KT, BT])
        xs = sb("xs", [P, KT, BT])
        xs_hi = sb("xs_hi", [P, 2, KT, BT], F32R)
        xs_lo = sb("xs_lo", [P, 2, KT, BT], F32R)
        out_scale = sb("out_scale_sb", [P, 2, HW])
        y_part = sb("y_part", [P, 2, HW])
        y = ahead["y"]
        stats = sb("ffn_stats", [P, NT, 2, 6])
        mean_var = sb("ffn_mean_var", [P, NT, 2])
        var_eps = sb("ffn_var_eps", [P, NT])
        rstd = sb("ffn_rstd", [P, NT])
        shift = sb("ffn_shift", [P, NT])
        minus_half = sb("ffn_minus_half", [P, NT])
        minus_one = sb("ffn_minus_one", [P, NT])
        logits_t = sb("logits_t", [E, BT])
        r_max = sb("r_max", [P, NT])
        r_exp = sb("r_exp", [P, NT, E])
        r_sum = sb("r_sum", [P, NT])
        r_inv = sb("r_inv", [P, NT])
        routing = sb("routing", [P, NT, E])
        r_stack = sb("r_stack", [P, NT, 4, E], F32R)
        r_stack_t = sb("r_stack_t", [P, 2, BT], F32R)
        wk = [ps(f"wk{i}", [P, 512]) for i in range(NW)]
        f_ps = [ps(f"f_ps{i}", [P, HW]) for i in range(2)]
        o_ps = ps("o_ps", [P, HW])
        r_ps = ps("r_ps", [P, 512])

        scales_in = sem("scales_in")
        bias_in = sem("bias_in")
        w_in = [sem(f"ffn_w_in{i}") for i in range(WBUF)]
        sign_ready = sem("sign_ready")
        gate_ready = sem("gate_f_ready")
        zeroed = sem("zeroed")
        scales_step = sem("scales_step")
        stack_ready = sem("stack_ready")
        bias_ready = sem("bias_ready")
        half_ready = sem("ffn_half_ready")
        ta_done = sem("ta_done")
        x1_ready = sem("x1_ready")
        stats_ready = sem("ffn_stats_ready")
        mean_ready = sem("ffn_mean_ready")
        var_ready = sem("ffn_var_ready")
        rstd_ready = sem("ffn_rstd_ready")
        mean_scaled = sem("ffn_mean_scaled")
        shift_ready = sem("ffn_shift_ready")
        x1n_ready = sem("x1n_ready")
        x1b_ready = sem("x1b_ready")
        tb_done = sem("tb_done")
        x1n_t_ready = sem("x1n_t_ready")
        logits_done = sem("logits_done")
        logits_copied = sem("logits_copied")
        lt_done = sem("lt_done")
        r_max_ready = sem("r_max_ready")
        r_shift_ready = sem("r_shift_ready")
        r_exp_ready = sem("r_exp_ready")
        r_sum_ready = sem("r_sum_ready")
        r_inv_ready = sem("r_inv_ready")
        routing_ready = sem("routing_ready")
        r_hi_ready = sem("r_hi_ready")
        r_stack_ready = sem("r_stack_ready")
        rt_done = sem("rt_done")
        r_stack_t_ready = sem("r_stack_t_ready")
        is_done = sem("is_done")
        xs_ready = sem("xs_ready")
        xs_hi_ready = sem("xs_hi_ready")
        xs_lo_ready = sem("xs_lo_ready")
        os_done = sem("os_done")
        os_copied = sem("os_copied")
        f_done = sem("f_done")
        y_part_ready = sem("y_part_ready")
        y_ready = sem("y_ready")
        y_stored = [sem(f"y_stored{i}") for i in range(NC)]

        block = ctx.enter_context(nc.Block())

        def has(i, lag):
            return 0 <= i - lag < NB if isinstance(i, int) else True

        @block.sync
        def _(sp):
            def load(i):
                wait(sp, ta_done, i)
                sp.dma_start(attn_in_sb[:], attn_block(scratch, i)).then_inc(attn_in, 16)
                wait(sp, x1_ready, i)
                sp.dma_start(x_in_sb, x_block(a, i)).then_inc(x_in, 16)

            def slot(i, j):
                if has(i, -2):
                    load(i + 2)
                if has(i, 1):
                    for c in range(NC):
                        sp.wait_ge(y_ready, NC * (i - 1) + c + 1)
                        dst = out.rearrange("(i n p) (h w) -> i n h p w", p=P, n=NT, h=2)[bass.ds(i - 1, 1), c // 2, c % 2]
                        sp.dma_start(dst.rearrange("o p w -> (o p) w"), y[:, c]).then_inc(y_stored[c], 16)

            def load_weights(ks):
                for k in ks:
                    wait(sp, sign_ready, k - WBUF + 1)
                    sp.dma_start(w_raw[:, k % WBUF], a["weight_t"][k * P:(k + 1) * P, :]).then_inc(w_in[k % WBUF], 16)

            load_weights(range(WBUF))
            slot(-1, 1)
            load_weights(range(WBUF, KT))
            sp.wait_ge(attn_stored, 16 * B // PB * NQ)
            slot(0, 0)
            slot(1, 1)
            with sp.Fori(1, NB // 2 - 1) as g:
                slot(2 * g, 0)
                slot(2 * g + 1, 1)
            for i in range(NB - 2, NB + 1):
                slot(i, i % 2)
            for c in range(NC):
                sp.wait_ge(y_stored[c], 16 * NB)

        @block.tensor
        def _(pe):
            def products(i, j, steps):
                for step in steps:
                    c, k = step // KT, step % KT
                    t, h = c // 2, c % 2
                    if k == 0:
                        wait(pe, os_copied, NC * i + c)
                        pe.matmul(o_ps[:], r_stack_t[:, j, t * P:(t + 1) * P], scale_stack[:, 1, h * HW:(h + 1) * HW],
                                  start=True, stop=True).then_inc(os_done, 1)
                        wait(pe, y_part_ready, NC * i + c - 1)
                    if c == 0 and k % 2 == 0:
                        pe.wait_ge(xs_lo_ready, NW * i + k // 2 + 1)
                    for n, part in enumerate((xs_hi, xs_lo)):
                        last = pe.matmul(f_ps[c % 2][:], part[:, j, k, t * P:(t + 1) * P], w_sign[:, k, h * HW:(h + 1) * HW],
                                         start=(k == 0 and n == 0), stop=(k == KT - 1 and n == 1))
                    if k == KT - 1:
                        last.then_inc(f_done, 1)

            def turn_attention(i):
                pe.wait_ge(attn_in, 16 * (i + 1))
                wait(pe, x1n_t_ready, i)
                for t in range(NT):
                    for k in range(KT):
                        last = pe.transpose(wk[2 * t + k // 4][:, k % 4 * P:(k % 4 + 1) * P],
                                            attn_in_sb[:, k, t * P:(t + 1) * P], ident[:])
                last.then_inc(ta_done, 1)

            def turn_normalised(i):
                pe.wait_ge(x1n_ready, i + 1)
                wait(pe, xs_ready, NW * i)
                for t in range(NT):
                    for k in range(KT):
                        last = pe.transpose(wk[k // 2][:, k % 2 * BT + t * P:k % 2 * BT + (t + 1) * P],
                                            x1n[:, t, k * P:(k + 1) * P], ident[:])
                last.then_inc(tb_done, 1)

            def router_logits(i):
                pe.wait_ge(x1n_t_ready, i + 1)
                wait(pe, r_stack_t_ready, i)
                for k in range(KT):
                    last = pe.matmul(r_ps[0:E, 0:BT], gate_w[:, k, :], x1n_t[:, k, :], start=k == 0, stop=k == KT - 1)
                last.then_inc(logits_done, 1)

            def turn_logits():
                for t in range(NT):
                    last = pe.transpose(r_ps[:, BT + t * E:BT + (t + 1) * E], logits_t[:, t * P:(t + 1) * P], ident[0:E, 0:E])
                last.then_inc(lt_done, 1)

            def turn_routing(i):
                pe.wait_ge(r_stack_ready, i + 1)
                for t in range(NT):
                    last = pe.transpose(r_ps[0:R, t * P:(t + 1) * P], r_stack[:, t].rearrange("p n e -> p (n e)").bitcast(F32), ident[:])
                last.then_inc(rt_done, 1)

            def in_scales(i, j):
                pe.wait_ge(r_stack_t_ready, i + 1)
                if isinstance(i, int) and i == 0:
                    pe.wait_ge(stack_ready, 1)
                wait(pe, x1_ready, i + 2 if has(i, -1) else i + 1)
                for k in range(KT):
                    last = pe.matmul(wk[k // 2][:, k % 2 * BT:(k % 2 + 1) * BT], scale_stack[:, 0, k * P:(k + 1) * P],
                                     r_stack_t[:, j, :], start=True, stop=True)
                last.then_inc(is_done, 1)

            def slot(i, j):
                def some_products(first, count):
                    if has(i, 1):
                        products(i - 1, 1 - j, range(first, first + count))

                if has(i, 0):
                    turn_normalised(i)
                if isinstance(i, int) and i == 1:
                    pe.wait_ge(sign_ready, KT)
                some_products(0, 6)
                if has(i, -1):
                    turn_attention(i + 1)
                if has(i, 0):
                    router_logits(i)
                some_products(6, 2)
                if has(i, 0):
                    pe.wait_ge(logits_copied, i + 1)
                some_products(8, 1)
                if has(i, 0):
                    turn_logits()
                some_products(9, 6)
                if has(i, 0):
                    turn_routing(i)
                some_products(15, 1)
                if has(i, 0):
                    in_scales(i, j)
                some_products(16, STEPS - 16)

            slot(-1, 1)
            pe.wait_ge(small_in, 48)
            slot(0, 0)
            slot(1, 1)
            with pe.Fori(1, NB // 2 - 1) as g:
                slot(2 * g, 0)
                slot(2 * g + 1, 1)
            for i in range(NB - 2, NB + 1):
                slot(i, i % 2)

        @block.scalar
        def _(act):
            def copy_out_scales(i, c):
                act.wait_ge(os_done, NC * i + c + 1)
                wait(act, y_part_ready, NC * i + c - 1)
                nc.scalar.copy(out_scale[:, c % 2], o_ps[:]).then_inc(os_copied, 1)

            def normalise(i, j):
                act.wait_ge(shift_ready, i + 1)
                wait(act, tb_done, i)
                for t in range(NT):
                    done = nc.scalar.activation(x1n[:, t], x1[:, j, t], ACT.Identity, bias=shift[:, t:t + 1], scale=rstd[:, t:t + 1])
                done.then_inc(x1n_ready, 1)

            def high(i, j, m):
                act.wait_ge(xs_ready, NW * i + m + 1)
                nc.scalar.copy(xs_hi[:, j, 2 * m:2 * m + 2, :], xs[:, 2 * m:2 * m + 2, :]).then_inc(xs_hi_ready, 1)

            FIRST_SIGNS = 3

            def sign(k):
                act.wait_ge(w_in[k % WBUF], 16 * (k // WBUF + 1))
                nc.scalar.activation(w_sign[:, k, :], w_raw[:, k % WBUF], ACT.Sign).then_inc(sign_ready, 1)

            def slot(i, j):
                if has(i, 0):
                    act.wait_ge(tb_done, i + 1)
                    for m in range(NW):
                        done = nc.scalar.copy(x1n_t[:, 2 * m:2 * m + 2, :], wk[m][:].rearrange("p (k t) -> p k t", k=2))
                    done.then_inc(x1n_t_ready, 1)
                if isinstance(i, int) and i == 0:
                    for k in range(FIRST_SIGNS, KT):
                        sign(k)
                if has(i, 1):
                    copy_out_scales(i - 1, 0)
                if has(i, 0):
                    act.wait_ge(logits_done, i + 1)
                    wait(act, lt_done, i)
                    nc.scalar.copy(logits_t[:], r_ps[0:E, 0:BT]).then_inc(logits_copied, 1)
                    act.wait_ge(r_shift_ready, i + 1)
                    nc.scalar.activation(r_exp[:], routing[:], ACT.Exp).then_inc(r_exp_ready, 1)
                if has(i, 1):
                    copy_out_scales(i - 1, 1)
                if has(i, 0):
                    act.wait_ge(rt_done, i + 1)
                    wait(act, os_done, NC * (i - 1))
                    nc.scalar.copy(r_stack_t[0:R, j, :], r_ps[0:R, 0:BT]).then_inc(r_stack_t_ready, 1)
                    wait(act, f_done, NC * (i - 1))
                    high(i, j, 0)
                    high(i, j, 1)
                if has(i, 1):
                    copy_out_scales(i - 1, 2)
                if has(i, 0):
                    high(i, j, 2)
                    high(i, j, 3)
                if has(i, -1):
                    normalise(i + 1, 1 - j)
                if has(i, 1):
                    copy_out_scales(i - 1, 3)

            act.dma_start(scale_raw[:], a["scales"]).then_inc(scales_in, 16)
            act.wait_ge(small_in, 48)
            nc.scalar.activation(tanh_gate[:], gate[:], ACT.Tanh).then_inc(gate_ready, 1)
            act.dma_start(bias[:], a["bias"]).then_inc(bias_in, 16)
            for k in range(FIRST_SIGNS):
                sign(k)
            for i in range(-1, 2):
                slot(i, i % 2)
            with act.Fori(1, NB // 2 - 1) as g:
                slot(2 * g, 0)
                slot(2 * g + 1, 1)
            for i in range(NB - 2, NB + 1):
                slot(i, i % 2)

        @block.gpsimd
        def _(pool):
            def add(i, j, c):
                t, h = c // 2, c % 2
                pool.wait_ge(y_part_ready, NC * i + c + 1)
                pool.wait_ge(x1b_ready, i + 1)
                wait(pool, y_stored[c], 16 * i)
                nc.gpsimd.tensor_tensor(y[:, c], y_part[:, c % 2], x1b[:, j, t, h * HW:(h + 1) * HW], ALU.add).then_inc(y_ready, 1)

            def slot(i, j):
                if has(i, 0):
                    wait(pool, y_ready, NC * (i - 1))
                    pool.wait_ge(x1_ready, i + 1)
                    nc.gpsimd.tensor_tensor(x1b[:, j], x1[:, j], bias[:].unsqueeze(1).to_broadcast([P, NT, D]), ALU.add).then_inc(x1b_ready, 1)
                if has(i, 1):
                    add(i - 1, 1 - j, 0)
                if has(i, -1):
                    pool.wait_ge(var_ready, i + 2)
                    wait(pool, x1n_ready, i + 1)
                    nc.gpsimd.tensor_tensor(rstd[:], var_eps[:], minus_half[:], ALU.pow).then_inc(rstd_ready, 1)
                    pool.wait_ge(rstd_ready, i + 2)
                    nc.gpsimd.tensor_tensor(shift[:], mean_var[:, :, 0], rstd[:], ALU.mult).then_inc(mean_scaled, 1)
                    pool.wait_ge(mean_scaled, i + 2)
                    nc.gpsimd.tensor_tensor(shift[:], shift[:], minus_one[:], ALU.mult).then_inc(shift_ready, 1)
                if has(i, 1):
                    for c in range(1, NC):
                        add(i - 1, 1 - j, c)

            nc.gpsimd.memset(minus_one[:], -1.0)
            nc.gpsimd.memset(minus_half[:], -0.5).then_inc(half_ready, 1)
            pool.wait_ge(half_ready, 1)
            slot(-1, 1)
            pool.wait_ge(bias_ready, 1)
            slot(0, 0)
            pool.wait_ge(attn_stored, 16 * B // PB * NQ)
            slot(1, 1)
            with pool.Fori(1, NB // 2 - 1) as g:
                slot(2 * g, 0)
                slot(2 * g + 1, 1)
            for i in range(NB - 2, NB + 1):
                slot(i, i % 2)

        @block.vector
        def _(dve):
            def scaled(i, c):
                dve.wait_ge(f_done, NC * i + c + 1)
                dve.wait_ge(os_copied, NC * i + c + 1)
                wait(dve, y_ready, NC * i + c - 1)
                nc.vector.tensor_tensor(y_part[:, c % 2], f_ps[c % 2][:], out_scale[:, c % 2], ALU.mult).then_inc(y_part_ready, 1)

            def residual(i, j):
                dve.wait_ge(ta_done, i + 1)
                dve.wait_ge(x_in, 16 * (i + 1))
                wait(dve, x1n_ready, i - 1)
                wait(dve, x1b_ready, i - 1)
                for t in range(NT):
                    for h in range(2):
                        at = (slice(None), t, slice(h * HW, (h + 1) * HW))
                        done = nc.vector.tensor_tensor(x1[:, j][at], wk[2 * t + h][:], x_in_sb[at], ALU.add)
                done.then_inc(x1_ready, 1)
                dve.wait_ge(x1_ready, i + 1)
                for t in range(NT):
                    for h in range(2):
                        done = nc.vector.bn_stats(stats[:, t, h, :], x1[:, j, t, h * HW:(h + 1) * HW])
                done.then_inc(stats_ready, 1)

            def slot(i, j):
                if has(i, -1):
                    residual(i + 1, 1 - j)
                    dve.wait_ge(stats_ready, i + 2)
                    wait(dve, shift_ready, i + 1)
                if has(i, 1):
                    scaled(i - 1, 0)
                if has(i, -1):
                    for t in range(NT):
                        done = nc.vector.bn_aggr(mean_var[:, t, :], stats[:, t])
                    done.then_inc(mean_ready, 1)
                    dve.wait_ge(mean_ready, i + 2)
                    nc.vector.tensor_scalar(var_eps[:], mean_var[:, :, 1], EPS, None, ALU.add).then_inc(var_ready, 1)
                if has(i, 0):
                    logits = r_ps[:, BT:BT + NT * E].rearrange("p (t e) -> p t e", e=E)
                    dve.wait_ge(lt_done, i + 1)
                    nc.vector.tensor_reduce(r_max[:], logits, AX.X, ALU.max).then_inc(r_max_ready, 1)
                    dve.wait_ge(r_max_ready, i + 1)
                    nc.vector.tensor_tensor(routing[:], logits, r_max[:].unsqueeze(2).to_broadcast([P, NT, E]),
                                            ALU.subtract).then_inc(r_shift_ready, 1)
                    dve.wait_ge(r_exp_ready, i + 1)
                    nc.vector.tensor_reduce(r_sum[:], r_exp[:], AX.X, ALU.add).then_inc(r_sum_ready, 1)
                    dve.wait_ge(r_sum_ready, i + 1)
                    nc.vector.reciprocal(r_inv[:], r_sum[:]).then_inc(r_inv_ready, 1)
                    dve.wait_ge(r_inv_ready, i + 1)
                    nc.vector.tensor_tensor(routing[:], r_exp[:], r_inv[:].unsqueeze(2).to_broadcast([P, NT, E]),
                                            ALU.mult).then_inc(routing_ready, 1)
                    dve.wait_ge(routing_ready, i + 1)
                    wait(dve, rt_done, i)
                    nc.vector.tensor_copy(r_stack[:, :, 0:2, :], routing[:].unsqueeze(2).to_broadcast([P, NT, 2, E])).then_inc(r_hi_ready, 1)
                    dve.wait_ge(r_hi_ready, i + 1)
                    for n in range(2):
                        done = nc.vector.tensor_tensor(r_stack[:, :, 2 + n, :], routing[:], r_stack[:, :, 0, :].bitcast(F32), ALU.subtract)
                    done.then_inc(r_stack_ready, 1)
                if has(i, 1):
                    scaled(i - 1, 1)
                if has(i, 0):
                    def low(m):
                        dve.wait_ge(xs_hi_ready, NW * i + m + 1)
                        at = (slice(None), slice(2 * m, 2 * m + 2))
                        nc.vector.tensor_tensor(xs_lo[:, j][at], xs[at], xs_hi[:, j][at].bitcast(F32), ALU.subtract).then_inc(xs_lo_ready, 1)

                    dve.wait_ge(is_done, i + 1)
                    wait(dve, xs_lo_ready, NW * i)
                    for m in range(NW):
                        at = (slice(None), slice(2 * m, 2 * m + 2))
                        nc.vector.tensor_tensor(xs[at], wk[m][:].rearrange("p (k t) -> p k t", k=2), x1n_t[at], ALU.mult).then_inc(xs_ready, 1)
                        if m >= 1:
                            low(m - 1)
                    low(NW - 1)
                if has(i, 1):
                    scaled(i - 1, 2)
                    scaled(i - 1, 3)

            def zero():
                nc.vector.memset(zeros[:], 0.0).then_inc(zeroed, 1)
                dve.wait_ge(zeroed, 1)
                for n in range(2):
                    nc.vector.tensor_copy(scale_stack[:, n], zeros[:, 0:1].to_broadcast([P, D]))
                    done = nc.vector.tensor_copy(r_stack_t[:, n], zeros[:, 0:1].to_broadcast([P, BT]))
                done.then_inc(zeroed, 1)

            def stack_scales():
                dve.wait_ge(scales_in, 16)
                dve.wait_ge(small_in, 48)
                dve.wait_ge(gate_ready, 1)
                nc.vector.tensor_scalar(scale_raw[:, 1], scale_raw[:, 1], tanh_gate[0:R, 0:1], None, ALU.mult).then_inc(scales_step, 1)
                dve.wait_ge(scales_step, 1)
                nc.vector.tensor_copy(scale_hi[:], scale_raw[:]).then_inc(scales_step, 1)
                dve.wait_ge(scales_step, 2)
                nc.vector.tensor_tensor(scale_lo[:], scale_raw[:], scale_hi[:].bitcast(F32), ALU.subtract).then_inc(scales_step, 1)
                dve.wait_ge(scales_step, 3)
                nc.vector.tensor_scalar(scale_lo[:], scale_lo[:], row_is_hi[:, 1:2], None, ALU.mult).then_inc(scales_step, 1)
                dve.wait_ge(scales_step, 4)
                dve.wait_ge(zeroed, 2)
                nc.vector.scalar_tensor_tensor(out=scale_stack[0:R], in0=scale_hi[:].bitcast(F32), scalar=row_is_hi[:, 0:1], in1=scale_lo[:],
                                               op0=ALU.mult, op1=ALU.add).then_inc(stack_ready, 1)
                dve.wait_ge(bias_in, 16)
                nc.vector.tensor_scalar(bias[:], bias[:], tanh_gate[:, 0:1], None, ALU.mult).then_inc(bias_ready, 1)

            zero()
            slot(-1, 1)
            stack_scales()
            slot(0, 0)
            slot(1, 1)
            with dve.Fori(1, NB // 2 - 1) as g:
                slot(2 * g, 0)
                slot(2 * g + 1, 1)
            for i in range(NB - 2, NB + 1):
                slot(i, i % 2)



_OUT = ((B, S, D), "float32")


def build(nc, a, out):
    scratch = {
        "keys": nc.dram_tensor("keys_scratch", (2, HKV * HALF, CTX), F32, kind="Internal").ap(),
        "values": nc.dram_tensor("values_scratch", (2, HKV, P, CTX), F32, kind="Internal").ap(),
        "probs": nc.dram_tensor("probs_scratch", (2, HP, P, T), F32, kind="Internal").ap(),
        "attn": nc.dram_tensor("attn_scratch", (D, T), F32, kind="Internal").ap(),
    }
    with ExitStack() as kept:
        ident = kept.enter_context(nc.sbuf_tensor("ident", [P, P], F32))
        w_raw = kept.enter_context(nc.sbuf_tensor("w_raw", [P, 2, KT, P], F32))
        with ExitStack() as until_feed:
            x_hi, x_lo = (until_feed.enter_context(nc.sbuf_tensor(name, [P, KT, T], F32R, side="right")) for name in ("x_hi", "x_lo"))
            w_hi, w_lo = (until_feed.enter_context(nc.sbuf_tensor(name, [P, 2, KT, P], F32R, side="right")) for name in ("w_hi", "w_lo"))
            prepare(nc, a, scratch, x_hi, x_lo, w_raw, w_hi, w_lo, ident)

            def as_wo(w):
                return w[:].rearrange("p c k n -> p (c k n)").rearrange("p (i h n) -> p i h n", i=WO_BUFS, h=2)

            def as_probs(x):
                return x[:].rearrange("p k (h t) -> p (k h) t", t=PB * S)

            early = {"p_hi": as_probs(x_hi), "p_lo": as_probs(x_lo), "wo_raw": as_wo(w_raw)}
            for name, count in (("p_in", HP), ("wo_in", WO_BUFS), ("pt_stored", 2)):
                early[name] = [kept.enter_context(nc.semaphore(f"{name}{i}")) for i in range(count)]
            attend(nc, a, scratch, x_hi, x_lo, w_raw, w_hi, w_lo, ident, early)

            ahead = {name: kept.enter_context(nc.sbuf_tensor(f"ahead_{name}", shape, F32)) for name, shape in (
                ("attn", [P, KT, BT]), ("y", [P, BT // P * 2, D // 2]), ("g_ffn", [P, 1]), ("row_is_hi", [R, 2]), ("gate_t", [P, KT, E]))}
            ahead["x"] = w_raw[:].rearrange("p c k n -> p (c k n)").rearrange("p (n d) -> p n d", d=D)
            for name in ("attn_in", "x_in", "small_in"):
                ahead[name] = kept.enter_context(nc.semaphore(name))
            attn_stored = kept.enter_context(nc.semaphore("attn_stored"))
            project(nc, a, scratch, early, as_wo(w_hi), as_wo(w_lo), attn_stored, ahead)
        feed(nc, a, scratch, ident, out, attn_stored, ahead)


def constants():
    inv_freq = (np.float32(1.0) / np.float32(10000.0) ** (np.arange(0, DK, 2, dtype=np.float32) / np.float32(DK)))
    angle = np.arange(S, dtype=np.float32)[:, None] * inv_freq.astype(np.float32)[None, :]
    cos = np.concatenate([np.cos(angle).T] * 2, 0).astype(np.float32)
    sin = np.concatenate([np.sin(angle).T] * 2, 0).astype(np.float32)
    scale = np.float32(1.0) / np.sqrt(np.float32(DK))
    row = np.arange(4 * E)
    is_hi = np.stack([row // E % 2 == 0, row // E % 2 == 1], 1).astype(np.float32)
    return {
        "row_is_hi": is_hi,
        "ident": np.eye(P, dtype=np.float32), "cos_q": cos, "sin_q": sin,
        "cos_k": np.tile(cos[:, :SK] * scale, (1, B)), "sin_k": np.tile(sin[:, :SK] * scale, (1, B)),
    }


def laid_out(x, ctx_4096, mask_BxSxS2_ff0, g_xattn, g_ffn, L0_xattn_wq, L0_xattn_wk, L0_xattn_wv, L0_xattn_wo,
             L0_ffn_weight, L0_ffn_bias, L0_ffn_gate_w, L0_ffn_in_channel_scale, L0_ffn_out_channel_scale):
    n = np.asarray
    wk = n(L0_xattn_wk).reshape(KT, P, GP, 2, 2, HALF).transpose(2, 4, 1, 0, 3, 5).reshape(HKV, P, KT, P)
    wv = n(L0_xattn_wv).reshape(KT, P, HKV, P).transpose(2, 1, 0, 3)
    return {
        "x": n(x).reshape(T, D),
        "ctx_t": n(ctx_4096).reshape(CTX, D).T,
        "mask": n(mask_BxSxS2_ff0).reshape(B, TT, P, SK).transpose(2, 0, 1, 3),
        "g_xattn": np.broadcast_to(n(g_xattn), (P, 1)), "g_ffn": np.broadcast_to(n(g_ffn), (P, 1)),
        "wq": n(L0_xattn_wq).reshape(KT, P, HP, 2, 2, HALF).transpose(2, 4, 1, 0, 3, 5).reshape(HP, 2, P, KT, P),
        "wkv": np.concatenate([wk, wv], 0),
        "wo": n(L0_xattn_wo).reshape(HP, 2, P, NQ, QW).transpose(3, 0, 2, 1, 4),
        "weight_t": n(L0_ffn_weight).T,
        "bias": np.broadcast_to(n(L0_ffn_bias), (P, D)),
        "gate_t": n(L0_ffn_gate_w).T.reshape(KT, P, E).transpose(1, 0, 2),
        "scales": np.stack([np.tile(n(s), (4, 1)) for s in (L0_ffn_in_channel_scale, L0_ffn_out_channel_scale)], 1),
    }


def kernel(**inputs):
    import concourse.bacc as bacc
    from concourse.bass_utils import run_bass_kernel_spmd

    nc = bacc.Bacc("TRN2", target_bir_lowering=False, num_devices=1)
    arrays, aps = {}, {}
    for name, value in (laid_out(**inputs) | constants()).items():
        value = np.ascontiguousarray(value)
        arrays[f"in_{name}"] = value
        aps[name] = nc.dram_tensor(f"in_{name}", value.shape, mybir.dt.from_np(value.dtype), kind="ExternalInput").ap()
    out = nc.dram_tensor("out_y", (T, D), F32, kind="ExternalOutput").ap()
    build(nc, aps, out)
    r = run_bass_kernel_spmd(nc, [arrays], core_ids=[0])
    return r.results[0]["out_y"].reshape(_OUT[0])
```
